# Optimizing a Trainium2 kernel written in Bass

```python
import numpy as np
import jax
import jax.numpy as jnp

def _softmax(x, axis=-1):
    return jax.nn.softmax(x, axis=axis)
def _gelu(x):
    return jax.nn.gelu(x, approximate=True)
def _silu(x):
    return jax.nn.silu(x)
def _sigmoid(x):
    return jax.nn.sigmoid(x)
def _layernorm(x, axis=-1, eps=1e-5):
    m = jnp.mean(x, axis=axis, keepdims=True)
    v = jnp.var(x, axis=axis, keepdims=True)
    return (x - m) / jnp.sqrt(v + eps)
def _scatter_add(tgt, idx, src, axis=0):
    return tgt.at[idx].add(src)
def _segment_sum(src, seg, n):
    return jax.ops.segment_sum(src, seg, n)

kernel_name = 'mk_conv_preact_d4_conv_nchw64_8cda5f'

def setup_inputs(seed: int = 0):
    np.random.seed(seed)
    _w = jnp.asarray
    def _rec_inputs():
        import jax
        import jax.numpy as jnp
        _gk = jax.random.key(seed)
        x = -0.000929 + 1 * jax.random.normal(jax.random.fold_in(_gk, 1), (16, 64, 32, 32), jnp.float32)
        return x
    x = _rec_inputs()
    def _L0_conv_setup():
        import jax, jax.numpy as jnp
        import numpy as np
        K, S, P = (3, 1, 1)
        EPS = 1e-05

        def _unfold_patches(x, k, s, p):
            B, C, H, W = x.shape
            xp = jnp.pad(x, ((0, 0), (0, 0), (p, p), (p, p)))
            Ho = (H + 2 * p - k) // s + 1
            Wo = (W + 2 * p - k) // s + 1
            slabs = []
            for ki in range(k):
                for kj in range(k):
                    slabs.append(xp[:, :, ki:ki + (Ho - 1) * s + 1:s, kj:kj + (Wo - 1) * s + 1:s])
            return jnp.stack(slabs, axis=2).reshape(B, C, k, k, Ho, Wo)
        key = jax.random.key(seed)
        k1, k2, k3 = jax.random.split(key, 3)
        B, Cin, Cout, IM = (16, 64, 64, 32)
        fold = (IM + 2 * P - K) // S + 1
        return {'x': jax.random.normal(k1, (B, Cin, IM, IM), dtype=jnp.float32), 'weight': jax.random.normal(k2, (Cout, fold, fold, Cin, K, K), dtype=jnp.float32), 'bias': jax.random.normal(k3, (Cout, fold, fold), dtype=jnp.float32), 'gamma': jnp.ones((Cout,), dtype=jnp.float32), 'beta': jnp.zeros((Cout,), dtype=jnp.float32)}
    _L0_conv_all = _L0_conv_setup()
    _L0_conv_in = {k: v for k, v in _L0_conv_all.items() if k in ('weight', 'bias', 'gamma', 'beta', )}
    del _L0_conv_all

    def _L1_conv_setup():
        import jax, jax.numpy as jnp
        import numpy as np
        PAD = 1
        KH = KW = 3
        K = KH * KW

        def conv2d(x, w, b):
            out = jax.lax.conv_general_dilated(x, w, (1, 1), [(PAD, PAD), (PAD, PAD)], dimension_numbers=('NCHW', 'OIHW', 'NCHW'))
            return out + b[None, :, None, None]

        def deform_conv2d(x, offset, mask, w):
            B, C, H, W = x.shape
            Co = w.shape[0]
            Ho, Wo = (offset.shape[2], offset.shape[3])
            off = offset.reshape(B, K, 2, Ho, Wo)
            ky, kx = jnp.meshgrid(jnp.arange(KH), jnp.arange(KW), indexing='ij')
            py = off[:, :, 0] + (ky.reshape(K, 1, 1) + jnp.arange(Ho).reshape(1, Ho, 1) - PAD).astype(x.dtype)
            px = off[:, :, 1] + (kx.reshape(K, 1, 1) + jnp.arange(Wo).reshape(1, 1, Wo) - PAD).astype(x.dtype)
            y0 = jnp.floor(py)
            x0 = jnp.floor(px)
            wy = py - y0
            wx = px - x0
            y0i = y0.astype(jnp.int32)
            x0i = x0.astype(jnp.int32)
            xf = x.reshape(B, C, H * W)
            gather = jax.vmap(lambda xb, idx: jnp.take(xb, idx, axis=1))
            val = jnp.zeros((B, C, K, Ho, Wo), x.dtype)
            corners = [(y0i, x0i, (1 - wy) * (1 - wx)), (y0i, x0i + 1, (1 - wy) * wx), (y0i + 1, x0i, wy * (1 - wx)), (y0i + 1, x0i + 1, wy * wx)]
            for yy, xx, wt in corners:
                valid = (yy >= 0) & (yy < H) & (xx >= 0) & (xx < W)
                flat = jnp.clip(yy, 0, H - 1) * W + jnp.clip(xx, 0, W - 1)
                val = val + gather(xf, flat) * (wt * valid)[:, None]
            val = val * mask[:, None]
            return jnp.einsum('bckhw,ock->bohw', val, w.reshape(Co, -1, K))
        key = jax.random.key(seed)
        ks = jax.random.split(key, 5)
        B, C, H, W = (4, 64, 128, 128)
        x = jax.random.normal(ks[0], (B, C, H, W), jnp.float32)
        offset_w = jax.random.normal(ks[1], (2 * K, C, KH, KW), jnp.float32) * 0.01
        offset_b = jax.random.normal(ks[2], (2 * K,), jnp.float32) * 0.01
        mod_w = jax.random.normal(ks[3], (K, C, KH, KW), jnp.float32) * 0.01
        mod_b = jnp.zeros((K,), jnp.float32)
        reg_w = jax.random.normal(ks[4], (C, C, KH, KW), jnp.float32) * (1.0 / np.sqrt(C * K))
        return {'x': x, 'offset_w': offset_w, 'offset_b': offset_b, 'mod_w': mod_w, 'mod_b': mod_b, 'reg_w': reg_w}
    _L1_conv_all = _L1_conv_setup()
    _L1_conv_in = {k: v for k, v in _L1_conv_all.items() if k in ('offset_w', 'offset_b', 'mod_w', 'mod_b', 'reg_w', )}
    del _L1_conv_all

    def _L2_conv_setup():
        import jax, jax.numpy as jnp
        import numpy as np
        B, C, M, N = (8, 64, 256, 256)
        THRESHOLD = 0.8
        EPS = 1e-05
        PAD = 3

        def conv2d(x, w, b=None):
            y = jax.lax.conv_general_dilated(x, w, window_strides=(1, 1), padding=[(PAD, PAD), (PAD, PAD)], dimension_numbers=('NCHW', 'OIHW', 'NCHW'))
            if b is not None:
                y = y + b[None, :, None, None]
            return y

        def region_norm(region, mask):
            s = jnp.sum(region, axis=(0, 2, 3))
            Sr = jnp.sum(mask, axis=(0, 2, 3))
            Sr = jnp.where(Sr == 0, 1.0, Sr)
            mu = (s / Sr)[None, :, None, None]
            t = region + (1.0 - mask) * mu
            m = jnp.mean(t, axis=(0, 2, 3), keepdims=True)
            v = jnp.mean((t - m) ** 2, axis=(0, 2, 3), keepdims=True)
            bn = (t - m) * jax.lax.rsqrt(v + EPS)
            scale = jnp.sqrt(Sr / (region.shape[0] * region.shape[2] * region.shape[3]))
            return bn * scale[None, :, None, None]
        key = jax.random.key(seed)
        k = jax.random.split(key, 6)
        x = jax.random.normal(k[0], (B, C, M, N), dtype=jnp.float32)
        w1 = jax.random.normal(k[1], (1, 2, 7, 7), dtype=jnp.float32) * 0.1
        wg = jax.random.normal(k[2], (1, 1, 7, 7), dtype=jnp.float32) * 0.1
        bg = jax.random.normal(k[3], (1,), dtype=jnp.float32) * 0.1
        wb = jax.random.normal(k[4], (1, 1, 7, 7), dtype=jnp.float32) * 0.1
        bb = jax.random.normal(k[5], (1,), dtype=jnp.float32) * 0.1
        return {'x': x, 'w1': w1, 'wg': wg, 'bg': bg, 'wb': wb, 'bb': bb}
    _L2_conv_all = _L2_conv_setup()
    _L2_conv_in = {k: v for k, v in _L2_conv_all.items() if k in ('w1', 'wg', 'bg', 'wb', 'bb', )}
    del _L2_conv_all

    def _L3_conv_setup():
        import jax, jax.numpy as jnp
        import numpy as np
        N, C, H, W, A = (32, 64, 32, 32, 4)
        CHW = C * H * W

        def _xavier(key, shape):
            fan_in, fan_out = (shape[-2], shape[-1])
            limit = float(np.sqrt(6.0 / (fan_in + fan_out)))
            return jax.random.uniform(key, shape, jnp.float32, -limit, limit)
        key = jax.random.key(seed)
        ks = jax.random.split(key, 5)
        x = jax.random.normal(ks[0], (N, C, H, W), jnp.float32)
        in_proj_weight = _xavier(ks[1], (3, C, H, W, A))
        in_proj_bias = jnp.zeros((3, C, H, W, A), jnp.float32)
        hid_proj_weight = _xavier(ks[2], (A, CHW, A))
        hid_proj_bias = jnp.zeros((A, CHW), jnp.float32)
        out_proj_weight = _xavier(ks[3], (A, CHW))
        out_proj_bias = jnp.zeros((CHW,), jnp.float32)
        return {'x': x, 'in_proj_weight': in_proj_weight, 'in_proj_bias': in_proj_bias, 'hid_proj_weight': hid_proj_weight, 'hid_proj_bias': hid_proj_bias, 'out_proj_weight': out_proj_weight, 'out_proj_bias': out_proj_bias}
    _L3_conv_all = _L3_conv_setup()
    _L3_conv_in = {k: v for k, v in _L3_conv_all.items() if k in ('in_proj_weight', 'in_proj_bias', 'hid_proj_weight', 'hid_proj_bias', 'out_proj_weight', 'out_proj_bias', )}
    del _L3_conv_all

    return {
        "x": x,
        "L0_conv_weight": _L0_conv_in["weight"],
        "L0_conv_bias": _L0_conv_in["bias"],
        "L0_conv_gamma": _L0_conv_in["gamma"],
        "L0_conv_beta": _L0_conv_in["beta"],
        "L1_conv_offset_w": _L1_conv_in["offset_w"],
        "L1_conv_offset_b": _L1_conv_in["offset_b"],
        "L1_conv_mod_w": _L1_conv_in["mod_w"],
        "L1_conv_mod_b": _L1_conv_in["mod_b"],
        "L1_conv_reg_w": _L1_conv_in["reg_w"],
        "L2_conv_w1": _L2_conv_in["w1"],
        "L2_conv_wg": _L2_conv_in["wg"],
        "L2_conv_bg": _L2_conv_in["bg"],
        "L2_conv_wb": _L2_conv_in["wb"],
        "L2_conv_bb": _L2_conv_in["bb"],
        "L3_conv_in_proj_weight": _L3_conv_in["in_proj_weight"],
        "L3_conv_in_proj_bias": _L3_conv_in["in_proj_bias"],
        "L3_conv_hid_proj_weight": _L3_conv_in["hid_proj_weight"],
        "L3_conv_hid_proj_bias": _L3_conv_in["hid_proj_bias"],
        "L3_conv_out_proj_weight": _L3_conv_in["out_proj_weight"],
        "L3_conv_out_proj_bias": _L3_conv_in["out_proj_bias"],
    }

def reference(x, L0_conv_weight, L0_conv_bias, L0_conv_gamma, L0_conv_beta, L1_conv_offset_w, L1_conv_offset_b, L1_conv_mod_w, L1_conv_mod_b, L1_conv_reg_w, L2_conv_w1, L2_conv_wg, L2_conv_bg, L2_conv_wb, L2_conv_bb, L3_conv_in_proj_weight, L3_conv_in_proj_bias, L3_conv_hid_proj_weight, L3_conv_hid_proj_bias, L3_conv_out_proj_weight, L3_conv_out_proj_bias):
    import jax
    import jax.numpy as jnp
    def _L0_conv_ref(x, weight, bias, gamma, beta):
        import jax, jax.numpy as jnp
        import numpy as np
        K, S, P = (3, 1, 1)
        EPS = 1e-05

        def _unfold_patches(x, k, s, p):
            B, C, H, W = x.shape
            xp = jnp.pad(x, ((0, 0), (0, 0), (p, p), (p, p)))
            Ho = (H + 2 * p - k) // s + 1
            Wo = (W + 2 * p - k) // s + 1
            slabs = []
            for ki in range(k):
                for kj in range(k):
                    slabs.append(xp[:, :, ki:ki + (Ho - 1) * s + 1:s, kj:kj + (Wo - 1) * s + 1:s])
            return jnp.stack(slabs, axis=2).reshape(B, C, k, k, Ho, Wo)
        patches = _unfold_patches(x, K, S, P)
        y = jnp.einsum('bcpqij,oijcpq->boij', patches, weight) + bias[None]
        mean = jnp.mean(y, axis=(0, 2, 3), keepdims=True)
        var = jnp.var(y, axis=(0, 2, 3), keepdims=True)
        y = (y - mean) * jax.lax.rsqrt(var + EPS)
        y = y * gamma[None, :, None, None] + beta[None, :, None, None]
        return jax.nn.relu(y)

    def _L1_conv_ref(x, offset_w, offset_b, mod_w, mod_b, reg_w):
        import jax, jax.numpy as jnp
        import numpy as np
        PAD = 1
        KH = KW = 3
        K = KH * KW

        def conv2d(x, w, b):
            out = jax.lax.conv_general_dilated(x, w, (1, 1), [(PAD, PAD), (PAD, PAD)], dimension_numbers=('NCHW', 'OIHW', 'NCHW'))
            return out + b[None, :, None, None]

        def deform_conv2d(x, offset, mask, w):
            B, C, H, W = x.shape
            Co = w.shape[0]
            Ho, Wo = (offset.shape[2], offset.shape[3])
            off = offset.reshape(B, K, 2, Ho, Wo)
            ky, kx = jnp.meshgrid(jnp.arange(KH), jnp.arange(KW), indexing='ij')
            py = off[:, :, 0] + (ky.reshape(K, 1, 1) + jnp.arange(Ho).reshape(1, Ho, 1) - PAD).astype(x.dtype)
            px = off[:, :, 1] + (kx.reshape(K, 1, 1) + jnp.arange(Wo).reshape(1, 1, Wo) - PAD).astype(x.dtype)
            y0 = jnp.floor(py)
            x0 = jnp.floor(px)
            wy = py - y0
            wx = px - x0
            y0i = y0.astype(jnp.int32)
            x0i = x0.astype(jnp.int32)
            xf = x.reshape(B, C, H * W)
            gather = jax.vmap(lambda xb, idx: jnp.take(xb, idx, axis=1))
            val = jnp.zeros((B, C, K, Ho, Wo), x.dtype)
            corners = [(y0i, x0i, (1 - wy) * (1 - wx)), (y0i, x0i + 1, (1 - wy) * wx), (y0i + 1, x0i, wy * (1 - wx)), (y0i + 1, x0i + 1, wy * wx)]
            for yy, xx, wt in corners:
                valid = (yy >= 0) & (yy < H) & (xx >= 0) & (xx < W)
                flat = jnp.clip(yy, 0, H - 1) * W + jnp.clip(xx, 0, W - 1)
                val = val + gather(xf, flat) * (wt * valid)[:, None]
            val = val * mask[:, None]
            return jnp.einsum('bckhw,ock->bohw', val, w.reshape(Co, -1, K))
        offset = conv2d(x, offset_w, offset_b)
        mask = 2.0 * jax.nn.sigmoid(conv2d(x, mod_w, mod_b))
        y = deform_conv2d(x, offset, mask, reg_w)
        axial = jnp.transpose(y, (0, 2, 3, 1))
        shape = axial.shape
        t, d = (shape[-2], shape[-1])
        axial = axial.reshape(-1, t, d)
        axial = axial.reshape(shape)
        return jnp.transpose(axial, (0, 3, 1, 2))

    def _L2_conv_ref(x, w1, wg, bg, wb, bb):
        import jax, jax.numpy as jnp
        import numpy as np
        B, C, M, N = (8, 64, 256, 256)
        THRESHOLD = 0.8
        EPS = 1e-05
        PAD = 3

        def conv2d(x, w, b=None):
            y = jax.lax.conv_general_dilated(x, w, window_strides=(1, 1), padding=[(PAD, PAD), (PAD, PAD)], dimension_numbers=('NCHW', 'OIHW', 'NCHW'))
            if b is not None:
                y = y + b[None, :, None, None]
            return y

        def region_norm(region, mask):
            s = jnp.sum(region, axis=(0, 2, 3))
            Sr = jnp.sum(mask, axis=(0, 2, 3))
            Sr = jnp.where(Sr == 0, 1.0, Sr)
            mu = (s / Sr)[None, :, None, None]
            t = region + (1.0 - mask) * mu
            m = jnp.mean(t, axis=(0, 2, 3), keepdims=True)
            v = jnp.mean((t - m) ** 2, axis=(0, 2, 3), keepdims=True)
            bn = (t - m) * jax.lax.rsqrt(v + EPS)
            scale = jnp.sqrt(Sr / (region.shape[0] * region.shape[2] * region.shape[3]))
            return bn * scale[None, :, None, None]
        avg_out = jnp.mean(x, axis=1, keepdims=True)
        max_out = jnp.max(x, axis=1, keepdims=True)
        sa_in = jnp.concatenate([avg_out, max_out], axis=1)
        sa_map = jax.nn.sigmoid(conv2d(sa_in, w1))
        gamma = conv2d(sa_map, wg, bg)
        beta = conv2d(sa_map, wb, bb)
        mask = (jax.lax.stop_gradient(sa_map) >= THRESHOLD).astype(x.dtype)
        mask = jnp.broadcast_to(mask, x.shape)
        rn_x = region_norm(x * mask, mask) + region_norm(x * (1.0 - mask), 1.0 - mask)
        return rn_x * (1.0 + gamma) + beta

    def _L3_conv_ref(x, in_proj_weight, in_proj_bias, hid_proj_weight, hid_proj_bias, out_proj_weight, out_proj_bias):
        import jax, jax.numpy as jnp
        import numpy as np
        N, C, H, W, A = (32, 64, 32, 32, 4)
        CHW = C * H * W

        def _xavier(key, shape):
            fan_in, fan_out = (shape[-2], shape[-1])
            limit = float(np.sqrt(6.0 / (fan_in + fan_out)))
            return jax.random.uniform(key, shape, jnp.float32, -limit, limit)
        n, c, h, w = x.shape
        a = in_proj_weight.shape[-1]
        qkv = in_proj_weight[None] * x[:, None, :, :, :, None] + in_proj_bias[None]
        q = qkv[:, 0].reshape(n, -1, a)
        k = qkv[:, 1].reshape(n, -1, a)
        v = qkv[:, 2].reshape(n, -1, a)
        q = jax.nn.softplus(q)
        k = jax.nn.softplus(k)
        s = jnp.cumsum(k[:, :, :, None] * v[:, :, None, :], axis=1)
        z = jnp.cumsum(k, axis=1)
        numer = jnp.einsum('nsi,nsij->nsj', q, s)
        denom = jnp.einsum('nsi,nsi->ns', q, z)[:, :, None]
        y = numer / denom
        y = jnp.concatenate([jnp.ones_like(y[:, :1]), y[:, :-1]], axis=1)
        y = jnp.sum(hid_proj_weight[None] * y[:, None], axis=-1) + hid_proj_bias[None]
        y = jnp.sum(out_proj_weight[None] * jnp.tanh(y), axis=1) + out_proj_bias[None]
        return y.reshape(n, c, h, w)

    def _gn(v, G=32, eps=1e-5):
        B_, C_, H_, W_ = v.shape
        g = v.reshape(B_, G, C_ // G, H_, W_)
        m = jnp.mean(g, axis=(2, 3, 4), keepdims=True)
        s = jnp.var(g, axis=(2, 3, 4), keepdims=True)
        return ((g - m) / jnp.sqrt(s + eps)).reshape(v.shape)

    def _ln_c(v, eps=1e-6):
        m = jnp.mean(v, axis=1, keepdims=True)
        s = jnp.var(v, axis=1, keepdims=True)
        return (v - m) / jnp.sqrt(s + eps)

    def _ln_t(v, eps=1e-5):
        m = jnp.mean(v, axis=-1, keepdims=True)
        s = jnp.var(v, axis=-1, keepdims=True)
        return (v - m) / jnp.sqrt(s + eps)

    def _to_tokens(v):
        B_, C_, H_, W_ = v.shape
        return v.reshape(B_, C_, H_ * W_).transpose(0, 2, 1)
    def _from_tokens(t, like):
        B_, C_, H_, W_ = like.shape
        return t.transpose(0, 2, 1).reshape(B_, C_, H_, W_)

    x = x + _L0_conv_ref(_gn(x), L0_conv_weight, L0_conv_bias, L0_conv_gamma, L0_conv_beta)
    x = x + _L1_conv_ref(_gn(x), L1_conv_offset_w, L1_conv_offset_b, L1_conv_mod_w, L1_conv_mod_b, L1_conv_reg_w)
    x = x + _L2_conv_ref(_gn(x), L2_conv_w1, L2_conv_wg, L2_conv_bg, L2_conv_wb, L2_conv_bb)
    x = x + _L3_conv_ref(_gn(x), L3_conv_in_proj_weight, L3_conv_in_proj_bias, L3_conv_hid_proj_weight, L3_conv_hid_proj_bias, L3_conv_out_proj_weight, L3_conv_out_proj_bias)
    return x


_drawn_inputs = setup_inputs


def setup_inputs(seed=0):
    import zlib

    import numpy as np

    out = dict(_drawn_inputs(seed))
    spreads = {'L0_conv_gamma': (1.0, 0.2),
     'L0_conv_beta': (0.0, 0.1),
     'L1_conv_mod_b': (0.0, 0.8),
     'L3_conv_in_proj_bias': (0.0, 2.0),
     'L3_conv_hid_proj_bias': (0.0, 2.0),
     'L3_conv_out_proj_bias': (0.0, 0.1)}
    factors = {'L1_conv_offset_b': 5.318,
     'L3_conv_in_proj_weight': 64.0,
     'L3_conv_hid_proj_weight': 64.0,
     'L3_conv_out_proj_weight': 24.997}
    for name, (base, spread) in spreads.items():
        noise = np.random.default_rng([zlib.crc32(name.encode()), seed]).standard_normal(out[name].shape)
        drawn = base * np.exp(spread * noise) if base else spread * noise
        out[name] = jnp.asarray(drawn.astype(out[name].dtype))
    for name, factor in factors.items():
        out[name] = (out[name] * factor).astype(out[name].dtype)
    return out
```

```python
import concourse.bass as bass
from concourse import mybir
from contextlib import ExitStack

F32 = mybir.dt.float32
I32 = mybir.dt.int32
U32 = mybir.dt.uint32
ALU = mybir.AluOpType
ACT = mybir.ActivationFunctionType
AX = mybir.AxisListType

B, C, H, W = 16, 64, 32, 32
P = 128
HALF = H * W // 2
RH = H // 2
WP = W + 2
TAPS = 9
GN_EPS = 1e-5


class Chain:

    def __init__(self, eng, sem, base=0):
        self.eng, self.sem, self.n = eng, sem, base

    def __call__(self, ins):
        self.n = self.n + 1
        ins.then_inc(self.sem, 1)
        self.eng.wait_ge(self.sem, self.n)


def group_norm_vector(nc, dve, link, x, t, s):
    for b in range(B):
        last = nc.vector.bn_stats(t["st"][:, b, :], x[:, b, :])
    link(last)
    for b in range(B):
        last = nc.vector.bn_aggr(t["mv"][:, b, :], t["st"][:, b, :])
    last.then_inc(s["row_stats"], 1)
    join_groups_vector(nc, dve, link, t["mv"][:, :, 0], t["mv"][:, :, 1], B, t, s)
    link(nc.vector.scalar_tensor_tensor(out=t["shift"][:, 0:B], in0=t["mean"][:, 0:B], scalar=-1.0,
                                        in1=t["scale"][:, 0:B], op0=ALU.mult, op1=ALU.mult))


def join_groups_vector(nc, dve, link, mean, var, n, t, s):
    dve.wait_ge(s["joined_mean"], 1)
    link(nc.vector.tensor_copy(t["mean"][:, 0:n], t["ps"][:, 0:n]))
    link(nc.vector.tensor_tensor(t["dev"][:, 0:n], mean, t["mean"][:, 0:n], ALU.subtract))
    link(nc.vector.tensor_tensor(t["dev"][:, 0:n], t["dev"][:, 0:n], t["dev"][:, 0:n], ALU.mult))
    nc.vector.tensor_tensor(t["dev"][:, 0:n], t["dev"][:, 0:n], var, ALU.add).then_inc(s["spread"], 1)
    dve.wait_ge(s["joined_var"], 1)
    nc.vector.tensor_scalar(t["var"][:, 0:n], t["ps"][:, B:B + n], GN_EPS, None, ALU.add).then_inc(s["var_eps"], 1)
    dve.wait_ge(s["deviation"], 1)
    link(nc.vector.reciprocal(t["scale"][:, 0:n], t["sd"][:, 0:n]))


def join_groups_tensor(nc, pe, matrix, mean, n, t, s):
    pe.wait_ge(s["row_stats"], 1)
    nc.tensor.matmul(t["ps"][:, 0:n], matrix, mean, start=True, stop=True).then_inc(s["joined_mean"], 1)
    pe.wait_ge(s["spread"], 1)
    nc.tensor.matmul(t["ps"][:, B:B + n], matrix, t["dev"][:, 0:n], start=True, stop=True).then_inc(s["joined_var"], 1)


def join_groups_scalar(nc, act, n, t, s):
    act.wait_ge(s["var_eps"], 1)
    nc.scalar.activation(t["sd"][:, 0:n], t["var"][:, 0:n], ACT.Sqrt).then_inc(s["deviation"], 1)


STAT_SEMS = ["row_stats", "joined_mean", "spread", "joined_var", "var_eps", "deviation"]


def stat_buffers(nc, ctx, tag):
    def sb(name, cols):
        return ctx.enter_context(nc.sbuf_tensor(f"{tag}_{name}", cols, F32))

    t = {"st": sb("st", [P, B, 6]), "mv": sb("mv", [P, B, 2])}
    for name in ("mean", "dev", "var", "sd", "scale", "shift"):
        t[name] = sb(name, [P, B])
    t["ps"] = ctx.enter_context(nc.psum_tensor(f"{tag}_ps", [P, 2 * B], F32))
    s = {name: ctx.enter_context(nc.semaphore(f"{tag}_{name}")) for name in STAT_SEMS}
    return t, s


def layer0(nc, xt, d):
    NQ, PX = 4, 8
    RING = 4
    with ExitStack() as ctx:
        def sb(name, shape):
            return ctx.enter_context(nc.sbuf_tensor(name, shape, F32))

        def sem(name):
            return ctx.enter_context(nc.semaphore(name))

        gn, gs = stat_buffers(nc, ctx, "gn0")
        bn, bs = stat_buffers(nc, ctx, "bn0")
        xh = sb("xh", [P, RH + 2, WP, B])
        win_a = sb("win_a", [P, 2, 2, 3, WP, B])
        win_b = sb("win_b", [P, 2, 2, W, B])
        ring = sb("ring", [P, RING, PX, TAPS, C])
        bias = sb("bias0", [P, HALF])
        gnmat = sb("gnmat0", [P, P])
        bnmat = sb("bnmat0", [P, P])
        affine = sb("affine0", [P, 2])
        fold = sb("fold0", [P, 2])
        acc = [ctx.enter_context(nc.psum_tensor(f"acc0_{i}", [P, W * B], F32)) for i in range(2)]

        x_in = sem("x_in"); consts_in = sem("consts_in")
        w_in = [sem(f"w_in{i}") for i in range(RING)]
        w_used = sem("w_used")
        own_dve = sem("own_dve"); border_done = sem("border_done")
        norm_done = sem("norm_done"); xh_ready = sem("xh_ready")
        win_a_ready = sem("win_a_ready"); win_b_ready = sem("win_b_ready")
        row_stored = sem("row_stored")
        bn_ready = sem("bn_ready"); slot_free = sem("slot_free"); relu_done = sem("relu_done"); xr_in = sem("xr_in")
        block = ctx.enter_context(nc.Block())
        xr = ring[:, 0:2].rearrange("p s a t c -> p (s a t c)")[:, 0:B * HALF].rearrange("p (b x) -> p b x", b=B)

        @block.sync
        def _(sp):
            sp.dma_start(xt[:], d["x"][:]).then_inc(x_in, 16)
            for name, tile in (("gnmat", gnmat), ("bnmat", bnmat), ("bias0", bias), ("affine0", affine)):
                sp.dma_start(tile[:], d[name][:]).then_inc(consts_in, 16)
            for q in range(NQ):
                sp.dma_start(ring[:, q], d["w0"][0, q]).then_inc(w_in[q], 16)
            with sp.Fori(1, RH) as r:
                for q in range(NQ):
                    sp.wait_ge(w_used, r * NQ + (q - NQ + 1))
                    sp.dma_start(ring[:, q], d["w0"][r, q]).then_inc(w_in[q], 16)
            sp.wait_ge(w_used, RH * NQ)
            sp.dma_start(xr, d["x"][:]).then_inc(xr_in, 16)

        @block.gpsimd
        def _(pool):
            nc.gpsimd.memset(xh[:], 0.0).then_inc(border_done, 1)

        @block.scalar
        def _(act):
            join_groups_scalar(nc, act, B, gn, gs)
            act.wait_ge(norm_done, 1)
            act.wait_ge(border_done, 1)
            xv = xh[:].rearrange("p r w b -> p b r w")
            for b in range(B):
                last = nc.scalar.activation(xv[:, b, 1:RH + 1, 1:W + 1],
                                            xt[:, b, :].rearrange("p (r w) -> p r w", w=W), ACT.Identity,
                                            bias=gn["shift"][:, b:b + 1], scale=gn["scale"][:, b:b + 1])
            last.then_inc(xh_ready, 1)


            def windows(r, u, first):
                if first:
                    act.wait_ge(xh_ready, 3)
                else:
                    act.wait_ge(w_used, NQ * r - NQ)
                    act.sem_inc(slot_free, 1)
                for h in range(2):
                    src = xh[h * C:(h + 1) * C]
                    nc.scalar.activation(win_b[0:C, u, h], src[:, bass.ds(r, 1), 2:WP].rearrange("p r w b -> p (r w) b"),
                                         ACT.Copy).then_inc(win_b_ready, 1)
                    nc.scalar.activation(win_b[C:P, u, h], src[:, bass.ds(r + 1, 1), 2:WP].rearrange("p r w b -> p (r w) b"),
                                         ACT.Copy).then_inc(win_b_ready, 1)

            for u in range(2):
                windows(u, u, True)
            with act.Fori(1, RH // 2) as rr:
                for u in range(2):
                    windows(rr * 2 + u, u, False)
            join_groups_scalar(nc, act, 1, bn, bs)
            act.wait_ge(bn_ready, 1)
            for b in range(B):
                nc.scalar.activation(xt[:, b, :], xt[:, b, :], ACT.Relu, bias=fold[:, 1:2],
                                     scale=fold[:, 0:1]).then_inc(relu_done, 1)

        @block.vector
        def _(dve):
            link = Chain(dve, own_dve)
            dve.wait_ge(x_in, 16)
            group_norm_vector(nc, dve, link, xt, gn, gs)
            nc.vector.tensor_copy(gn["st"][:, 0, 0:1], gn["st"][:, 0, 0:1]).then_inc(norm_done, 1)
            dve.wait_ge(xh_ready, 1)
            nc.vector.tensor_copy(xh[0:C, RH + 1], xh[C:P, 1]).then_inc(xh_ready, 1)
            nc.vector.tensor_copy(xh[C:P, 0], xh[0:C, RH]).then_inc(xh_ready, 1)
            dve.wait_ge(xh_ready, 3)

            def windows(r, u, first):
                if not first:
                    dve.wait_ge(w_used, NQ * r - NQ)
                for h in range(2):
                    src = xh[h * C:(h + 1) * C]
                    nc.vector.tensor_copy(win_a[0:C, u, h], src[:, bass.ds(r, 3)]).then_inc(win_a_ready, 1)
                    nc.vector.tensor_copy(win_a[C:P, u, h, :, 0:WP - 1], src[:, bass.ds(r, 3), 1:WP]).then_inc(win_a_ready, 1)

            def store(r, u):
                dve.wait_ge(w_used, NQ * r + NQ)
                bcol = bias[:, bass.ds(r * W, W)].rearrange("p (o w) -> p o w", o=1).to_broadcast([P, B, W])
                nc.vector.tensor_tensor(xt[:, :, bass.ds(r * W, W)], acc[u][:].rearrange("p (w b) -> p b w", b=B),
                                        bcol, ALU.add).then_inc(row_stored, 1)

            dve.wait_ge(consts_in, 64)
            for u in range(2):
                windows(u, u, True)
            with dve.Fori(1, RH // 2) as rr:
                for u in range(2):
                    store(rr * 2 + (u - 2), u)
                    windows(rr * 2 + u, u, False)
            for u in range(2):
                store(RH - 2 + u, u)
            dve.wait_ge(row_stored, RH)
            for b in range(B):
                last = nc.vector.bn_stats(bn["st"][:, b, :], xt[:, b, :])
            link(last)
            nc.vector.bn_aggr(bn["mv"][:, 0, :], bn["st"][:].rearrange("p b s -> p (b s)")).then_inc(bs["row_stats"], 1)
            join_groups_vector(nc, dve, link, bn["mv"][:, 0, 0:1], bn["mv"][:, 0, 1:2], 1, bn, bs)
            link(nc.vector.tensor_tensor(fold[:, 0:1], bn["scale"][:, 0:1], affine[:, 0:1], ALU.mult))
            link(nc.vector.tensor_tensor(fold[:, 1:2], bn["mean"][:, 0:1], fold[:, 0:1], ALU.mult))
            nc.vector.tensor_tensor(fold[:, 1:2], affine[:, 1:2], fold[:, 1:2], ALU.subtract).then_inc(bn_ready, 1)
            dve.wait_ge(xr_in, 16)
            for b in range(B):
                dve.wait_ge(relu_done, b + 1)
                nc.vector.tensor_tensor(xt[:, b, :], xt[:, b, :], xr[:, b, :], ALU.add)

        @block.tensor
        def _(pe):
            pe.wait_ge(consts_in, 64)
            join_groups_tensor(nc, pe, gnmat[:], gn["mv"][:, :, 0], B, gn, gs)

            def row(r, u, first):
                pe.wait_ge(win_a_ready, 4 * r + 4)
                pe.wait_ge(win_b_ready, 4 * r + 4)
                if not first:
                    pe.wait_ge(row_stored, r - 1)
                for q in range(NQ):
                    pe.wait_ge(w_in[q], 16 * r + 16)
                    wt = ring[:, q]
                    for k in range(PX):
                        j = q * PX + k
                        for m in range(4):
                            for h in range(2):
                                if m < 3:
                                    mov = win_a[:, u, h, m, j]
                                else:
                                    mov = win_b[:, u, h, j]
                                nc.tensor.matmul(acc[u][h * C:(h + 1) * C, j * B:(j + 1) * B], wt[:, k, 4 * h + m], mov,
                                                 start=(j == 0 and m == 0), stop=False)
                    for k in range(PX):
                        j = q * PX + k
                        for h in range(2):
                            last = nc.tensor.matmul(acc[u][h * C:(h + 1) * C, j * B:(j + 1) * B],
                                                    wt[h * C:(h + 1) * C, k, 8],
                                                    win_a[h * C:(h + 1) * C, u, h, 2, j + 2 - h],
                                                    start=False, stop=(j == W - 1))
                    last.then_inc(w_used, 1)
            def rows(rr, first):
                for u in range(2):
                    row(rr * 2 + u, u, first)
            rows(0, True)
            with pe.Fori(1, RH // 2) as rr:
                rows(rr, False)
            pe.wait_ge(w_used, RH * NQ)
            join_groups_tensor(nc, pe, bnmat[:], bn["mv"][:, 0, 0:1], 1, bn, bs)



ENTRY = 4 * C
NT = H * W // P


def layer1(nc, xt, d):
    SLOTS = 4
    tables = [nc.dram_tensor(f"table{u}", (WP, WP, 4, C), F32, kind="Internal").ap() for u in range(2)]
    entries = [t.rearrange("y x n c -> (y x) (n c)") for t in tables]
    with ExitStack() as ctx:
        def sb(name, shape, dt=F32):
            return ctx.enter_context(nc.sbuf_tensor(name + "_1", shape, dt))

        def pb(name, shape):
            return ctx.enter_context(nc.psum_tensor(name + "_1", shape, F32))

        def sem(name):
            return ctx.enter_context(nc.semaphore(name + "_1"))

        gn, gs = stat_buffers(nc, ctx, "gn1")
        xn = sb("xn", [P, B, HALF])
        zero = sb("zero", [WP, ENTRY])
        pad01 = [sb(f"pad01_{u}", [P, WP, W]) for u in range(2)]
        pad22 = [sb(f"pad22_{u}", [P, WP, W]) for u in range(2)]
        pix = [sb(f"pix{u}", [P, NT, C]) for u in range(2)]
        gath = sb("gath", [P, SLOTS, TAPS, 4, C])
        cols = [sb(f"cols{u}", [P, TAPS, P]) for u in range(2)]
        wconv = sb("wconv", [P, 5, 27]); wreg = sb("wreg", [P, TAPS, C])
        ident = sb("ident", [P, P]); gnmat = sb("gnmat", [P, P])
        base = sb("base", [P, NT, 18]); obias = sb("obias", [P, 27])
        off = sb("off", [P, NT, 27]); pos = sb("pos", [P, NT, 18]); posi = sb("posi", [P, NT, 18], I32)
        low = sb("low", [P, NT, 18]); over = sb("over", [P, NT, 18])
        frac = sb("frac", [P, NT, 18]); rest = sb("rest", [P, NT, 18])
        gate = sb("gate", [P, NT, TAPS]); rowg = sb("rowg", [P, 2, NT, TAPS]); flat = sb("flat", [P, NT, TAPS])
        idx = [sb(f"idx{u}", [P, NT, TAPS], I32) for u in range(2)]
        wts = [sb(f"wts{u}", [P, NT, TAPS, 4]) for u in range(2)]
        p_off = pb("p_off", [P, 2, 256])
        p_pix = pb("p_pix", [P, NT, C])
        p_col = [pb(f"p_col{g}", [P, 3, P]) for g in range(3)]
        p_y = [pb(f"p_y{u}", [P, HALF]) for u in range(2)]

        consts_in = sem("consts_in"); own_dve = sem("own_dve"); norm_done = sem("norm_done"); xn_ready = sem("xn_ready")
        zero_ready = sem("zero_ready"); border_out = sem("border_out"); slot_free = sem("slot_free"); own_pool = sem("own_pool")
        pad_clear = sem("pad_clear"); pad_ready = sem("pad_ready"); conv_done = sem("conv_done")
        turned = sem("turned"); pix_ready = sem("pix_ready"); table_out = [sem(f"table_out{u}") for u in range(2)]
        off_ready = sem("off_ready"); gate_ready = sem("gate_ready"); coords_ready = sem("coords_ready")
        gath_in = [sem(f"gath_in{s}") for s in range(SLOTS)]
        weighted = sem("weighted"); turned_taps = sem("turned_taps"); cols_ready = sem("cols_ready")
        tile_done = sem("tile_done"); y_added = sem("y_added")
        block = ctx.enter_context(nc.Block())
        NCONST = 7

        def over_batches(eng, prep, main):
            prep(0, 0)
            prep(1, 1)
            main(0, 0)
            with eng.Fori(1, B // 2) as rr:
                prep(rr * 2, 0)
                main(rr * 2 - 1, 1)
                prep(rr * 2 + 1, 1)
                main(rr * 2, 0)
            main(B - 1, 1)

        def known(b):
            return isinstance(b, int)

        @block.sync
        def _(sp):
            for name, tile in (("wconv", wconv), ("wreg", wreg), ("ident", ident), ("gnmat", gnmat), ("base", base),
                               ("obias", obias)):
                sp.dma_start(tile[:], d[name][:]).then_inc(consts_in, 16)
            sp.wait_ge(zero_ready, 1)
            for table in tables:
                for e in (0, H, H + 1):
                    sp.dma_start(table[e].rearrange("x n c -> x (n c)"), zero[:]).then_inc(border_out, 16)
            sp.wait_ge(border_out, 96)
            for table in tables:
                for e in (0, H, H + 1):
                    sp.dma_start(table[:, e].rearrange("y n c -> y (n c)"), zero[:]).then_inc(border_out, 16)
            sp.wait_ge(border_out, 192)

            def prep(b, u):
                sp.wait_ge(pix_ready, b + 1)
                if not known(b):
                    sp.wait_ge(weighted, (b - 1) * NT * 2)
                for n in range(4):
                    y0, x0 = 1 - n // 2, 1 - n % 2
                    for r in range(4):
                        dst = tables[u][y0:y0 + H, x0:x0 + W, n, :].rearrange("(t r) x c -> r x t c", r=4)[r]
                        sp.dma_start(dst, pix[u][r * W:(r + 1) * W]).then_inc(table_out[u], 16)

            over_batches(sp, prep, lambda b, u: None)
            for u in range(2):
                sp.wait_ge(table_out[u], 256 * (B // 2))

        @block.gpsimd
        def _(pool):
            nc.gpsimd.memset(zero[:], 0.0).then_inc(zero_ready, 1)
            for tile in (*pad01, *pad22):
                nc.gpsimd.memset(tile[:], 0.0).then_inc(pad_clear, 1)

            pool.wait_ge(border_out, 192)

            def main(b, u):
                pool.wait_ge(coords_ready, b + 1)
                if known(b):
                    pool.wait_ge(table_out[u], 256 * (b // 2 + 1))
                elif u == 0:
                    pool.wait_ge(table_out[u], b * 128 + 256)
                else:
                    pool.wait_ge(table_out[u], (b + 1) * 128)
                for t in range(NT):
                    if not (known(b) and b == 0 and t < SLOTS):
                        pool.wait_ge(turned_taps, (b * NT + (t + 1 - SLOTS)) * 3)
                        pool.sem_inc(slot_free, 1)
                    for k in range(TAPS):
                        nc.gpsimd.indirect_dma_start(
                            out=gath[:, t % SLOTS, k].rearrange("p n c -> p (n c)"), out_offset=None, in_=entries[u],
                            in_offset=bass.IndirectOffsetOnAxis(ap=idx[u][:, t, k:k + 1], axis=0),
                        ).then_inc(gath_in[t % SLOTS], 16)

            over_batches(pool, lambda b, u: None, main)

        @block.scalar
        def _(act):
            join_groups_scalar(nc, act, B, gn, gs)
            act.wait_ge(norm_done, 1)
            for b in range(B):
                last = nc.scalar.activation(xn[:, b, :], xt[:, b, :], ACT.Identity,
                                            bias=gn["shift"][:, b:b + 1], scale=gn["scale"][:, b:b + 1])
            last.then_inc(xn_ready, 1)
            act.wait_ge(pad_clear, 4)

            def prep(b, u):
                if not known(b):
                    act.wait_ge(conv_done, b - 1)
                act.wait_ge(xn_ready, 1)
                for h in range(2):
                    src = xn[h * C:(h + 1) * C, bass.ds(b, 1), :].rearrange("p o (r w) -> p (o r) w", w=W)
                    rows, rows_on = slice(1 + h * RH, 1 + (h + 1) * RH), slice(h * RH, (h + 1) * RH)
                    nc.scalar.activation(pad01[u][0:C, rows, 1:W], src[:, :, 0:W - 1], ACT.Copy).then_inc(pad_ready, 1)
                    nc.scalar.activation(pad01[u][C:P, rows], src, ACT.Copy).then_inc(pad_ready, 1)
                    nc.scalar.activation(pad22[u][0:C, rows, 0:W - 1], src[:, :, 1:W], ACT.Copy).then_inc(pad_ready, 1)
                    nc.scalar.activation(pad22[u][C:P, rows_on, 0:W - 1], src[:, :, 1:W], ACT.Copy).then_inc(pad_ready, 1)
                if known(b):
                    act.wait_ge(turned, b + 1)
                else:
                    act.wait_ge(turned, b + 1)
                    act.wait_ge(table_out[u], b * 128 if u == 0 else (b - 1) * 128)
                nc.scalar.activation(pix[u][:], p_pix[:], ACT.Copy).then_inc(pix_ready, 1)
                act.wait_ge(off_ready, b + 1)
                nc.scalar.activation(gate[:], off[:, :, 18:27], ACT.Sigmoid).then_inc(gate_ready, 1)

            def main(b, u):
                for t in range(NT):
                    if not (known(b) and b == 0 and t < 2):
                        act.wait_ge(tile_done, b * NT + (t - 1))
                    for g in range(3):
                        act.wait_ge(turned_taps, (b * NT + t) * 3 + (g + 1))
                        nc.scalar.activation(cols[t % 2][:, 3 * g:3 * g + 3], p_col[g][:], ACT.Copy).then_inc(cols_ready, 1)

            over_batches(act, prep, main)

        @block.vector
        def _(dve):
            link = Chain(dve, own_dve)
            group_norm_vector(nc, dve, link, xt, gn, gs)
            dve.nop().then_inc(norm_done, 1)
            dve.wait_ge(consts_in, 96)
            start = link.n
            STEPS = 13

            def prep(b, u):
                step = Chain(dve, own_dve, b * STEPS + start)
                tt, ts = nc.vector.tensor_tensor, nc.vector.tensor_scalar
                dve.wait_ge(conv_done, b + 1)
                if not (known(b) and b == 0):
                    dve.wait_ge(gate_ready, b)
                step(tt(off[:], p_off[:, u, 0:NT * 27].rearrange("p (t n) -> p t n", t=NT),
                        obias[:].rearrange("p (o n) -> p o n", o=1).to_broadcast([P, NT, 27]), ALU.add))
                tt(pos[:], off[:, :, 0:18], base[:], ALU.add).then_inc(off_ready, 1)
                dve.wait_ge(off_ready, b + 1)
                step(ts(pos[:], pos[:], -1.0, float(H), ALU.max, ALU.min))
                step(nc.vector.tensor_copy(posi[:], pos[:]))
                step(nc.vector.tensor_copy(low[:], posi[:]))
                step(tt(over[:], low[:], pos[:], ALU.is_gt))
                step(tt(low[:], low[:], over[:], ALU.subtract))
                step(tt(frac[:], pos[:], low[:], ALU.subtract))
                step(ts(rest[:], frac[:], -1.0, 1.0, ALU.mult, ALU.add))
                step(nc.vector.scalar_tensor_tensor(out=flat[:], in0=low[:, :, 0::2], scalar=float(WP), in1=low[:, :, 1::2],
                                                    op0=ALU.mult, op1=ALU.add))
                step(ts(idx[u][:], flat[:], float(WP + 1), None, ALU.add))
                dve.wait_ge(gate_ready, b + 1)
                step(ts(gate[:], gate[:], 2.0, None, ALU.mult))
                step(tt(rowg[:, 0], rest[:, :, 0::2], gate[:], ALU.mult))
                step(tt(rowg[:, 1], frac[:, :, 0::2], gate[:], ALU.mult))
                for n in range(4):
                    last = tt(wts[u][:, :, :, n], rowg[:, n // 2], (frac if n % 2 else rest)[:, :, 1::2], ALU.mult)
                last.then_inc(coords_ready, 1)
                dve.wait_ge(coords_ready, b + 1)

            def main(b, u):
                for t in range(NT):
                    uses = 2 * b + t // SLOTS + 1
                    dve.wait_ge(gath_in[t % SLOTS], uses * (16 * TAPS))
                    e = gath[:, t % SLOTS]
                    g = e.rearrange("p k n c -> p (k n) c")
                    w = wts[u][:, t].rearrange("p k n -> p (k n)").rearrange("p (m o) -> p m o", o=1).to_broadcast([P, 4 * TAPS, C])
                    nc.vector.tensor_tensor(g, g, w, ALU.mult).then_inc(weighted, 1)
                    dve.wait_ge(weighted, (b * NT + t) * 2 + 1)
                    nc.vector.tensor_tensor(e[:, :, 0:2], e[:, :, 0:2], e[:, :, 2:4], ALU.add).then_inc(weighted, 1)
                dve.wait_ge(tile_done, b * NT + NT)
                nc.vector.tensor_tensor(xt[:, bass.ds(b, 1), :].rearrange("p o x -> p (o x)"),
                                        xt[:, bass.ds(b, 1), :].rearrange("p o x -> p (o x)"), p_y[u][:], ALU.add).then_inc(y_added, 1)

            over_batches(dve, prep, main)

        @block.tensor
        def _(pe):
            pe.wait_ge(consts_in, 96)
            join_groups_tensor(nc, pe, gnmat[:], gn["mv"][:, :, 0], B, gn, gs)
            pe.wait_ge(xn_ready, 1)

            def prep(b, u):
                if not (known(b) and b == 0):
                    pe.wait_ge(pix_ready, b)
                pe.wait_ge(pad_ready, b * 8 + 8)
                if not known(b):
                    pe.wait_ge(coords_ready, b - 1)
                for t in range(NT):
                    for m in range(5):
                        k = C if m == 4 else P
                        src, r0 = (pad01[u], m) if m < 3 else (pad22[u], 2 * (m - 3))
                        lhs = src[0:k, 4 * t + r0:4 * t + r0 + 4].rearrange("p r w -> p (r w)")
                        last = nc.tensor.matmul(p_off[:, u, t * 27:(t + 1) * 27], lhs, wconv[0:k, m],
                                                start=(m == 0), stop=(m == 4))
                last.then_inc(conv_done, 1)
                for t in range(NT):
                    last = nc.tensor.transpose(p_pix[:, t], pad01[u][C:P, 1 + 4 * t:5 + 4 * t].rearrange("p r w -> p (r w)"),
                                               ident[C:P, C:P])
                last.then_inc(turned, 1)

            def main(b, u):
                if not known(b):
                    pe.wait_ge(y_added, b - 1)
                elif b >= 2:
                    pe.wait_ge(y_added, b - 1)

                def finish(t):
                    pe.wait_ge(cols_ready, (b * NT + (t + 1)) * 3)
                    h, q = t // 4, t % 4
                    for k in range(TAPS):
                        last = nc.tensor.matmul(p_y[u][h * C:(h + 1) * C, q * P:(q + 1) * P], wreg[:, k], cols[t % 2][:, k],
                                                start=(k == 0), stop=(k == TAPS - 1))
                    last.then_inc(tile_done, 1)

                for t in range(NT):
                    pe.wait_ge(weighted, (b * NT + (t + 1)) * 2)
                    for g in range(3):
                        if not (known(b) and b == 0 and t < 1):
                            pe.wait_ge(cols_ready, (b * NT + (t - 1)) * 3 + (g + 1))
                        for k in range(3):
                            last = nc.tensor.transpose(p_col[g][:, k],
                                                       gath[:, t % SLOTS, 3 * g + k, 0:2].rearrange("p n c -> p (n c)"), ident[:])
                        last.then_inc(turned_taps, 1)
                    if t:
                        finish(t - 1)
                finish(NT - 1)

            over_batches(pe, prep, main)



MAP_K, REACH = 7, 3
THRESHOLD = 0.8


def layer2(nc, xt, d):
    N = B * H * W
    with ExitStack() as ctx:
        def sb(name, shape, dt=F32):
            return ctx.enter_context(nc.sbuf_tensor(name + "_2", shape, dt))

        def pb(name, shape):
            return ctx.enter_context(nc.psum_tensor(name + "_2", shape, F32))

        def sem(name):
            return ctx.enter_context(nc.semaphore(name + "_2"))

        gn, gs = stat_buffers(nc, ctx, "gn2")
        xn = sb("xn", [P, B, HALF]); maskc = sb("maskc", [P, B, HALF])
        scratch = [sb(f"scratch{u}", [P, HALF]) for u in range(2)]
        spare = sb("spare", [P, 2, HALF])
        upper = [sb(f"upper{u}", [P, HALF]) for u in range(2)]
        lower = [sb(f"lower{u}", [P, HALF]) for u in range(2)]
        band = sb("band", [P, 12, P]); ident = sb("ident", [P, P]); gnmat = sb("gnmat", [P, P]); bnmat = sb("bnmat", [P, P])
        ones = sb("ones", [P, P]); mbias = sb("mbias", [P, 2])
        pooled = sb("pooled", [P, 2, NT + 2, B])
        attn = sb("attn", [P, NT + 2, B])
        mask = sb("mask", [P, NT, B]); mod = sb("mod", [P, 2, NT, B])
        sums = sb("sums", [P, 4, B])
        tot = sb("tot", [P, 4]); pair = sb("pair", [P, 4]); size = sb("size", [P, 2]); sizew = sb("sizew", [P, 2])
        rs = sb("rs", [P, 2]); rq = sb("rq", [P, 2]); mu = sb("mu", [P, 2]); amp2 = sb("amp2", [P, 2]); amp = sb("amp", [P, 2])
        tmp = sb("tmp", [P, 2]); cst = sb("cst", [P, 2]); damp = sb("damp", [P, 1]); dcst = sb("dcst", [P, 1]); ncst = sb("ncst", [P, 1])
        p_t = [pb(f"p_t{u}", [P, 4, 2, C]) for u in range(2)]
        p_m = pb("p_m", [P, 4, P])
        p_g = [pb(f"p_g{u}", [P, HALF]) for u in range(2)]
        p_b = [pb(f"p_b{u}", [P, HALF]) for u in range(2)]

        consts_in = sem("consts_in"); own_dve = sem("own_dve"); norm_done = sem("norm_done"); xn_ready = sem("xn_ready")
        turned = sem("turned"); reduced = sem("reduced"); pooled_ready = sem("pooled_ready"); map_conv = sem("map_conv")
        attn_ready = sem("attn_ready"); mods_conv = sem("mods_conv"); mask_ready = sem("mask_ready"); counted = sem("counted")
        mask_spread = sem("mask_spread"); maskc_ready = sem("maskc_ready"); masked_sums = sem("masked_sums")
        plain_sums = sem("plain_sums"); totals = sem("totals"); paired = sem("paired"); amp2_ready = sem("amp2_ready")
        amp_ready = sem("amp_ready"); coef_ready = sem("coef_ready"); affine_ready = sem("affine_ready")
        mod_ready = sem("mod_ready"); mod_spread = sem("mod_spread"); joined = sem("joined"); batch_done = sem("batch_done")
        zeroed = sem("zeroed"); own_pool = sem("own_pool")
        block = ctx.enter_context(nc.Block())

        @block.sync
        def _(sp):
            for name, tile in (("gnmat", gnmat), ("bnmat", bnmat), ("ident", ident), ("band", band), ("mbias", mbias)):
                sp.dma_start(tile[:], d[name][:]).then_inc(consts_in, 16)

        @block.gpsimd
        def _(pool):
            nc.gpsimd.memset(pooled[:], 0.0).then_inc(zeroed, 1)
            nc.gpsimd.memset(attn[:], 0.0).then_inc(zeroed, 1)
            nc.gpsimd.memset(ones[:], 1.0).then_inc(zeroed, 1)
            for b in range(B):
                u = b % 2
                pool.wait_ge(affine_ready, b + 1)
                nc.gpsimd.tensor_tensor(upper[u][:], upper[u][:], maskc[:, b], ALU.mult).then_inc(own_pool, 1)
                pool.wait_ge(own_pool, b + 1)
                nc.gpsimd.tensor_tensor(upper[u][:], upper[u][:], lower[u][:], ALU.add).then_inc(joined, 1)

        @block.scalar
        def _(act):
            join_groups_scalar(nc, act, B, gn, gs)
            act.wait_ge(norm_done, 1)
            for b in range(B):
                nc.scalar.activation(xn[:, b, :], xt[:, b, :], ACT.Identity, bias=gn["shift"][:, b:b + 1],
                                     scale=gn["scale"][:, b:b + 1]).then_inc(xn_ready, 1)
            act.wait_ge(map_conv, 1)
            nc.scalar.activation(attn[:, 1:NT + 1].rearrange("p t b -> p (t b)"), p_m[:, 0], ACT.Sigmoid).then_inc(attn_ready, 1)
            act.wait_ge(xn_ready, B)
            for b in range(B):
                if b:
                    act.wait_ge(plain_sums, 2 * b)
                nc.scalar.activation(spare[:, 0], xn[:, b], ACT.Copy, accum_out=sums[:, 2, b:b + 1]).then_inc(plain_sums, 1)
                nc.scalar.activation(spare[:, 1], xn[:, b], ACT.Square, accum_out=sums[:, 3, b:b + 1]).then_inc(plain_sums, 1)
                act.wait_ge(mask_spread, b + 1)
                nc.scalar.activation(maskc[:, b], p_g[b % 2][:], ACT.Copy).then_inc(maskc_ready, 1)
            act.wait_ge(amp2_ready, 1)
            nc.scalar.activation(amp[:], amp2[:], ACT.Sqrt).then_inc(amp_ready, 1)
            act.wait_ge(coef_ready, 1)
            for b in range(B):
                u = b % 2
                if b >= 2:
                    act.wait_ge(batch_done, b - 1)
                nc.scalar.activation(upper[u][:], xn[:, b], ACT.Identity, bias=dcst[:], scale=damp[:])
                nc.scalar.activation(lower[u][:], xn[:, b], ACT.Identity, bias=ncst[:], scale=amp[:, 1:2]).then_inc(affine_ready, 1)

        @block.vector
        def _(dve):
            tt, ts, stt = nc.vector.tensor_tensor, nc.vector.tensor_scalar, nc.vector.scalar_tensor_tensor
            link = Chain(dve, own_dve)
            group_norm_vector(nc, dve, link, xt, gn, gs)
            dve.nop().then_inc(norm_done, 1)
            dve.wait_ge(zeroed, 2)
            for b in range(B):
                dve.wait_ge(turned, b + 1)
                for n, op in ((0, ALU.add), (1, ALU.max)):
                    last = nc.vector.tensor_reduce(pooled[:, n, 1:NT + 1, b].rearrange("p (h q) -> p q h", h=2),
                                                   p_t[b % 2][:], AX.X, op)
                last.then_inc(reduced, 1)
            dve.wait_ge(reduced, B)
            ts(pooled[:, 0], pooled[:, 0], 1.0 / C, None, ALU.mult).then_inc(pooled_ready, 1)
            dve.wait_ge(attn_ready, 1)
            ts(mask[:], attn[:, 1:NT + 1], THRESHOLD, None, ALU.is_ge).then_inc(mask_ready, 1)
            dve.wait_ge(mods_conv, 1)
            dve.wait_ge(counted, 1)
            link(ts(mod[:, 0].rearrange("p t b -> p (t b)"), p_m[:, 1], mbias[:, 0:1], 1.0, ALU.add, ALU.add))
            ts(mod[:, 1].rearrange("p t b -> p (t b)"), p_m[:, 2], mbias[:, 1:2], None, ALU.add).then_inc(mod_ready, 1)
            link(nc.vector.tensor_reduce(size[:, 0:1], p_m[:, 3], AX.X, ALU.add))
            link(ts(size[:, 1:2], size[:, 0:1], -1.0, float(N), ALU.mult, ALU.add))
            link(ts(sizew[:], size[:], 1.0, None, ALU.max))
            for b in range(B):
                dve.wait_ge(maskc_ready, b + 1)
                s = scratch[b % 2]
                link(stt(out=s[:], in0=xn[:, b], scalar=1.0, in1=maskc[:, b], op0=ALU.mult, op1=ALU.mult,
                         accum_out=sums[:, 0, b:b + 1]))
                stt(out=s[:], in0=s[:], scalar=1.0, in1=xn[:, b], op0=ALU.mult, op1=ALU.mult,
                    accum_out=sums[:, 1, b:b + 1]).then_inc(masked_sums, 1)
            dve.wait_ge(masked_sums, B)
            dve.wait_ge(plain_sums, 2 * B)
            nc.vector.tensor_reduce(tot[:], sums[:], AX.X, ALU.add).then_inc(totals, 1)
            dve.wait_ge(paired, 1)
            link(ts(pair[:], gn["ps"][:, 0:4], 2.0, None, ALU.mult))
            link(nc.vector.tensor_copy(rs[:, 0:1], pair[:, 0:1]))
            link(tt(rs[:, 1:2], pair[:, 2:3], pair[:, 0:1], ALU.subtract))
            link(nc.vector.tensor_copy(rq[:, 0:1], pair[:, 1:2]))
            link(tt(rq[:, 1:2], pair[:, 3:4], pair[:, 1:2], ALU.subtract))
            link(nc.vector.reciprocal(tmp[:], sizew[:]))
            link(tt(mu[:], rs[:], tmp[:], ALU.mult))
            link(tt(tmp[:], mu[:], rs[:], ALU.mult))
            link(tt(rq[:], rq[:], tmp[:], ALU.subtract))
            link(ts(rq[:], rq[:], 0.0, 1.0 / N, ALU.max, ALU.mult))
            link(ts(rq[:], rq[:], GN_EPS, None, ALU.add))
            link(nc.vector.reciprocal(tmp[:], rq[:]))
            link(ts(amp2[:], sizew[:], 1.0 / N, None, ALU.mult))
            tt(amp2[:], amp2[:], tmp[:], ALU.mult).then_inc(amp2_ready, 1)
            dve.wait_ge(amp_ready, 1)
            link(tt(cst[:], amp[:], mu[:], ALU.mult))
            link(tt(damp[:], amp[:, 0:1], amp[:, 1:2], ALU.subtract))
            link(tt(dcst[:], cst[:, 1:2], cst[:, 0:1], ALU.subtract))
            ts(ncst[:], cst[:, 1:2], -1.0, None, ALU.mult).then_inc(coef_ready, 1)
            for b in range(B):
                u = b % 2
                dve.wait_ge(joined, b + 1)
                dve.wait_ge(mod_spread, b + 1)
                link(tt(upper[u][:], upper[u][:], p_g[u][:], ALU.mult))
                link(tt(upper[u][:], upper[u][:], p_b[u][:], ALU.add))
                tt(xt[:, b], xt[:, b], upper[u][:], ALU.add).then_inc(batch_done, 1)

        @block.tensor
        def _(pe):
            pe.wait_ge(consts_in, 80)
            join_groups_tensor(nc, pe, gnmat[:], gn["mv"][:, :, 0], B, gn, gs)
            for b in range(B):
                pe.wait_ge(xn_ready, b + 1)
                if b >= 2:
                    pe.wait_ge(reduced, b - 1)
                for q in range(4):
                    last = nc.tensor.transpose(p_t[b % 2][:, q].rearrange("p h c -> p (h c)"), xn[:, b, q * P:(q + 1) * P], ident[:])
                last.then_inc(turned, 1)

            def conv(out, src, m0, first, stop):
                for dt in range(3):
                    last = nc.tensor.matmul(out, band[:, m0 + dt], src[:, dt:dt + NT].rearrange("p t b -> p (t b)"),
                                            start=(first and dt == 0), stop=(stop and dt == 2))
                return last

            pe.wait_ge(zeroed, 3)
            pe.wait_ge(pooled_ready, 1)
            conv(p_m[:, 0], pooled[:, 0], 0, True, False)
            conv(p_m[:, 0], pooled[:, 1], 3, False, True).then_inc(map_conv, 1)
            pe.wait_ge(attn_ready, 1)
            conv(p_m[:, 1], attn, 6, True, True)
            conv(p_m[:, 2], attn, 9, True, True).then_inc(mods_conv, 1)
            pe.wait_ge(mask_ready, 1)
            nc.tensor.matmul(p_m[:, 3], ones[:], mask[:].rearrange("p t b -> p (t b)"), start=True, stop=True).then_inc(counted, 1)

            def spread(out, src, b):
                for q in range(4):
                    for h in range(2):
                        last = nc.tensor.matmul(out[h * C:(h + 1) * C, q * P:(q + 1) * P],
                                                src[:, h * 4 + q, b:b + 1].to_broadcast([P, C]), ident[:], start=True, stop=True)
                return last

            for b in range(B):
                if b >= 2:
                    pe.wait_ge(maskc_ready, b - 1)
                spread(p_g[b % 2], mask, b).then_inc(mask_spread, 1)
            pe.wait_ge(totals, 1)
            nc.tensor.matmul(gn["ps"][:, 0:4], bnmat[:], tot[:], start=True, stop=True).then_inc(paired, 1)
            pe.wait_ge(mod_ready, 1)
            pe.wait_ge(maskc_ready, B)
            for b in range(B):
                if b >= 2:
                    pe.wait_ge(batch_done, b - 1)
                spread(p_g[b % 2], mod[:, 0], b)
                spread(p_b[b % 2], mod[:, 1], b).then_inc(mod_spread, 1)



def layer3(nc, xt, d, out):
    A = 4
    with ExitStack() as ctx:
        def sb(name, shape, dt=F32):
            return ctx.enter_context(nc.sbuf_tensor(name + "_3", shape, dt))

        def sem(name):
            return ctx.enter_context(nc.semaphore(name + "_3"))

        inw = sb("inw", [P, 3 * A, HALF]); inb = sb("inb", [P, 3 * A, HALF])
        hidw = sb("hidw", [P, A, A, HALF]); hidb = sb("hidb", [P, A, HALF])
        outw = sb("outw", [P, A, HALF]); outb = sb("outb", [P, HALF])
        ident = sb("ident", [P, P]); before = sb("before", [P, P]); follow = sb("follow", [P, P])
        first = sb("first", [P, 1])
        xh = sb("xh", [P, HALF])
        xres = sb("xres", [P, HALF])
        z = sb("z", [P, 3 * A, HALF])
        expo = xt[:, 0:2 * A].rearrange("p (g i) x -> p g i x", g=2)
        lost = xt[:, 2 * A:4 * A].rearrange("p (g i) x -> p g i x", g=2)
        scale = sb("scale", [P, B]); shift = sb("shift", [P, B])
        gnmat = z[:, 0, 0:P]
        gn = {"st": z[:, 1, 0:6 * B].rearrange("p (b s) -> p b s", b=B), "mv": z[:, 2, 0:2 * B].rearrange("p (b s) -> p b s", b=B),
              "mean": z[:, 3, 0:B], "dev": z[:, 4, 0:B], "var": z[:, 5, 0:B], "sd": z[:, 6, 0:B], "scale": scale, "shift": shift}
        gs = {name: ctx.enter_context(nc.semaphore(f"gn3_{name}")) for name in STAT_SEMS}
        work = sb("work", [P, A * (A + 1), HALF])
        kv = work[:].rearrange("p (i j) x -> p i j x", j=A + 1)
        hid = work[:, 0:A * A].rearrange("p (a j) x -> p a j x", j=A)
        gated = work[:, A * A:]
        y = sb("y", [P, A, HALF + 1])
        p_num = ctx.enter_context(nc.psum_tensor("p_num_3", [P, A + 1, HALF], F32))
        p_out = ctx.enter_context(nc.psum_tensor("p_out_3", [P, HALF], F32))
        p_small = ctx.enter_context(nc.psum_tensor("p_small_3", [P, HALF], F32))
        gn["ps"] = p_small
        resid = nc.dram_tensor("resid", (B, P, HALF), F32, kind="Internal").ap()

        consts_in = sem("consts_in"); own_dve = sem("own_dve"); norm_done = sem("norm_done")
        xh_ready = sem("xh_ready"); scaled = sem("scaled"); biased = sem("biased"); soft = sem("soft")
        scanned = sem("scanned"); carried = sem("carried"); queried = sem("queried"); summed = sem("summed")
        y_ready = sem("y_ready"); shifted = sem("shifted"); y_first = sem("y_first")
        hid_scaled = sem("hid_scaled"); hid_ready = sem("hid_ready"); hid_summed = sem("hid_summed"); tanh_ready = sem("tanh_ready")
        saved = sem("saved"); x_in = sem("x_in"); res_in = sem("res_in"); out_done = sem("out_done")
        own_act = sem("own_act"); expd = sem("expd"); lost_ready = sem("lost_ready"); logd = sem("logd"); relud = sem("relud")
        key_copied = sem("key_copied"); gated_ready = sem("gated_ready"); out_summed = sem("out_summed"); added = sem("added")
        block = ctx.enter_context(nc.Block())

        def known(b):
            return isinstance(b, int)

        def over_batches(eng, prep, main):
            prep(0)
            main(0, prep)
            with eng.Fori(1, B - 1) as b:
                main(b, prep)
            main(B - 1, None)

        @block.sync
        def _(sp):
            sp.dma_start(gnmat, d["gnmat"][:]).then_inc(consts_in, 16)
            for b in range(B):
                sp.dma_start(resid[b], xt[:, b]).then_inc(saved, 16)
            for name, tile in (("ident", ident), ("before", before), ("follow", follow), ("first", first),
                               ("inw", inw), ("inb", inb), ("hidw", hidw), ("hidb", hidb), ("outw", outw), ("outb", outb)):
                sp.dma_start(tile[:], d[name][:]).then_inc(consts_in, 16)
            sp.wait_ge(saved, 16 * B)

            def load(b):
                sp.dma_start(xh[:], resid[bass.ds(b, 1)].rearrange("o p x -> (o p) x")).then_inc(x_in, 16)

            def main(b, nxt):
                if nxt:
                    if not (known(b) and b == 0):
                        sp.wait_ge(y_ready, b)
                    else:
                        sp.wait_ge(scaled, 1)
                    load(b + 1)
                if not (known(b) and b == 0):
                    sp.wait_ge(out_done, b * 16)
                sp.dma_start(xres[:], resid[bass.ds(b, 1)].rearrange("o p x -> (o p) x")).then_inc(res_in, 16)
                sp.wait_ge(added, b + 1)
                sp.dma_start(out[:, bass.ds(b, 1)].rearrange("p o x -> p (o x)"), xres[:]).then_inc(out_done, 16)

            load(0)
            over_batches(sp, lambda b: None, main)
            sp.wait_ge(out_done, 16 * B)

        @block.gpsimd
        def _(pool):
            tt = nc.gpsimd.tensor_tensor

            def prep(b):
                pool.wait_ge(scaled, b + 1)
                for n in (1, 0, 2):
                    part = z[:, n * A:(n + 1) * A]
                    tt(part, part, inb[:, n * A:(n + 1) * A], ALU.add).then_inc(biased, 1)
                for g in range(2):
                    pool.wait_ge(expd, b * 2 + (g + 1))
                    tt(lost[:, g], expo[:, g], lost[:, g], ALU.subtract).then_inc(lost_ready, 1)
                for g in range(2):
                    pool.wait_ge(relud, b * 2 + (g + 1))
                    tt(expo[:, g], expo[:, g], lost[:, g], ALU.add).then_inc(soft, 1)

            def main(b, nxt):
                if nxt:
                    nxt(b + 1)

            over_batches(pool, prep, main)

        @block.scalar
        def _(act):
            join_groups_scalar(nc, act, B, gn, gs)
            act.wait_ge(norm_done, 1)
            act.wait_ge(saved, 16 * B)

            def normalise(b):
                act.wait_ge(x_in, b * 16 + 16)
                nc.scalar.activation(xh[:], xh[:], ACT.Identity,
                                     bias=shift[:, bass.ds(b, 1)], scale=scale[:, bass.ds(b, 1)]).then_inc(xh_ready, 1)

            def prep(b):
                step = Chain(act, own_act, b * 6)
                if not (known(b) and b == 0):
                    act.wait_ge(queried, b * A)
                for g, n in ((0, 1), (1, 0)):
                    act.wait_ge(biased, b * 3 + (g + 1))
                    step(nc.scalar.activation(expo[:, g], z[:, n * A:(n + 1) * A], ACT.Abs))
                    step(nc.scalar.activation(expo[:, g], expo[:, g], ACT.Exp, scale=-1.0))
                    step(nc.scalar.activation(lost[:, g], expo[:, g], ACT.Copy, bias=1.0))
                    nc.scalar.activation(lost[:, g], lost[:, g], ACT.Copy, bias=-1.0).then_inc(expd, 1)
                for g in range(2):
                    act.wait_ge(lost_ready, b * 2 + (g + 1))
                    nc.scalar.activation(expo[:, g], expo[:, g], ACT.Ln, bias=1.0).then_inc(logd, 1)

            def main(b, nxt):
                act.wait_ge(soft, b * 2 + 1)
                if not (known(b) and b == 0):
                    act.wait_ge(out_summed, b)
                nc.scalar.activation(kv[:, :, A], expo[:, 0], ACT.Copy).then_inc(key_copied, 1)
                if nxt:
                    normalise(b + 1)
                act.wait_ge(shifted, b + 1)
                nc.scalar.activation(y[:, :, 0], p_small[:, 32:32 + A], ACT.Identity, bias=first[:]).then_inc(y_first, 1)
                for a in range(A):
                    act.wait_ge(hid_summed, b * A + (a + 1))
                    nc.scalar.activation(gated[:, a], p_num[:, a], ACT.Tanh).then_inc(tanh_ready, 1)
                if nxt:
                    nxt(b + 1)

            act.wait_ge(consts_in, 176)
            normalise(0)
            over_batches(act, prep, main)

        @block.vector
        def _(dve):
            tt, ts, stt = nc.vector.tensor_tensor, nc.vector.tensor_scalar, nc.vector.scalar_tensor_tensor
            link = Chain(dve, own_dve)
            group_norm_vector(nc, dve, link, xt, gn, gs)
            dve.nop().then_inc(norm_done, 1)
            dve.wait_ge(consts_in, 176)
            start = link.n

            def prep(b):
                dve.wait_ge(xh_ready, b + 1)
                tt(z[:], inw[:], xh[:].rearrange("p (o x) -> p o x", o=1).to_broadcast([P, 3 * A, HALF]), ALU.mult).then_inc(scaled, 1)

            def main(b, nxt):
                dve.wait_ge(biased, b * 3 + 3)
                dve.wait_ge(soft, b * 2 + 1)
                tt(kv[:, :, 0:A], expo[:, 0].rearrange("p i (o x) -> p i o x", o=1).to_broadcast([P, A, A, HALF]),
                   z[:, 2 * A:].rearrange("p (o j) x -> p o j x", o=1).to_broadcast([P, A, A, HALF]), ALU.mult).then_inc(scanned, 1)
                dve.wait_ge(scanned, b * 2 + 1)
                dve.wait_ge(key_copied, b + 1)
                for n in range(A * (A + 1)):
                    last = nc.vector.tensor_tensor_scan(out=work[:, n], data0=work[:, n], data1=work[:, n], initial=0.0,
                                                        op0=ALU.add, op1=ALU.bypass)
                last.then_inc(scanned, 1)
                dve.wait_ge(scanned, b * 2 + 2)
                dve.wait_ge(soft, b * 2 + 2)
                dve.wait_ge(carried, b + 1)
                for i in range(A):
                    for j in range(A + 1):
                        n = i * (A + 1) + j
                        last = stt(out=work[:, n], in0=work[:, n], scalar=p_small[:, n:n + 1], in1=expo[:, 1, i], op0=ALU.add, op1=ALU.mult)
                    last.then_inc(queried, 1)
                dve.wait_ge(queried, b * A + A)
                dve.wait_ge(summed, b + 1)
                if nxt:
                    nxt(b + 1)
                    dve.wait_ge(scaled, b + 2)
                nc.vector.reciprocal(xh[:], p_num[:, A]).then_inc(own_dve, 1)
                dve.wait_ge(own_dve, b + (start + 1))
                tt(y[:, :, 1:], p_num[:, 0:A], xh[:].rearrange("p (o x) -> p o x", o=1).to_broadcast([P, A, HALF]),
                   ALU.mult).then_inc(y_ready, 1)
                dve.wait_ge(y_ready, b + 1)
                dve.wait_ge(y_first, b + 1)
                for a in range(A):
                    tt(hid[:, a], hidw[:, a], y[:, :, 0:HALF], ALU.mult).then_inc(hid_scaled, 1)
                    dve.wait_ge(hid_scaled, b * A + (a + 1))
                    tt(hid[:, a, 0:2], hid[:, a, 0:2], hid[:, a, 2:4], ALU.add).then_inc(hid_ready, 1)
                if nxt:
                    relu(b + 1)
                dve.wait_ge(tanh_ready, b * A + A)
                tt(gated, gated, outw[:], ALU.mult).then_inc(gated_ready, 1)
                dve.wait_ge(out_summed, b + 1)
                dve.wait_ge(res_in, b * 16 + 16)
                tt(xres[:], xres[:], p_out[:], ALU.add).then_inc(added, 1)

            def relu(b):
                for g, n in ((0, 1), (1, 0)):
                    dve.wait_ge(logd, b * 2 + (g + 1))
                    stt(out=expo[:, g], in0=z[:, n * A:(n + 1) * A], scalar=0.0, in1=expo[:, g],
                        op0=ALU.max, op1=ALU.add).then_inc(relud, 1)

            prep(0)
            relu(0)
            main(0, prep)
            with dve.Fori(1, B - 1) as b:
                main(b, prep)
            main(B - 1, None)

        @block.tensor
        def _(pe):
            pe.wait_ge(consts_in, 176)
            join_groups_tensor(nc, pe, gnmat[:], gn["mv"][:, :, 0], B, gn, gs)

            def main(b, nxt):
                pe.wait_ge(scanned, b * 2 + 2)
                nc.tensor.matmul(p_small[:, 0:A * (A + 1)], before[:], work[:, :, HALF - 1], start=True, stop=True).then_inc(carried, 1)
                for i in range(A):
                    pe.wait_ge(queried, b * A + (i + 1))
                    for j in range(A + 1):
                        last = nc.tensor.matmul(p_num[:, j], ident[:], kv[:, i, j], start=(i == 0), stop=(i == A - 1))
                last.then_inc(summed, 1)
                pe.wait_ge(y_ready, b + 1)
                nc.tensor.matmul(p_small[:, 32:32 + A], follow[:], y[:, :, HALF], start=True, stop=True).then_inc(shifted, 1)
                for a in range(A):
                    nc.tensor.matmul(p_num[:, a], ident[:], hidb[:, a], start=True, stop=False)
                    pe.wait_ge(hid_ready, b * A + (a + 1))
                    nc.tensor.matmul(p_num[:, a], ident[:], hid[:, a, 0], start=False, stop=False)
                    nc.tensor.matmul(p_num[:, a], ident[:], hid[:, a, 1], start=False, stop=True).then_inc(hid_summed, 1)
                if not (known(b) and b == 0):
                    pe.wait_ge(added, b)
                nc.tensor.matmul(p_out[:], ident[:], outb[:], start=True, stop=False)
                pe.wait_ge(gated_ready, b + 1)
                for a in range(A):
                    last = nc.tensor.matmul(p_out[:], ident[:], gated[:, a], start=False, stop=(a == A - 1))
                last.then_inc(out_summed, 1)

            over_batches(pe, lambda b: None, main)


def build_program(nc, d, out):
    with nc.sbuf_tensor("xt", [P, B, HALF], F32) as xt:
        layer0(nc, xt, d)
        layer1(nc, xt, d)
        layer2(nc, xt, d)
        layer3(nc, xt, d, out)


def layouts(inp):
    import numpy as np
    f = lambda n: np.asarray(inp[n])
    a = {}
    x = f("x").reshape(B, C, 2, HALF)
    a["x"] = x.transpose(2, 1, 0, 3).reshape(P, B, HALF)
    w = f("L0_conv_weight").reshape(C, 2, RH, 4, 8, C, 3, 3)
    w0 = np.zeros((RH, 4, 2, C, 8, 9, C), np.float32)
    t = w.transpose(1, 2, 3, 5, 4, 6, 7, 0)
    for h in range(2):
        for m in range(3):
            w0[:, :, 0, :, :, 4 * h + m] = t[h, :, :, :, :, m, 0]
            w0[:, :, 1, :, :, 4 * h + m] = t[h, :, :, :, :, m, 1]
        w0[:, :, 0, :, :, 4 * h + 3] = t[h, :, :, :, :, 0, 2]
        w0[:, :, 1, :, :, 4 * h + 3] = t[h, :, :, :, :, 1, 2]
        w0[:, :, h, :, :, 8] = t[h, :, :, :, :, 2, 2]
    a["w0"] = w0.reshape(RH, 4, P, 8, 9, C)
    a["bias0"] = f("L0_conv_bias").reshape(C, 2, HALF).transpose(1, 0, 2).reshape(P, HALF)
    a["affine0"] = np.stack([np.tile(f("L0_conv_gamma"), 2), np.tile(f("L0_conv_beta"), 2)], axis=1)
    p = np.arange(P)
    a["gnmat"] = (((p[:, None] % C) // 2 == (p[None, :] % C) // 2) / 4.0).astype(np.float32)
    a["bnmat"] = ((p[:, None] % C == p[None, :] % C) / 2.0).astype(np.float32)
    w = np.concatenate([f("L1_conv_offset_w"), f("L1_conv_mod_w")], axis=0)
    w1 = np.zeros((2, C, 5, 27), np.float32)
    for m in range(3):
        w1[0, :, m] = w[:, :, m, 0].T
        w1[1, :, m] = w[:, :, m, 1].T
    w1[0, :, 3], w1[1, :, 3], w1[0, :, 4] = w[:, :, 0, 2].T, w[:, :, 1, 2].T, w[:, :, 2, 2].T
    a["wconv"] = w1.reshape(P, 5, 27)
    r = f("L1_conv_reg_w").reshape(C, C, TAPS)
    a["wreg"] = np.tile(r.transpose(1, 2, 0), (2, 1, 1))
    a["ident"] = np.eye(P, dtype=np.float32)
    a["obias"] = np.tile(np.concatenate([f("L1_conv_offset_b"), f("L1_conv_mod_b")]), (P, 1))
    t, k = np.arange(NT), np.arange(TAPS)
    base = np.zeros((P, NT, TAPS, 2), np.float32)
    base[..., 0] = (4 * t[None, :] + p[:, None] // W)[:, :, None] + k // 3 - 1
    base[..., 1] = (p % W)[:, None, None] + k % 3 - 1
    a["base"] = base.reshape(P, NT, 18)
    band = np.zeros((P, 4, 3, P), np.float32)
    kern = [f("L2_conv_w1")[0, 0], f("L2_conv_w1")[0, 1], f("L2_conv_wg")[0, 0], f("L2_conv_wb")[0, 0]]
    for n, w in enumerate(kern):
        for dt in range(3):
            for r in range(4):
                for q in range(4):
                    dy = 4 * (dt - 1) + r - q + REACH
                    if 0 <= dy < MAP_K:
                        for x in range(W):
                            for o in range(max(0, x - REACH), min(W, x + REACH + 1)):
                                band[r * W + x, n, dt, q * W + o] = w[dy, x - o + REACH]
    a["band"] = band.reshape(P, 12, P)
    a["mbias"] = np.tile(np.concatenate([f("L2_conv_bg"), f("L2_conv_bb")]), (P, 1))
    def by_position(v, lead):
        v = v.reshape(lead + (C, 2, HALF, -1))
        n = len(lead)
        v = v.transpose((n + 1, n) + tuple(range(n)) + (n + 3, n + 2))
        return v.reshape((P,) + lead + (-1, HALF))
    a["inw"] = by_position(f("L3_conv_in_proj_weight"), (3,)).reshape(P, 12, HALF)
    a["inb"] = by_position(f("L3_conv_in_proj_bias"), (3,)).reshape(P, 12, HALF)
    a["hidw"] = by_position(f("L3_conv_hid_proj_weight"), (4,))
    a["hidb"] = by_position(f("L3_conv_hid_proj_bias"), (4,)).reshape(P, 4, HALF)
    a["outw"] = by_position(f("L3_conv_out_proj_weight"), (4,)).reshape(P, 4, HALF)
    a["outb"] = by_position(f("L3_conv_out_proj_bias"), ()).reshape(P, HALF)
    segment = 2 * (p % C) + p // C
    a["before"] = (segment[:, None] < segment[None, :]).astype(np.float32)
    a["follow"] = (segment[:, None] + 1 == segment[None, :]).astype(np.float32)
    a["first"] = (segment == 0).astype(np.float32).reshape(P, 1)
    return a


def kernel(**inputs):
    import numpy as np
    import concourse.bacc as bacc
    from concourse.bass_utils import run_bass_kernel_spmd

    arrays = {"in_" + n: np.ascontiguousarray(v) for n, v in layouts(inputs).items()}
    nc = bacc.Bacc("TRN2", target_bir_lowering=False, num_devices=1)
    d = {n[3:]: nc.dram_tensor(n, a.shape, mybir.dt.from_np(a.dtype), kind="ExternalInput").ap() for n, a in arrays.items()}
    y = nc.dram_tensor("y", (P, B, HALF), F32, kind="ExternalOutput").ap()
    build_program(nc, d, y)
    got = run_bass_kernel_spmd(nc, [arrays], core_ids=[0]).results[0]["y"]
    return got.reshape(2, C, B, RH, W).transpose(2, 1, 0, 3, 4).reshape(B, C, H, W)
```

```python
import concourse.bass as bass
from concourse import mybir
from contextlib import ExitStack

F32 = mybir.dt.float32
I32 = mybir.dt.int32
U32 = mybir.dt.uint32
ALU = mybir.AluOpType
ACT = mybir.ActivationFunctionType
AX = mybir.AxisListType

B, C, H, W = 16, 64, 32, 32
P = 128
HALF = H * W // 2
RH = H // 2
WP = W + 2
TAPS = 9
GN_EPS = 1e-5


class Chain:

    def __init__(self, eng, sem, base=0):
        self.eng, self.sem, self.n = eng, sem, base

    def __call__(self, ins):
        self.n = self.n + 1
        ins.then_inc(self.sem, 1)
        self.eng.wait_ge(self.sem, self.n)


def group_norm_vector(nc, dve, link, x, t, s):
    for b in range(B):
        last = nc.vector.bn_stats(t["st"][:, b, :], x[:, b, :])
    link(last)
    for b in range(B):
        last = nc.vector.bn_aggr(t["mv"][:, b, :], t["st"][:, b, :])
    last.then_inc(s["row_stats"], 1)
    join_groups_vector(nc, dve, link, t["mv"][:, :, 0], t["mv"][:, :, 1], B, t, s)
    link(nc.vector.scalar_tensor_tensor(out=t["shift"][:, 0:B], in0=t["mean"][:, 0:B], scalar=-1.0,
                                        in1=t["scale"][:, 0:B], op0=ALU.mult, op1=ALU.mult))


def join_groups_vector(nc, dve, link, mean, var, n, t, s):
    dve.wait_ge(s["joined_mean"], 1)
    link(nc.vector.tensor_copy(t["mean"][:, 0:n], t["ps"][:, 0:n]))
    link(nc.vector.tensor_tensor(t["dev"][:, 0:n], mean, t["mean"][:, 0:n], ALU.subtract))
    link(nc.vector.tensor_tensor(t["dev"][:, 0:n], t["dev"][:, 0:n], t["dev"][:, 0:n], ALU.mult))
    nc.vector.tensor_tensor(t["dev"][:, 0:n], t["dev"][:, 0:n], var, ALU.add).then_inc(s["spread"], 1)
    dve.wait_ge(s["joined_var"], 1)
    nc.vector.tensor_scalar(t["var"][:, 0:n], t["ps"][:, B:B + n], GN_EPS, None, ALU.add).then_inc(s["var_eps"], 1)
    dve.wait_ge(s["deviation"], 1)
    link(nc.vector.reciprocal(t["scale"][:, 0:n], t["sd"][:, 0:n]))


def join_groups_tensor(nc, pe, matrix, mean, n, t, s):
    pe.wait_ge(s["row_stats"], 1)
    nc.tensor.matmul(t["ps"][:, 0:n], matrix, mean, start=True, stop=True).then_inc(s["joined_mean"], 1)
    pe.wait_ge(s["spread"], 1)
    nc.tensor.matmul(t["ps"][:, B:B + n], matrix, t["dev"][:, 0:n], start=True, stop=True).then_inc(s["joined_var"], 1)


def join_groups_scalar(nc, act, n, t, s):
    act.wait_ge(s["var_eps"], 1)
    nc.scalar.activation(t["sd"][:, 0:n], t["var"][:, 0:n], ACT.Sqrt).then_inc(s["deviation"], 1)


STAT_SEMS = ["row_stats", "joined_mean", "spread", "joined_var", "var_eps", "deviation"]


def stat_buffers(nc, ctx, tag):
    def sb(name, cols):
        return ctx.enter_context(nc.sbuf_tensor(f"{tag}_{name}", cols, F32))

    t = {"st": sb("st", [P, B, 6]), "mv": sb("mv", [P, B, 2])}
    for name in ("mean", "dev", "var", "sd", "scale", "shift"):
        t[name] = sb(name, [P, B])
    t["ps"] = ctx.enter_context(nc.psum_tensor(f"{tag}_ps", [P, 2 * B], F32))
    s = {name: ctx.enter_context(nc.semaphore(f"{tag}_{name}")) for name in STAT_SEMS}
    return t, s


def layer0(nc, xt, d):
    NQ, PX = 4, 8
    RING = 4
    G, QUAD = 4, 32
    with ExitStack() as ctx:
        def sb(name, shape):
            return ctx.enter_context(nc.sbuf_tensor(name, shape, F32))

        def sem(name):
            return ctx.enter_context(nc.semaphore(name))

        gn, gs = stat_buffers(nc, ctx, "gn0")
        bn, bs = stat_buffers(nc, ctx, "bn0")
        xh = sb("xh", [P, RH + 2, WP, B])
        win_a = sb("win_a", [P, 2, 2, 3, WP, B])
        win_b = sb("win_b", [P, 2, 2, W, B])
        ring = sb("ring", [P, RING, PX, TAPS, C])
        bias = sb("bias0", [P, HALF])
        gnmat = sb("gnmat0", [P, P])
        bnmat = sb("bnmat0", [P, P])
        affine = sb("affine0", [P, 2])
        fold = sb("fold0", [P, 2])
        sums = sb("sums0", [P, 2, W // G, P])
        acc = [ctx.enter_context(nc.psum_tensor(f"acc0_{i}", [P, 2, W // G, C], F32)) for i in range(2)]
        turn = ctx.enter_context(nc.psum_tensor("turn0", [P, W, QUAD], F32))
        ident = sb("ident0", [P, P])

        x_in = sem("x_in"); consts_in = sem("consts_in")
        w_in = [sem(f"w_in{i}") for i in range(RING)]
        w_used = sem("w_used")
        own_dve = sem("own_dve"); border_done = sem("border_done")
        norm_done = sem("norm_done"); xh_ready = sem("xh_ready")
        win_a_ready = sem("win_a_ready"); win_b_ready = sem("win_b_ready")
        row_stored = sem("row_stored"); acc_clear = sem("acc_clear"); copied = sem("copied"); turned = sem("turned0")
        bn_ready = sem("bn_ready"); slot_free = sem("slot_free"); relu_done = sem("relu_done"); xr_in = sem("xr_in")
        block = ctx.enter_context(nc.Block())
        xr = ring[:, 0:2].rearrange("p s a t c -> p (s a t c)")[:, 0:B * HALF].rearrange("p (b x) -> p b x", b=B)

        @block.sync
        def _(sp):
            sp.dma_start(xt[:], d["x"][:]).then_inc(x_in, 16)
            for name, tile in (("gnmat", gnmat), ("bnmat", bnmat), ("bias0", bias), ("affine0", affine), ("ident", ident)):
                sp.dma_start(tile[:], d[name][:]).then_inc(consts_in, 16)
            for q in range(NQ):
                sp.dma_start(ring[:, q], d["w0"][0, q]).then_inc(w_in[q], 16)
            with sp.Fori(1, RH) as r:
                for q in range(NQ):
                    sp.wait_ge(w_used, r * NQ + (q - NQ + 1))
                    sp.dma_start(ring[:, q], d["w0"][r, q]).then_inc(w_in[q], 16)
            sp.wait_ge(w_used, RH * NQ)
            sp.dma_start(xr, d["x"][:]).then_inc(xr_in, 16)

        @block.gpsimd
        def _(pool):
            nc.gpsimd.memset(xh[:], 0.0).then_inc(border_done, 1)

        @block.scalar
        def _(act):
            join_groups_scalar(nc, act, B, gn, gs)
            act.wait_ge(norm_done, 1)
            act.wait_ge(border_done, 1)
            xv = xh[:].rearrange("p r w b -> p b r w")
            for b in range(B):
                last = nc.scalar.activation(xv[:, b, 1:RH + 1, 1:W + 1],
                                            xt[:, b, :].rearrange("p (r w) -> p r w", w=W), ACT.Identity,
                                            bias=gn["shift"][:, b:b + 1], scale=gn["scale"][:, b:b + 1])
            last.then_inc(xh_ready, 1)


            def windows(r, u, first):
                if first:
                    act.wait_ge(xh_ready, 3)
                else:
                    act.wait_ge(w_used, NQ * r - NQ)
                    act.sem_inc(slot_free, 1)
                for h in range(2):
                    src = xh[h * C:(h + 1) * C]
                    nc.scalar.activation(win_b[0:C, u, h], src[:, bass.ds(r, 1), 2:WP].rearrange("p r w b -> p (r w) b"),
                                         ACT.Copy).then_inc(win_b_ready, 1)
                    nc.scalar.activation(win_b[C:P, u, h], src[:, bass.ds(r + 1, 1), 2:WP].rearrange("p r w b -> p (r w) b"),
                                         ACT.Copy).then_inc(win_b_ready, 1)

            def copy(r, u, first):
                act.wait_ge(w_used, NQ * r + NQ)
                if not first:
                    act.wait_ge(turned, r - 1)
                for n in range(2):
                    nc.scalar.activation(sums[:, u, :, n * C:(n + 1) * C], acc[u][:, n], ACT.Copy).then_inc(copied, 1)

            windows(0, 0, True)
            windows(1, 1, True)
            copy(0, 0, True)
            windows(2, 0, False)
            copy(1, 1, True)
            windows(3, 1, False)
            with act.Fori(1, RH // 2 - 1) as rr:
                copy(rr * 2, 0, False)
                windows(rr * 2 + 2, 0, False)
                copy(rr * 2 + 1, 1, False)
                windows(rr * 2 + 3, 1, False)
            copy(RH - 2, 0, False)
            copy(RH - 1, 1, False)
            join_groups_scalar(nc, act, 1, bn, bs)
            act.wait_ge(bn_ready, 1)
            for b in range(B):
                nc.scalar.activation(xt[:, b, :], xt[:, b, :], ACT.Relu, bias=fold[:, 1:2],
                                     scale=fold[:, 0:1]).then_inc(relu_done, 1)

        @block.vector
        def _(dve):
            link = Chain(dve, own_dve)
            for u in range(2):
                nc.vector.memset(acc[u][:], 0.0).then_inc(acc_clear, 1)
            dve.wait_ge(x_in, 16)
            group_norm_vector(nc, dve, link, xt, gn, gs)
            nc.vector.tensor_copy(gn["st"][:, 0, 0:1], gn["st"][:, 0, 0:1]).then_inc(norm_done, 1)
            dve.wait_ge(xh_ready, 1)
            nc.vector.tensor_copy(xh[0:C, RH + 1], xh[C:P, 1]).then_inc(xh_ready, 1)
            nc.vector.tensor_copy(xh[C:P, 0], xh[0:C, RH]).then_inc(xh_ready, 1)
            dve.wait_ge(xh_ready, 3)

            def windows(r, u, first):
                if not first:
                    dve.wait_ge(w_used, NQ * r - NQ)
                for h in range(2):
                    src = xh[h * C:(h + 1) * C]
                    nc.vector.tensor_copy(win_a[0:C, u, h], src[:, bass.ds(r, 3)]).then_inc(win_a_ready, 1)
                    nc.vector.tensor_copy(win_a[C:P, u, h, :, 0:WP - 1], src[:, bass.ds(r, 3), 1:WP]).then_inc(win_a_ready, 1)

            def store(r, u):
                dve.wait_ge(turned, r + 1)
                bcol = bias[:, bass.ds(r * W, W)].rearrange("p (o w) -> p o w", o=1).to_broadcast([P, B, W])
                nc.vector.tensor_tensor(xt[:, :, bass.ds(r * W, W)], turn[:, :, 0:B].rearrange("p w b -> p b w"),
                                        bcol, ALU.add).then_inc(row_stored, 1)

            dve.wait_ge(consts_in, 80)
            for u in range(2):
                windows(u, u, True)
            with dve.Fori(1, RH // 2) as rr:
                for u in range(2):
                    windows(rr * 2 + u, u, False)
                    store(rr * 2 + (u - 2), u)
            for u in range(2):
                store(RH - 2 + u, u)
            dve.wait_ge(row_stored, RH)
            for b in range(B):
                last = nc.vector.bn_stats(bn["st"][:, b, :], xt[:, b, :])
            link(last)
            nc.vector.bn_aggr(bn["mv"][:, 0, :], bn["st"][:].rearrange("p b s -> p (b s)")).then_inc(bs["row_stats"], 1)
            join_groups_vector(nc, dve, link, bn["mv"][:, 0, 0:1], bn["mv"][:, 0, 1:2], 1, bn, bs)
            link(nc.vector.tensor_tensor(fold[:, 0:1], bn["scale"][:, 0:1], affine[:, 0:1], ALU.mult))
            link(nc.vector.tensor_tensor(fold[:, 1:2], bn["mean"][:, 0:1], fold[:, 0:1], ALU.mult))
            nc.vector.tensor_tensor(fold[:, 1:2], affine[:, 1:2], fold[:, 1:2], ALU.subtract).then_inc(bn_ready, 1)
            dve.wait_ge(xr_in, 16)
            for b in range(B):
                dve.wait_ge(relu_done, b + 1)
                nc.vector.tensor_tensor(xt[:, b, :], xt[:, b, :], xr[:, b, :], ALU.add)

        @block.tensor
        def _(pe):
            pe.wait_ge(consts_in, 80)
            join_groups_tensor(nc, pe, gnmat[:], gn["mv"][:, :, 0], B, gn, gs)

            def turn_row(r, u, first):
                pe.wait_ge(copied, 2 * r + 2)
                if not first:
                    pe.wait_ge(row_stored, r)
                for n in range(W // G):
                    last = nc.tensor.transpose(turn[:, n * G:(n + 1) * G].rearrange("p g b -> p (g b)"), sums[:, u, n], ident[:])
                last.then_inc(turned, 1)

            def row(r, u, known):
                pe.wait_ge(win_b_ready, 4 * r + 4)
                if known is None or known >= 2:
                    pe.wait_ge(copied, 2 * r - 2)
                pe.wait_ge(win_a_ready, 4 * r + 4)
                for q in range(NQ):
                    pe.wait_ge(w_in[q], 16 * r + 16)
                    wt = ring[:, q]
                    for n in range(PX // G):
                        for m in range(4):
                            for h in range(2):
                                for g in range(G):
                                    j = q * PX + n * G + g
                                    mov = win_a[:, u, h, m, j] if m < 3 else win_b[:, u, h, j]
                                    nc.tensor.matmul(acc[u][g * QUAD:g * QUAD + B, h, j // G], mov, wt[:, n * G + g, 4 * h + m],
                                                     start=(j < G and m == 0), stop=False)
                    for n in range(PX // G):
                        for h in range(2):
                            for g in range(G):
                                j = q * PX + n * G + g
                                last = nc.tensor.matmul(acc[u][g * QUAD:g * QUAD + B, h, j // G],
                                                        win_a[h * C:(h + 1) * C, u, h, 2, j + 2 - h],
                                                        wt[h * C:(h + 1) * C, n * G + g, 8],
                                                        start=False, stop=(j >= W - G))
                    last.then_inc(w_used, 1)
                    if q == 0 and known != 0:
                        turn_row(r - 1, 1 - u, known == 1)

            pe.wait_ge(acc_clear, 2)
            row(0, 0, 0)
            row(1, 1, 1)
            with pe.Fori(1, RH // 2) as rr:
                for u in range(2):
                    row(rr * 2 + u, u, None)
            turn_row(RH - 1, 1, False)
            pe.wait_ge(w_used, RH * NQ)
            join_groups_tensor(nc, pe, bnmat[:], bn["mv"][:, 0, 0:1], 1, bn, bs)



ENTRY = 4 * C
NT = H * W // P


def layer1(nc, xt, d):
    SLOTS = 4
    tables = [nc.dram_tensor(f"table{u}", (WP, WP, 4, C), F32, kind="Internal").ap() for u in range(2)]
    entries = [t.rearrange("y x n c -> (y x) (n c)") for t in tables]
    with ExitStack() as ctx:
        def sb(name, shape, dt=F32):
            return ctx.enter_context(nc.sbuf_tensor(name + "_1", shape, dt))

        def pb(name, shape):
            return ctx.enter_context(nc.psum_tensor(name + "_1", shape, F32))

        def sem(name):
            return ctx.enter_context(nc.semaphore(name + "_1"))

        gn, gs = stat_buffers(nc, ctx, "gn1")
        xn = sb("xn", [P, B, HALF])
        zero = sb("zero", [WP, ENTRY])
        pad01 = [sb(f"pad01_{u}", [P, WP, W]) for u in range(2)]
        pad22 = [sb(f"pad22_{u}", [P, WP, W]) for u in range(2)]
        pix = [sb(f"pix{u}", [P, NT, C]) for u in range(2)]
        gath = sb("gath", [P, SLOTS, TAPS, 4, C])
        cols = [sb(f"cols{u}", [P, TAPS, P]) for u in range(2)]
        wconv = sb("wconv", [P, 5, 27]); wreg = sb("wreg", [P, TAPS, C])
        ident = sb("ident", [P, P]); gnmat = sb("gnmat", [P, P])
        base = sb("base", [P, NT, 18]); obias = sb("obias", [P, 27])
        off = sb("off", [P, NT, 27]); pos = sb("pos", [P, NT, 18]); posi = sb("posi", [P, NT, 18], I32)
        low = sb("low", [P, NT, 18]); over = sb("over", [P, NT, 18])
        frac = sb("frac", [P, NT, 18]); rest = sb("rest", [P, NT, 18])
        gate = sb("gate", [P, NT, TAPS]); rowg = sb("rowg", [P, 2, NT, TAPS]); flat = sb("flat", [P, NT, TAPS])
        idx = [sb(f"idx{u}", [P, NT, TAPS], I32) for u in range(2)]
        wts = [sb(f"wts{u}", [P, NT, TAPS, 4]) for u in range(2)]
        p_off = pb("p_off", [P, 2, 256])
        p_pix = pb("p_pix", [P, NT, C])
        p_col = [pb(f"p_col{g}", [P, 3, P]) for g in range(3)]
        p_y = [pb(f"p_y{u}", [P, HALF]) for u in range(2)]

        consts_in = sem("consts_in"); own_dve = sem("own_dve"); norm_done = sem("norm_done"); xn_ready = sem("xn_ready")
        zero_ready = sem("zero_ready"); border_out = sem("border_out"); slot_free = sem("slot_free"); own_pool = sem("own_pool")
        pad_clear = sem("pad_clear"); pad_ready = sem("pad_ready"); conv_done = sem("conv_done")
        turned = sem("turned"); pix_ready = sem("pix_ready"); table_out = [sem(f"table_out{u}") for u in range(2)]
        off_ready = sem("off_ready"); gate_ready = sem("gate_ready"); coords_ready = sem("coords_ready")
        gath_in = [sem(f"gath_in{s}") for s in range(SLOTS)]
        weighted = sem("weighted"); turned_taps = sem("turned_taps"); cols_ready = sem("cols_ready")
        tile_done = sem("tile_done"); y_added = sem("y_added")
        block = ctx.enter_context(nc.Block())
        NCONST = 7

        def over_batches(eng, prep, main):
            prep(0, 0)
            prep(1, 1)
            main(0, 0)
            with eng.Fori(1, B // 2) as rr:
                prep(rr * 2, 0)
                main(rr * 2 - 1, 1)
                prep(rr * 2 + 1, 1)
                main(rr * 2, 0)
            main(B - 1, 1)

        def known(b):
            return isinstance(b, int)

        @block.sync
        def _(sp):
            for name, tile in (("wconv", wconv), ("wreg", wreg), ("ident", ident), ("gnmat", gnmat), ("base", base),
                               ("obias", obias)):
                sp.dma_start(tile[:], d[name][:]).then_inc(consts_in, 16)
            sp.wait_ge(zero_ready, 1)
            for table in tables:
                for e in (0, H, H + 1):
                    sp.dma_start(table[e].rearrange("x n c -> x (n c)"), zero[:]).then_inc(border_out, 16)
            sp.wait_ge(border_out, 96)
            for table in tables:
                for e in (0, H, H + 1):
                    sp.dma_start(table[:, e].rearrange("y n c -> y (n c)"), zero[:]).then_inc(border_out, 16)
            sp.wait_ge(border_out, 192)

            def prep(b, u):
                sp.wait_ge(pix_ready, b + 1)
                if not known(b):
                    sp.wait_ge(weighted, (b - 1) * NT * 2)
                for n in range(4):
                    y0, x0 = 1 - n // 2, 1 - n % 2
                    for r in range(4):
                        dst = tables[u][y0:y0 + H, x0:x0 + W, n, :].rearrange("(t r) x c -> r x t c", r=4)[r]
                        sp.dma_start(dst, pix[u][r * W:(r + 1) * W]).then_inc(table_out[u], 16)

            over_batches(sp, prep, lambda b, u: None)
            for u in range(2):
                sp.wait_ge(table_out[u], 256 * (B // 2))

        @block.gpsimd
        def _(pool):
            nc.gpsimd.memset(zero[:], 0.0).then_inc(zero_ready, 1)
            for tile in (*pad01, *pad22):
                nc.gpsimd.memset(tile[:], 0.0).then_inc(pad_clear, 1)

            pool.wait_ge(border_out, 192)

            def main(b, u):
                pool.wait_ge(coords_ready, b + 1)
                if known(b):
                    pool.wait_ge(table_out[u], 256 * (b // 2 + 1))
                elif u == 0:
                    pool.wait_ge(table_out[u], b * 128 + 256)
                else:
                    pool.wait_ge(table_out[u], (b + 1) * 128)
                for t in range(NT):
                    if not (known(b) and b == 0 and t < SLOTS):
                        pool.wait_ge(turned_taps, (b * NT + (t + 1 - SLOTS)) * 3)
                        pool.sem_inc(slot_free, 1)
                    for k in range(TAPS):
                        nc.gpsimd.indirect_dma_start(
                            out=gath[:, t % SLOTS, k].rearrange("p n c -> p (n c)"), out_offset=None, in_=entries[u],
                            in_offset=bass.IndirectOffsetOnAxis(ap=idx[u][:, t, k:k + 1], axis=0),
                        ).then_inc(gath_in[t % SLOTS], 16)

            over_batches(pool, lambda b, u: None, main)

        @block.scalar
        def _(act):
            join_groups_scalar(nc, act, B, gn, gs)
            act.wait_ge(norm_done, 1)
            for b in range(B):
                last = nc.scalar.activation(xn[:, b, :], xt[:, b, :], ACT.Identity,
                                            bias=gn["shift"][:, b:b + 1], scale=gn["scale"][:, b:b + 1])
            last.then_inc(xn_ready, 1)
            act.wait_ge(pad_clear, 4)

            def prep(b, u):
                if not known(b):
                    act.wait_ge(conv_done, b - 1)
                act.wait_ge(xn_ready, 1)
                for h in range(2):
                    src = xn[h * C:(h + 1) * C, bass.ds(b, 1), :].rearrange("p o (r w) -> p (o r) w", w=W)
                    rows, rows_on = slice(1 + h * RH, 1 + (h + 1) * RH), slice(h * RH, (h + 1) * RH)
                    nc.scalar.activation(pad01[u][0:C, rows, 1:W], src[:, :, 0:W - 1], ACT.Copy).then_inc(pad_ready, 1)
                    nc.scalar.activation(pad01[u][C:P, rows], src, ACT.Copy).then_inc(pad_ready, 1)
                    nc.scalar.activation(pad22[u][0:C, rows, 0:W - 1], src[:, :, 1:W], ACT.Copy).then_inc(pad_ready, 1)
                    nc.scalar.activation(pad22[u][C:P, rows_on, 0:W - 1], src[:, :, 1:W], ACT.Copy).then_inc(pad_ready, 1)
                if known(b):
                    act.wait_ge(turned, b + 1)
                else:
                    act.wait_ge(turned, b + 1)
                    act.wait_ge(table_out[u], b * 128 if u == 0 else (b - 1) * 128)
                nc.scalar.activation(pix[u][:], p_pix[:], ACT.Copy).then_inc(pix_ready, 1)
                act.wait_ge(off_ready, b + 1)
                nc.scalar.activation(gate[:], off[:, :, 18:27], ACT.Sigmoid).then_inc(gate_ready, 1)

            def main(b, u):
                for t in range(NT):
                    if not (known(b) and b == 0 and t < 2):
                        act.wait_ge(tile_done, b * NT + (t - 1))
                    for g in range(3):
                        act.wait_ge(turned_taps, (b * NT + t) * 3 + (g + 1))
                        nc.scalar.activation(cols[t % 2][:, 3 * g:3 * g + 3], p_col[g][:], ACT.Copy).then_inc(cols_ready, 1)

            over_batches(act, prep, main)

        @block.vector
        def _(dve):
            link = Chain(dve, own_dve)
            group_norm_vector(nc, dve, link, xt, gn, gs)
            dve.nop().then_inc(norm_done, 1)
            dve.wait_ge(consts_in, 96)
            start = link.n
            STEPS = 13

            def prep(b, u):
                step = Chain(dve, own_dve, b * STEPS + start)
                tt, ts = nc.vector.tensor_tensor, nc.vector.tensor_scalar
                dve.wait_ge(conv_done, b + 1)
                if not (known(b) and b == 0):
                    dve.wait_ge(gate_ready, b)
                step(tt(off[:], p_off[:, u, 0:NT * 27].rearrange("p (t n) -> p t n", t=NT),
                        obias[:].rearrange("p (o n) -> p o n", o=1).to_broadcast([P, NT, 27]), ALU.add))
                tt(pos[:], off[:, :, 0:18], base[:], ALU.add).then_inc(off_ready, 1)
                dve.wait_ge(off_ready, b + 1)
                step(ts(pos[:], pos[:], -1.0, float(H), ALU.max, ALU.min))
                step(nc.vector.tensor_copy(posi[:], pos[:]))
                step(nc.vector.tensor_copy(low[:], posi[:]))
                step(tt(over[:], low[:], pos[:], ALU.is_gt))
                step(tt(low[:], low[:], over[:], ALU.subtract))
                step(tt(frac[:], pos[:], low[:], ALU.subtract))
                step(ts(rest[:], frac[:], -1.0, 1.0, ALU.mult, ALU.add))
                step(nc.vector.scalar_tensor_tensor(out=flat[:], in0=low[:, :, 0::2], scalar=float(WP), in1=low[:, :, 1::2],
                                                    op0=ALU.mult, op1=ALU.add))
                step(ts(idx[u][:], flat[:], float(WP + 1), None, ALU.add))
                dve.wait_ge(gate_ready, b + 1)
                step(ts(gate[:], gate[:], 2.0, None, ALU.mult))
                step(tt(rowg[:, 0], rest[:, :, 0::2], gate[:], ALU.mult))
                step(tt(rowg[:, 1], frac[:, :, 0::2], gate[:], ALU.mult))
                for n in range(4):
                    last = tt(wts[u][:, :, :, n], rowg[:, n // 2], (frac if n % 2 else rest)[:, :, 1::2], ALU.mult)
                last.then_inc(coords_ready, 1)
                dve.wait_ge(coords_ready, b + 1)

            def main(b, u):
                for t in range(NT):
                    uses = 2 * b + t // SLOTS + 1
                    dve.wait_ge(gath_in[t % SLOTS], uses * (16 * TAPS))
                    e = gath[:, t % SLOTS]
                    g = e.rearrange("p k n c -> p (k n) c")
                    w = wts[u][:, t].rearrange("p k n -> p (k n)").rearrange("p (m o) -> p m o", o=1).to_broadcast([P, 4 * TAPS, C])
                    nc.vector.tensor_tensor(g, g, w, ALU.mult).then_inc(weighted, 1)
                    dve.wait_ge(weighted, (b * NT + t) * 2 + 1)
                    nc.vector.tensor_tensor(e[:, :, 0:2], e[:, :, 0:2], e[:, :, 2:4], ALU.add).then_inc(weighted, 1)
                dve.wait_ge(tile_done, b * NT + NT)
                nc.vector.tensor_tensor(xt[:, bass.ds(b, 1), :].rearrange("p o x -> p (o x)"),
                                        xt[:, bass.ds(b, 1), :].rearrange("p o x -> p (o x)"), p_y[u][:], ALU.add).then_inc(y_added, 1)

            over_batches(dve, prep, main)

        @block.tensor
        def _(pe):
            pe.wait_ge(consts_in, 96)
            join_groups_tensor(nc, pe, gnmat[:], gn["mv"][:, :, 0], B, gn, gs)
            pe.wait_ge(xn_ready, 1)

            def prep(b, u):
                if not (known(b) and b == 0):
                    pe.wait_ge(pix_ready, b)
                pe.wait_ge(pad_ready, b * 8 + 8)
                if not known(b):
                    pe.wait_ge(coords_ready, b - 1)
                for t in range(NT):
                    for m in range(5):
                        k = C if m == 4 else P
                        src, r0 = (pad01[u], m) if m < 3 else (pad22[u], 2 * (m - 3))
                        lhs = src[0:k, 4 * t + r0:4 * t + r0 + 4].rearrange("p r w -> p (r w)")
                        last = nc.tensor.matmul(p_off[:, u, t * 27:(t + 1) * 27], lhs, wconv[0:k, m],
                                                start=(m == 0), stop=(m == 4))
                last.then_inc(conv_done, 1)
                for t in range(NT):
                    last = nc.tensor.transpose(p_pix[:, t], pad01[u][C:P, 1 + 4 * t:5 + 4 * t].rearrange("p r w -> p (r w)"),
                                               ident[C:P, C:P])
                last.then_inc(turned, 1)

            def main(b, u):
                if not known(b):
                    pe.wait_ge(y_added, b - 1)
                elif b >= 2:
                    pe.wait_ge(y_added, b - 1)

                def finish(t):
                    pe.wait_ge(cols_ready, (b * NT + (t + 1)) * 3)
                    h, q = t // 4, t % 4
                    for k in range(TAPS):
                        last = nc.tensor.matmul(p_y[u][h * C:(h + 1) * C, q * P:(q + 1) * P], wreg[:, k], cols[t % 2][:, k],
                                                start=(k == 0), stop=(k == TAPS - 1))
                    last.then_inc(tile_done, 1)

                for t in range(NT):
                    pe.wait_ge(weighted, (b * NT + (t + 1)) * 2)
                    for g in range(3):
                        if not (known(b) and b == 0 and t < 1):
                            pe.wait_ge(cols_ready, (b * NT + (t - 1)) * 3 + (g + 1))
                        for k in range(3):
                            last = nc.tensor.transpose(p_col[g][:, k],
                                                       gath[:, t % SLOTS, 3 * g + k, 0:2].rearrange("p n c -> p (n c)"), ident[:])
                        last.then_inc(turned_taps, 1)
                    if t:
                        finish(t - 1)
                finish(NT - 1)

            over_batches(pe, prep, main)



MAP_K, REACH = 7, 3
THRESHOLD = 0.8


def layer2(nc, xt, d):
    N = B * H * W
    with ExitStack() as ctx:
        def sb(name, shape, dt=F32):
            return ctx.enter_context(nc.sbuf_tensor(name + "_2", shape, dt))

        def pb(name, shape):
            return ctx.enter_context(nc.psum_tensor(name + "_2", shape, F32))

        def sem(name):
            return ctx.enter_context(nc.semaphore(name + "_2"))

        gn, gs = stat_buffers(nc, ctx, "gn2")
        xn = sb("xn", [P, B, HALF]); maskc = sb("maskc", [P, B, HALF])
        scratch = [sb(f"scratch{u}", [P, HALF]) for u in range(2)]
        spare = sb("spare", [P, 2, HALF])
        upper = [sb(f"upper{u}", [P, HALF]) for u in range(2)]
        lower = [sb(f"lower{u}", [P, HALF]) for u in range(2)]
        band = sb("band", [P, 12, P]); ident = sb("ident", [P, P]); gnmat = sb("gnmat", [P, P]); bnmat = sb("bnmat", [P, P])
        ones = sb("ones", [P, P]); mbias = sb("mbias", [P, 2])
        pooled = sb("pooled", [P, 2, NT + 2, B])
        attn = sb("attn", [P, NT + 2, B])
        mask = sb("mask", [P, NT, B]); mod = sb("mod", [P, 2, NT, B])
        sums = sb("sums", [P, 4, B])
        tot = sb("tot", [P, 4]); pair = sb("pair", [P, 4]); size = sb("size", [P, 2]); sizew = sb("sizew", [P, 2])
        rs = sb("rs", [P, 2]); rq = sb("rq", [P, 2]); mu = sb("mu", [P, 2]); amp2 = sb("amp2", [P, 2]); amp = sb("amp", [P, 2])
        tmp = sb("tmp", [P, 2]); cst = sb("cst", [P, 2]); damp = sb("damp", [P, 1]); dcst = sb("dcst", [P, 1]); ncst = sb("ncst", [P, 1])
        p_t = [pb(f"p_t{u}", [P, 4, 2, C]) for u in range(2)]
        p_m = pb("p_m", [P, 4, P])
        p_g = [pb(f"p_g{u}", [P, HALF]) for u in range(2)]
        p_b = [pb(f"p_b{u}", [P, HALF]) for u in range(2)]

        consts_in = sem("consts_in"); own_dve = sem("own_dve"); norm_done = sem("norm_done"); xn_ready = sem("xn_ready")
        turned = sem("turned"); reduced = sem("reduced"); pooled_ready = sem("pooled_ready"); map_conv = sem("map_conv")
        attn_ready = sem("attn_ready"); mods_conv = sem("mods_conv"); mask_ready = sem("mask_ready"); counted = sem("counted")
        mask_spread = sem("mask_spread"); maskc_ready = sem("maskc_ready"); masked_sums = sem("masked_sums")
        plain_sums = sem("plain_sums"); totals = sem("totals"); paired = sem("paired"); amp2_ready = sem("amp2_ready")
        amp_ready = sem("amp_ready"); coef_ready = sem("coef_ready"); affine_ready = sem("affine_ready")
        mod_ready = sem("mod_ready"); mod_spread = sem("mod_spread"); joined = sem("joined"); batch_done = sem("batch_done")
        zeroed = sem("zeroed"); own_pool = sem("own_pool")
        block = ctx.enter_context(nc.Block())

        @block.sync
        def _(sp):
            for name, tile in (("gnmat", gnmat), ("bnmat", bnmat), ("ident", ident), ("band", band), ("mbias", mbias)):
                sp.dma_start(tile[:], d[name][:]).then_inc(consts_in, 16)

        @block.gpsimd
        def _(pool):
            nc.gpsimd.memset(pooled[:], 0.0).then_inc(zeroed, 1)
            nc.gpsimd.memset(attn[:], 0.0).then_inc(zeroed, 1)
            nc.gpsimd.memset(ones[:], 1.0).then_inc(zeroed, 1)
            for b in range(B):
                u = b % 2
                pool.wait_ge(affine_ready, b + 1)
                nc.gpsimd.tensor_tensor(upper[u][:], upper[u][:], maskc[:, b], ALU.mult).then_inc(own_pool, 1)
                pool.wait_ge(own_pool, b + 1)
                nc.gpsimd.tensor_tensor(upper[u][:], upper[u][:], lower[u][:], ALU.add).then_inc(joined, 1)

        @block.scalar
        def _(act):
            join_groups_scalar(nc, act, B, gn, gs)
            act.wait_ge(norm_done, 1)
            for b in range(B):
                nc.scalar.activation(xn[:, b, :], xt[:, b, :], ACT.Identity, bias=gn["shift"][:, b:b + 1],
                                     scale=gn["scale"][:, b:b + 1]).then_inc(xn_ready, 1)
            act.wait_ge(map_conv, 1)
            nc.scalar.activation(attn[:, 1:NT + 1].rearrange("p t b -> p (t b)"), p_m[:, 0], ACT.Sigmoid).then_inc(attn_ready, 1)
            act.wait_ge(xn_ready, B)
            for b in range(B):
                if b:
                    act.wait_ge(plain_sums, 2 * b)
                nc.scalar.activation(spare[:, 0], xn[:, b], ACT.Copy, accum_out=sums[:, 2, b:b + 1]).then_inc(plain_sums, 1)
                nc.scalar.activation(spare[:, 1], xn[:, b], ACT.Square, accum_out=sums[:, 3, b:b + 1]).then_inc(plain_sums, 1)
                act.wait_ge(mask_spread, b + 1)
                nc.scalar.activation(maskc[:, b], p_g[b % 2][:], ACT.Copy).then_inc(maskc_ready, 1)
            act.wait_ge(amp2_ready, 1)
            nc.scalar.activation(amp[:], amp2[:], ACT.Sqrt).then_inc(amp_ready, 1)
            act.wait_ge(coef_ready, 1)
            for b in range(B):
                u = b % 2
                if b >= 2:
                    act.wait_ge(batch_done, b - 1)
                nc.scalar.activation(upper[u][:], xn[:, b], ACT.Identity, bias=dcst[:], scale=damp[:])
                nc.scalar.activation(lower[u][:], xn[:, b], ACT.Identity, bias=ncst[:], scale=amp[:, 1:2]).then_inc(affine_ready, 1)

        @block.vector
        def _(dve):
            tt, ts, stt = nc.vector.tensor_tensor, nc.vector.tensor_scalar, nc.vector.scalar_tensor_tensor
            link = Chain(dve, own_dve)
            group_norm_vector(nc, dve, link, xt, gn, gs)
            dve.nop().then_inc(norm_done, 1)
            dve.wait_ge(zeroed, 2)
            for b in range(B):
                dve.wait_ge(turned, b + 1)
                for n, op in ((0, ALU.add), (1, ALU.max)):
                    last = nc.vector.tensor_reduce(pooled[:, n, 1:NT + 1, b].rearrange("p (h q) -> p q h", h=2),
                                                   p_t[b % 2][:], AX.X, op)
                last.then_inc(reduced, 1)
            dve.wait_ge(reduced, B)
            ts(pooled[:, 0], pooled[:, 0], 1.0 / C, None, ALU.mult).then_inc(pooled_ready, 1)
            dve.wait_ge(attn_ready, 1)
            ts(mask[:], attn[:, 1:NT + 1], THRESHOLD, None, ALU.is_ge).then_inc(mask_ready, 1)
            dve.wait_ge(mods_conv, 1)
            dve.wait_ge(counted, 1)
            link(ts(mod[:, 0].rearrange("p t b -> p (t b)"), p_m[:, 1], mbias[:, 0:1], 1.0, ALU.add, ALU.add))
            ts(mod[:, 1].rearrange("p t b -> p (t b)"), p_m[:, 2], mbias[:, 1:2], None, ALU.add).then_inc(mod_ready, 1)
            link(nc.vector.tensor_reduce(size[:, 0:1], p_m[:, 3], AX.X, ALU.add))
            link(ts(size[:, 1:2], size[:, 0:1], -1.0, float(N), ALU.mult, ALU.add))
            link(ts(sizew[:], size[:], 1.0, None, ALU.max))
            for b in range(B):
                dve.wait_ge(maskc_ready, b + 1)
                s = scratch[b % 2]
                link(stt(out=s[:], in0=xn[:, b], scalar=1.0, in1=maskc[:, b], op0=ALU.mult, op1=ALU.mult,
                         accum_out=sums[:, 0, b:b + 1]))
                stt(out=s[:], in0=s[:], scalar=1.0, in1=xn[:, b], op0=ALU.mult, op1=ALU.mult,
                    accum_out=sums[:, 1, b:b + 1]).then_inc(masked_sums, 1)
            dve.wait_ge(masked_sums, B)
            dve.wait_ge(plain_sums, 2 * B)
            nc.vector.tensor_reduce(tot[:], sums[:], AX.X, ALU.add).then_inc(totals, 1)
            dve.wait_ge(paired, 1)
            link(ts(pair[:], gn["ps"][:, 0:4], 2.0, None, ALU.mult))
            link(nc.vector.tensor_copy(rs[:, 0:1], pair[:, 0:1]))
            link(tt(rs[:, 1:2], pair[:, 2:3], pair[:, 0:1], ALU.subtract))
            link(nc.vector.tensor_copy(rq[:, 0:1], pair[:, 1:2]))
            link(tt(rq[:, 1:2], pair[:, 3:4], pair[:, 1:2], ALU.subtract))
            link(nc.vector.reciprocal(tmp[:], sizew[:]))
            link(tt(mu[:], rs[:], tmp[:], ALU.mult))
            link(tt(tmp[:], mu[:], rs[:], ALU.mult))
            link(tt(rq[:], rq[:], tmp[:], ALU.subtract))
            link(ts(rq[:], rq[:], 0.0, 1.0 / N, ALU.max, ALU.mult))
            link(ts(rq[:], rq[:], GN_EPS, None, ALU.add))
            link(nc.vector.reciprocal(tmp[:], rq[:]))
            link(ts(amp2[:], sizew[:], 1.0 / N, None, ALU.mult))
            tt(amp2[:], amp2[:], tmp[:], ALU.mult).then_inc(amp2_ready, 1)
            dve.wait_ge(amp_ready, 1)
            link(tt(cst[:], amp[:], mu[:], ALU.mult))
            link(tt(damp[:], amp[:, 0:1], amp[:, 1:2], ALU.subtract))
            link(tt(dcst[:], cst[:, 1:2], cst[:, 0:1], ALU.subtract))
            ts(ncst[:], cst[:, 1:2], -1.0, None, ALU.mult).then_inc(coef_ready, 1)
            for b in range(B):
                u = b % 2
                dve.wait_ge(joined, b + 1)
                dve.wait_ge(mod_spread, b + 1)
                link(tt(upper[u][:], upper[u][:], p_g[u][:], ALU.mult))
                link(tt(upper[u][:], upper[u][:], p_b[u][:], ALU.add))
                tt(xt[:, b], xt[:, b], upper[u][:], ALU.add).then_inc(batch_done, 1)

        @block.tensor
        def _(pe):
            pe.wait_ge(consts_in, 80)
            join_groups_tensor(nc, pe, gnmat[:], gn["mv"][:, :, 0], B, gn, gs)
            for b in range(B):
                pe.wait_ge(xn_ready, b + 1)
                if b >= 2:
                    pe.wait_ge(reduced, b - 1)
                for q in range(4):
                    last = nc.tensor.transpose(p_t[b % 2][:, q].rearrange("p h c -> p (h c)"), xn[:, b, q * P:(q + 1) * P], ident[:])
                last.then_inc(turned, 1)

            def conv(out, src, m0, first, stop):
                for dt in range(3):
                    last = nc.tensor.matmul(out, band[:, m0 + dt], src[:, dt:dt + NT].rearrange("p t b -> p (t b)"),
                                            start=(first and dt == 0), stop=(stop and dt == 2))
                return last

            pe.wait_ge(zeroed, 3)
            pe.wait_ge(pooled_ready, 1)
            conv(p_m[:, 0], pooled[:, 0], 0, True, False)
            conv(p_m[:, 0], pooled[:, 1], 3, False, True).then_inc(map_conv, 1)
            pe.wait_ge(attn_ready, 1)
            conv(p_m[:, 1], attn, 6, True, True)
            conv(p_m[:, 2], attn, 9, True, True).then_inc(mods_conv, 1)
            pe.wait_ge(mask_ready, 1)
            nc.tensor.matmul(p_m[:, 3], ones[:], mask[:].rearrange("p t b -> p (t b)"), start=True, stop=True).then_inc(counted, 1)

            def spread(out, src, b):
                for q in range(4):
                    for h in range(2):
                        last = nc.tensor.matmul(out[h * C:(h + 1) * C, q * P:(q + 1) * P],
                                                src[:, h * 4 + q, b:b + 1].to_broadcast([P, C]), ident[:], start=True, stop=True)
                return last

            for b in range(B):
                if b >= 2:
                    pe.wait_ge(maskc_ready, b - 1)
                spread(p_g[b % 2], mask, b).then_inc(mask_spread, 1)
            pe.wait_ge(totals, 1)
            nc.tensor.matmul(gn["ps"][:, 0:4], bnmat[:], tot[:], start=True, stop=True).then_inc(paired, 1)
            pe.wait_ge(mod_ready, 1)
            pe.wait_ge(maskc_ready, B)
            for b in range(B):
                if b >= 2:
                    pe.wait_ge(batch_done, b - 1)
                spread(p_g[b % 2], mod[:, 0], b)
                spread(p_b[b % 2], mod[:, 1], b).then_inc(mod_spread, 1)



def layer3(nc, xt, d, out):
    A = 4
    with ExitStack() as ctx:
        def sb(name, shape, dt=F32):
            return ctx.enter_context(nc.sbuf_tensor(name + "_3", shape, dt))

        def sem(name):
            return ctx.enter_context(nc.semaphore(name + "_3"))

        inw = sb("inw", [P, 3 * A, HALF]); inb = sb("inb", [P, 3 * A, HALF])
        hidw = sb("hidw", [P, A, A, HALF]); hidb = sb("hidb", [P, A, HALF])
        outw = sb("outw", [P, A, HALF]); outb = sb("outb", [P, HALF])
        ident = sb("ident", [P, P]); before = sb("before", [P, P]); follow = sb("follow", [P, P])
        first = sb("first", [P, 1])
        xh = [sb(f"xh{u}", [P, HALF]) for u in range(2)]
        xres = sb("xres", [P, HALF])
        recip = sb("recip", [P, HALF])
        expo, lost = xt[:, 0:A], xt[:, A:2 * A]
        z = [xt[:, 2 * A:4 * A], sb("z1", [P, 2 * A, HALF])]
        value_y = sb("value_y", [P, A * (HALF + 1)])
        value = value_y[:, 0:A * HALF].rearrange("p (i x) -> p i x", i=A)
        y = value_y[:].rearrange("p (i x) -> p i x", i=A)
        work = sb("work", [P, A * (A + 1), HALF])
        kv = work[:].rearrange("p (i j) x -> p i j x", j=A + 1)
        hid = work[:, 0:A * A].rearrange("p (a j) x -> p a j x", j=A)
        gated = work[:, A * A:]
        scale = sb("scale", [P, B]); shift = sb("shift", [P, B])
        gnmat = work[:, 0, 0:P]
        gn = {"st": work[:, 1, 0:6 * B].rearrange("p (b s) -> p b s", b=B), "mv": work[:, 2, 0:2 * B].rearrange("p (b s) -> p b s", b=B),
              "mean": work[:, 3, 0:B], "dev": work[:, 4, 0:B], "var": work[:, 5, 0:B], "sd": work[:, 6, 0:B], "scale": scale, "shift": shift}
        gs = {name: ctx.enter_context(nc.semaphore(f"gn3_{name}")) for name in STAT_SEMS}
        p_num = ctx.enter_context(nc.psum_tensor("p_num_3", [P, A + 1, HALF], F32))
        p_out = ctx.enter_context(nc.psum_tensor("p_out_3", [P, HALF], F32))
        p_small = ctx.enter_context(nc.psum_tensor("p_small_3", [P, HALF], F32))
        gn["ps"] = p_small
        resid = nc.dram_tensor("resid", (B, P, HALF), F32, kind="Internal").ap()

        consts_in = sem("consts_in"); own_dve = sem("own_dve"); norm_done = sem("norm_done")
        v_scaled = sem("v_scaled"); v_biased = sem("v_biased"); xh_ready = sem("xh_ready"); scaled = sem("scaled"); biased = sem("biased"); soft = sem("soft")
        scanned = sem("scanned"); carried = sem("carried"); queried = sem("queried"); summed = sem("summed")
        y_ready = sem("y_ready"); shifted = sem("shifted"); y_first = sem("y_first")
        hid_scaled = sem("hid_scaled"); hid_ready = sem("hid_ready"); hid_summed = sem("hid_summed"); tanh_ready = sem("tanh_ready")
        saved = sem("saved"); x_in = [sem(f"x_in{u}") for u in range(2)]; res_in = sem("res_in"); out_done = sem("out_done")
        own_act = sem("own_act"); expd = sem("expd"); lost_ready = sem("lost_ready"); logd = sem("logd"); relud = sem("relud")
        key_copied = sem("key_copied"); gated_ready = sem("gated_ready"); out_summed = sem("out_summed"); added = sem("added")
        block = ctx.enter_context(nc.Block())

        def known(b):
            return isinstance(b, int)

        def over_batches(eng, main):
            main(0, 0, True)
            with eng.Fori(0, B // 2 - 1) as rr:
                main(rr * 2 + 1, 1, True)
                main(rr * 2 + 2, 0, True)
            main(B - 1, 1, False)

        @block.sync
        def _(sp):
            sp.dma_start(gnmat, d["gnmat"][:]).then_inc(consts_in, 16)
            for b in range(B):
                sp.dma_start(resid[b], xt[:, b]).then_inc(saved, 16)
            for name, tile in (("ident", ident), ("before", before), ("follow", follow), ("first", first),
                               ("inw", inw), ("inb", inb), ("hidw", hidw), ("hidb", hidb), ("outw", outw), ("outb", outb)):
                sp.dma_start(tile[:], d[name][:]).then_inc(consts_in, 16)
            sp.wait_ge(saved, 16 * B)

            def load(b, u):
                sp.dma_start(xh[u][:], resid[bass.ds(b, 1)].rearrange("o p x -> (o p) x")).then_inc(x_in[u], 16)

            def main(b, u, nxt):
                if not (known(b) and b == 0):
                    sp.wait_ge(out_done, b * 16)
                    if nxt:
                        sp.wait_ge(v_scaled, b)
                if nxt:
                    load(b + 1, 1 - u)
                sp.dma_start(xres[:], resid[bass.ds(b, 1)].rearrange("o p x -> (o p) x")).then_inc(res_in, 16)
                sp.wait_ge(added, b + 1)
                sp.dma_start(out[:, bass.ds(b, 1)].rearrange("p o x -> p (o x)"), xres[:]).then_inc(out_done, 16)

            load(0, 0)
            over_batches(sp, main)
            sp.wait_ge(out_done, 16 * B)

        @block.gpsimd
        def _(pool):
            tt = nc.gpsimd.tensor_tensor

            def add_bias(b, u, g):
                pool.wait_ge(scaled, b + 1)
                part = z[u][:, g * A:(g + 1) * A]
                tt(part, part, inb[:, (1 - g) * A:(2 - g) * A], ALU.add).then_inc(biased, 1)

            def add_value_bias(b):
                pool.wait_ge(v_scaled, b + 1)
                tt(value, value, inb[:, 2 * A:], ALU.add).then_inc(v_biased, 1)

            def lost_part(b, g):
                pool.wait_ge(expd, b * 2 + (g + 1))
                tt(lost, expo, lost, ALU.subtract).then_inc(lost_ready, 1)

            def softplus_end(b, u, g):
                pool.wait_ge(relud, b * 2 + (g + 1))
                part = z[u][:, g * A:(g + 1) * A]
                tt(part, part, lost, ALU.add).then_inc(soft, 1)

            def main(b, u, nxt):
                if nxt:
                    add_bias(b + 1, 1 - u, 0)
                softplus_end(b, u, 1)
                if nxt:
                    add_bias(b + 1, 1 - u, 1)
                    lost_part(b + 1, 0)
                    softplus_end(b + 1, 1 - u, 0)
                for a in range(A):
                    pool.wait_ge(hid_scaled, b * A + (a + 1))
                    tt(hid[:, a, 0:2], hid[:, a, 0:2], hid[:, a, 2:4], ALU.add).then_inc(hid_ready, 1)
                if nxt:
                    add_value_bias(b + 1)
                    lost_part(b + 1, 1)

            add_bias(0, 0, 0)
            add_bias(0, 0, 1)
            add_value_bias(0)
            lost_part(0, 0)
            softplus_end(0, 0, 0)
            lost_part(0, 1)
            over_batches(pool, main)

        @block.scalar
        def _(act):
            join_groups_scalar(nc, act, B, gn, gs)
            act.wait_ge(norm_done, 1)
            act.wait_ge(saved, 16 * B)

            def normalise(b, u):
                act.wait_ge(x_in[u], (b // 2 + 1) * 16 if known(b) else (b * 8 + 16 if u == 0 else b * 8 + 8))
                nc.scalar.activation(xh[u][:], xh[u][:], ACT.Identity,
                                     bias=shift[:, bass.ds(b, 1)], scale=scale[:, bass.ds(b, 1)]).then_inc(xh_ready, 1)

            def exponential(b, u, g):
                step = Chain(act, own_act, (b * 2 + g) * 3)
                if not (known(b) and b == 0 and g == 0):
                    act.wait_ge(relud, b * 2 + g)
                    act.wait_ge(soft, b * 2 + g)
                act.wait_ge(biased, b * 2 + (g + 1))
                step(nc.scalar.activation(expo, z[u][:, g * A:(g + 1) * A], ACT.Abs))
                step(nc.scalar.activation(expo, expo, ACT.Exp, scale=-1.0))
                step(nc.scalar.activation(lost, expo, ACT.Copy, bias=1.0))
                nc.scalar.activation(lost, lost, ACT.Copy, bias=-1.0).then_inc(expd, 1)

            def logarithm(b, g):
                act.wait_ge(lost_ready, b * 2 + (g + 1))
                nc.scalar.activation(expo, expo, ACT.Ln, bias=1.0).then_inc(logd, 1)

            def main(b, u, nxt):
                if not (known(b) and b == 0):
                    act.wait_ge(out_summed, b)
                act.wait_ge(soft, b * 2 + 1)
                nc.scalar.activation(kv[:, :, A], z[u][:, 0:A], ACT.Copy).then_inc(key_copied, 1)
                if nxt:
                    normalise(b + 1, 1 - u)
                    exponential(b + 1, 1 - u, 0)
                    logarithm(b + 1, 0)
                act.wait_ge(shifted, b + 1)
                nc.scalar.activation(y[:, :, 0], p_small[:, 32:32 + A], ACT.Identity, bias=first[:]).then_inc(y_first, 1)
                if nxt:
                    exponential(b + 1, 1 - u, 1)
                for a in range(A):
                    act.wait_ge(hid_summed, b * A + (a + 1))
                    nc.scalar.activation(gated[:, a], p_num[:, a], ACT.Tanh).then_inc(tanh_ready, 1)
                if nxt:
                    logarithm(b + 1, 1)

            act.wait_ge(consts_in, 176)
            normalise(0, 0)
            exponential(0, 0, 0)
            logarithm(0, 0)
            exponential(0, 0, 1)
            logarithm(0, 1)
            over_batches(act, main)

        @block.vector
        def _(dve):
            tt, ts, stt = nc.vector.tensor_tensor, nc.vector.tensor_scalar, nc.vector.scalar_tensor_tensor
            link = Chain(dve, own_dve)
            group_norm_vector(nc, dve, link, xt, gn, gs)
            dve.nop().then_inc(norm_done, 1)
            dve.wait_ge(consts_in, 176)
            start = link.n

            def keys_queries(b, u):
                dve.wait_ge(xh_ready, b + 1)
                x = xh[u][:].rearrange("p (o x) -> p o x", o=1).to_broadcast([P, A, HALF])
                tt(z[u][:, 0:A], inw[:, A:2 * A], x, ALU.mult)
                tt(z[u][:, A:], inw[:, 0:A], x, ALU.mult).then_inc(scaled, 1)

            def values(b, u):
                if not (known(b) and b == 0):
                    dve.wait_ge(hid_scaled, b * A)
                tt(value, inw[:, 2 * A:], xh[u][:].rearrange("p (o x) -> p o x", o=1).to_broadcast([P, A, HALF]),
                   ALU.mult).then_inc(v_scaled, 1)

            def relu_log(b, u, g):
                dve.wait_ge(logd, b * 2 + (g + 1))
                part = z[u][:, g * A:(g + 1) * A]
                stt(out=part, in0=part, scalar=0.0, in1=expo, op0=ALU.max, op1=ALU.add).then_inc(relud, 1)

            def main(b, u, nxt):
                dve.wait_ge(v_biased, b + 1)
                dve.wait_ge(soft, b * 2 + 1)
                tt(kv[:, :, 0:A], z[u][:, 0:A].rearrange("p i (o x) -> p i o x", o=1).to_broadcast([P, A, A, HALF]),
                   value.rearrange("p (o j) x -> p o j x", o=1).to_broadcast([P, A, A, HALF]), ALU.mult).then_inc(scanned, 1)
                if nxt:
                    keys_queries(b + 1, 1 - u)
                relu_log(b, u, 1)
                dve.wait_ge(scanned, b * 2 + 1)
                dve.wait_ge(key_copied, b + 1)
                for n in range(A * (A + 1)):
                    last = nc.vector.tensor_tensor_scan(out=work[:, n], data0=work[:, n], data1=work[:, n], initial=0.0,
                                                        op0=ALU.add, op1=ALU.bypass)
                last.then_inc(scanned, 1)
                dve.wait_ge(scanned, b * 2 + 2)
                dve.wait_ge(soft, b * 2 + 2)
                dve.wait_ge(carried, b + 1)
                for i in range(A):
                    for j in range(A + 1):
                        n = i * (A + 1) + j
                        last = stt(out=work[:, n], in0=work[:, n], scalar=p_small[:, n:n + 1], in1=z[u][:, A + i],
                                   op0=ALU.add, op1=ALU.mult)
                    last.then_inc(queried, 1)
                if nxt:
                    relu_log(b + 1, 1 - u, 0)
                dve.wait_ge(summed, b + 1)
                nc.vector.reciprocal(recip[:], p_num[:, A]).then_inc(own_dve, 1)
                dve.wait_ge(own_dve, b + (start + 1))
                tt(y[:, :, 1:], p_num[:, 0:A], recip[:].rearrange("p (o x) -> p o x", o=1).to_broadcast([P, A, HALF]),
                   ALU.mult).then_inc(y_ready, 1)
                dve.wait_ge(y_ready, b + 1)
                dve.wait_ge(y_first, b + 1)
                for a in range(A):
                    tt(hid[:, a], hidw[:, a], y[:, :, 0:HALF], ALU.mult).then_inc(hid_scaled, 1)
                if nxt:
                    values(b + 1, 1 - u)
                dve.wait_ge(tanh_ready, b * A + A)
                tt(gated, gated, outw[:], ALU.mult).then_inc(gated_ready, 1)
                dve.wait_ge(out_summed, b + 1)
                dve.wait_ge(res_in, b * 16 + 16)
                tt(xres[:], xres[:], p_out[:], ALU.add).then_inc(added, 1)

            keys_queries(0, 0)
            values(0, 0)
            relu_log(0, 0, 0)
            over_batches(dve, main)

        @block.tensor
        def _(pe):
            pe.wait_ge(consts_in, 176)
            join_groups_tensor(nc, pe, gnmat[:], gn["mv"][:, :, 0], B, gn, gs)

            def main(b, u, nxt):
                pe.wait_ge(scanned, b * 2 + 2)
                nc.tensor.matmul(p_small[:, 0:A * (A + 1)], before[:], work[:, :, HALF - 1], start=True, stop=True).then_inc(carried, 1)
                for i in range(A):
                    pe.wait_ge(queried, b * A + (i + 1))
                    for j in range(A + 1):
                        last = nc.tensor.matmul(p_num[:, j], ident[:], kv[:, i, j], start=(i == 0), stop=(i == A - 1))
                last.then_inc(summed, 1)
                pe.wait_ge(y_ready, b + 1)
                nc.tensor.matmul(p_small[:, 32:32 + A], follow[:], y[:, :, HALF], start=True, stop=True).then_inc(shifted, 1)
                for a in range(A):
                    nc.tensor.matmul(p_num[:, a], ident[:], hidb[:, a], start=True, stop=False)
                    pe.wait_ge(hid_ready, b * A + (a + 1))
                    nc.tensor.matmul(p_num[:, a], ident[:], hid[:, a, 0], start=False, stop=False)
                    nc.tensor.matmul(p_num[:, a], ident[:], hid[:, a, 1], start=False, stop=True).then_inc(hid_summed, 1)
                if not (known(b) and b == 0):
                    pe.wait_ge(added, b)
                nc.tensor.matmul(p_out[:], ident[:], outb[:], start=True, stop=False)
                pe.wait_ge(gated_ready, b + 1)
                for a in range(A):
                    last = nc.tensor.matmul(p_out[:], ident[:], gated[:, a], start=False, stop=(a == A - 1))
                last.then_inc(out_summed, 1)

            over_batches(pe, main)


def build_program(nc, d, out):
    with nc.sbuf_tensor("xt", [P, B, HALF], F32) as xt:
        layer0(nc, xt, d)
        layer1(nc, xt, d)
        layer2(nc, xt, d)
        layer3(nc, xt, d, out)


def layouts(inp):
    import numpy as np
    f = lambda n: np.asarray(inp[n])
    a = {}
    x = f("x").reshape(B, C, 2, HALF)
    a["x"] = x.transpose(2, 1, 0, 3).reshape(P, B, HALF)
    w = f("L0_conv_weight").reshape(C, 2, RH, 4, 8, C, 3, 3)
    w0 = np.zeros((RH, 4, 2, C, 8, 9, C), np.float32)
    t = w.transpose(1, 2, 3, 5, 4, 6, 7, 0)
    for h in range(2):
        for m in range(3):
            w0[:, :, 0, :, :, 4 * h + m] = t[h, :, :, :, :, m, 0]
            w0[:, :, 1, :, :, 4 * h + m] = t[h, :, :, :, :, m, 1]
        w0[:, :, 0, :, :, 4 * h + 3] = t[h, :, :, :, :, 0, 2]
        w0[:, :, 1, :, :, 4 * h + 3] = t[h, :, :, :, :, 1, 2]
        w0[:, :, h, :, :, 8] = t[h, :, :, :, :, 2, 2]
    a["w0"] = w0.reshape(RH, 4, P, 8, 9, C)
    a["bias0"] = f("L0_conv_bias").reshape(C, 2, HALF).transpose(1, 0, 2).reshape(P, HALF)
    a["affine0"] = np.stack([np.tile(f("L0_conv_gamma"), 2), np.tile(f("L0_conv_beta"), 2)], axis=1)
    p = np.arange(P)
    a["gnmat"] = (((p[:, None] % C) // 2 == (p[None, :] % C) // 2) / 4.0).astype(np.float32)
    a["bnmat"] = ((p[:, None] % C == p[None, :] % C) / 2.0).astype(np.float32)
    w = np.concatenate([f("L1_conv_offset_w"), f("L1_conv_mod_w")], axis=0)
    w1 = np.zeros((2, C, 5, 27), np.float32)
    for m in range(3):
        w1[0, :, m] = w[:, :, m, 0].T
        w1[1, :, m] = w[:, :, m, 1].T
    w1[0, :, 3], w1[1, :, 3], w1[0, :, 4] = w[:, :, 0, 2].T, w[:, :, 1, 2].T, w[:, :, 2, 2].T
    a["wconv"] = w1.reshape(P, 5, 27)
    r = f("L1_conv_reg_w").reshape(C, C, TAPS)
    a["wreg"] = np.tile(r.transpose(1, 2, 0), (2, 1, 1))
    a["ident"] = np.eye(P, dtype=np.float32)
    a["obias"] = np.tile(np.concatenate([f("L1_conv_offset_b"), f("L1_conv_mod_b")]), (P, 1))
    t, k = np.arange(NT), np.arange(TAPS)
    base = np.zeros((P, NT, TAPS, 2), np.float32)
    base[..., 0] = (4 * t[None, :] + p[:, None] // W)[:, :, None] + k // 3 - 1
    base[..., 1] = (p % W)[:, None, None] + k % 3 - 1
    a["base"] = base.reshape(P, NT, 18)
    band = np.zeros((P, 4, 3, P), np.float32)
    kern = [f("L2_conv_w1")[0, 0], f("L2_conv_w1")[0, 1], f("L2_conv_wg")[0, 0], f("L2_conv_wb")[0, 0]]
    for n, w in enumerate(kern):
        for dt in range(3):
            for r in range(4):
                for q in range(4):
                    dy = 4 * (dt - 1) + r - q + REACH
                    if 0 <= dy < MAP_K:
                        for x in range(W):
                            for o in range(max(0, x - REACH), min(W, x + REACH + 1)):
                                band[r * W + x, n, dt, q * W + o] = w[dy, x - o + REACH]
    a["band"] = band.reshape(P, 12, P)
    a["mbias"] = np.tile(np.concatenate([f("L2_conv_bg"), f("L2_conv_bb")]), (P, 1))
    def by_position(v, lead):
        v = v.reshape(lead + (C, 2, HALF, -1))
        n = len(lead)
        v = v.transpose((n + 1, n) + tuple(range(n)) + (n + 3, n + 2))
        return v.reshape((P,) + lead + (-1, HALF))
    a["inw"] = by_position(f("L3_conv_in_proj_weight"), (3,)).reshape(P, 12, HALF)
    a["inb"] = by_position(f("L3_conv_in_proj_bias"), (3,)).reshape(P, 12, HALF)
    a["hidw"] = by_position(f("L3_conv_hid_proj_weight"), (4,))
    a["hidb"] = by_position(f("L3_conv_hid_proj_bias"), (4,)).reshape(P, 4, HALF)
    a["outw"] = by_position(f("L3_conv_out_proj_weight"), (4,)).reshape(P, 4, HALF)
    a["outb"] = by_position(f("L3_conv_out_proj_bias"), ()).reshape(P, HALF)
    segment = 2 * (p % C) + p // C
    a["before"] = (segment[:, None] < segment[None, :]).astype(np.float32)
    a["follow"] = (segment[:, None] + 1 == segment[None, :]).astype(np.float32)
    a["first"] = (segment == 0).astype(np.float32).reshape(P, 1)
    return a


def kernel(**inputs):
    import numpy as np
    import concourse.bacc as bacc
    from concourse.bass_utils import run_bass_kernel_spmd

    arrays = {"in_" + n: np.ascontiguousarray(v) for n, v in layouts(inputs).items()}
    nc = bacc.Bacc("TRN2", target_bir_lowering=False, num_devices=1)
    d = {n[3:]: nc.dram_tensor(n, a.shape, mybir.dt.from_np(a.dtype), kind="ExternalInput").ap() for n, a in arrays.items()}
    y = nc.dram_tensor("y", (P, B, HALF), F32, kind="ExternalOutput").ap()
    build_program(nc, d, y)
    got = run_bass_kernel_spmd(nc, [arrays], core_ids=[0]).results[0]["y"]
    return got.reshape(2, C, B, RH, W).transpose(2, 1, 0, 3, 4).reshape(B, C, H, W)
```

```python
import concourse.bass as bass
from concourse import mybir
from contextlib import ExitStack

F32 = mybir.dt.float32
I32 = mybir.dt.int32
U32 = mybir.dt.uint32
ALU = mybir.AluOpType
ACT = mybir.ActivationFunctionType
AX = mybir.AxisListType

B, C, H, W = 16, 64, 32, 32
P = 128
HALF = H * W // 2
RH = H // 2
WP = W + 2
TAPS = 9
GN_EPS = 1e-5


class Chain:

    def __init__(self, eng, sem, base=0):
        self.eng, self.sem, self.n = eng, sem, base

    def __call__(self, ins):
        self.n = self.n + 1
        ins.then_inc(self.sem, 1)
        self.eng.wait_ge(self.sem, self.n)


def group_norm_vector(nc, dve, link, x, t, s, row_stats=None):
    if row_stats is None:
        row_stats = t["st"]
        for b in range(B):
            last = nc.vector.bn_stats(row_stats[:, b, :], x[:, b, :])
        link(last)
    for b in range(B):
        last = nc.vector.bn_aggr(t["mv"][:, b, :], row_stats[:, b, :])
    last.then_inc(s["row_stats"], 1)
    join_groups_vector(nc, dve, link, t["mv"][:, :, 0], t["mv"][:, :, 1], B, t, s)
    link(nc.vector.scalar_tensor_tensor(out=t["shift"][:, 0:B], in0=t["mean"][:, 0:B], scalar=-1.0,
                                        in1=t["scale"][:, 0:B], op0=ALU.mult, op1=ALU.mult))


def join_groups_vector(nc, dve, link, mean, var, n, t, s):
    dve.wait_ge(s["joined_mean"], 1)
    link(nc.vector.tensor_copy(t["mean"][:, 0:n], t["ps"][:, 0:n]))
    link(nc.vector.tensor_tensor(t["dev"][:, 0:n], mean, t["mean"][:, 0:n], ALU.subtract))
    link(nc.vector.tensor_tensor(t["dev"][:, 0:n], t["dev"][:, 0:n], t["dev"][:, 0:n], ALU.mult))
    nc.vector.tensor_tensor(t["dev"][:, 0:n], t["dev"][:, 0:n], var, ALU.add).then_inc(s["spread"], 1)
    dve.wait_ge(s["joined_var"], 1)
    nc.vector.tensor_scalar(t["var"][:, 0:n], t["ps"][:, B:B + n], GN_EPS, None, ALU.add).then_inc(s["var_eps"], 1)
    dve.wait_ge(s["deviation"], 1)
    link(nc.vector.reciprocal(t["scale"][:, 0:n], t["sd"][:, 0:n]))


def join_groups_tensor(nc, pe, matrix, mean, n, t, s):
    pe.wait_ge(s["row_stats"], 1)
    nc.tensor.matmul(t["ps"][:, 0:n], matrix, mean, start=True, stop=True).then_inc(s["joined_mean"], 1)
    pe.wait_ge(s["spread"], 1)
    nc.tensor.matmul(t["ps"][:, B:B + n], matrix, t["dev"][:, 0:n], start=True, stop=True).then_inc(s["joined_var"], 1)


def join_groups_scalar(nc, act, n, t, s):
    act.wait_ge(s["var_eps"], 1)
    nc.scalar.activation(t["sd"][:, 0:n], t["var"][:, 0:n], ACT.Sqrt).then_inc(s["deviation"], 1)


STAT_SEMS = ["row_stats", "joined_mean", "spread", "joined_var", "var_eps", "deviation"]


def stat_buffers(nc, ctx, tag):
    def sb(name, cols):
        return ctx.enter_context(nc.sbuf_tensor(f"{tag}_{name}", cols, F32))

    t = {"st": sb("st", [P, B, 6]), "mv": sb("mv", [P, B, 2])}
    for name in ("mean", "dev", "var", "sd", "scale", "shift"):
        t[name] = sb(name, [P, B])
    t["ps"] = ctx.enter_context(nc.psum_tensor(f"{tag}_ps", [P, 2 * B], F32))
    s = {name: ctx.enter_context(nc.semaphore(f"{tag}_{name}")) for name in STAT_SEMS}
    return t, s


def layer0(nc, xt, d):
    NQ, PX = 4, 8
    RING = 4
    G, QUAD = 4, 32
    with ExitStack() as ctx:
        def sb(name, shape):
            return ctx.enter_context(nc.sbuf_tensor(name, shape, F32))

        def sem(name):
            return ctx.enter_context(nc.semaphore(name))

        gn, gs = stat_buffers(nc, ctx, "gn0")
        bn, bs = stat_buffers(nc, ctx, "bn0")
        xh = sb("xh", [P, RH + 2, WP, B])
        win_a = sb("win_a", [P, 2, 2, 3, WP, B])
        win_b = sb("win_b", [P, 2, 2, W, B])
        ring = sb("ring", [P, RING, PX, TAPS, C])
        bias = sb("bias0", [P, HALF])
        gnmat = sb("gnmat0", [P, P])
        bnmat = sb("bnmat0", [P, P])
        affine = sb("affine0", [P, 2])
        fold = sb("fold0", [P, 2])
        sums = sb("sums0", [P, 2, W // G, P])
        acc = [ctx.enter_context(nc.psum_tensor(f"acc0_{i}", [P, 2, W // G, C], F32)) for i in range(2)]
        turn = ctx.enter_context(nc.psum_tensor("turn0", [P, W, QUAD], F32))
        ident = sb("ident0", [P, P])

        x_in = sem("x_in"); consts_in = sem("consts_in")
        w_in = [sem(f"w_in{i}") for i in range(RING)]
        w_used = sem("w_used")
        own_dve = sem("own_dve"); border_done = sem("border_done")
        norm_done = sem("norm_done"); xh_ready = sem("xh_ready")
        win_a_ready = sem("win_a_ready"); win_b_ready = sem("win_b_ready")
        row_stored = sem("row_stored"); acc_clear = sem("acc_clear"); copied = sem("copied"); turned = sem("turned0")
        bn_ready = sem("bn_ready"); slot_free = sem("slot_free"); relu_done = sem("relu_done"); xr_in = sem("xr_in")
        block = ctx.enter_context(nc.Block())
        xr = ring[:, 0:2].rearrange("p s a t c -> p (s a t c)")[:, 0:B * HALF].rearrange("p (b x) -> p b x", b=B)

        @block.sync
        def _(sp):
            sp.dma_start(xt[:], d["x"][:]).then_inc(x_in, 16)
            for name, tile in (("gnmat", gnmat), ("bnmat", bnmat), ("bias0", bias), ("affine0", affine), ("ident", ident)):
                sp.dma_start(tile[:], d[name][:]).then_inc(consts_in, 16)
            for q in range(NQ):
                sp.dma_start(ring[:, q], d["w0"][0, q]).then_inc(w_in[q], 16)
            with sp.Fori(1, RH) as r:
                for q in range(NQ):
                    sp.wait_ge(w_used, r * NQ + (q - NQ + 1))
                    sp.dma_start(ring[:, q], d["w0"][r, q]).then_inc(w_in[q], 16)
            sp.wait_ge(w_used, RH * NQ)
            sp.dma_start(xr, d["x"][:]).then_inc(xr_in, 16)

        @block.gpsimd
        def _(pool):
            nc.gpsimd.memset(xh[:], 0.0).then_inc(border_done, 1)

        @block.scalar
        def _(act):
            join_groups_scalar(nc, act, B, gn, gs)
            act.wait_ge(norm_done, 1)
            act.wait_ge(border_done, 1)
            xv = xh[:].rearrange("p r w b -> p b r w")
            for b in range(B):
                last = nc.scalar.activation(xv[:, b, 1:RH + 1, 1:W + 1],
                                            xt[:, b, :].rearrange("p (r w) -> p r w", w=W), ACT.Identity,
                                            bias=gn["shift"][:, b:b + 1], scale=gn["scale"][:, b:b + 1])
            last.then_inc(xh_ready, 1)


            def windows(r, u, first):
                if first:
                    act.wait_ge(xh_ready, 3)
                else:
                    act.wait_ge(w_used, NQ * r - NQ)
                    act.sem_inc(slot_free, 1)
                for h in range(2):
                    src = xh[h * C:(h + 1) * C]
                    nc.scalar.activation(win_b[0:C, u, h], src[:, bass.ds(r, 1), 2:WP].rearrange("p r w b -> p (r w) b"),
                                         ACT.Copy).then_inc(win_b_ready, 1)
                    nc.scalar.activation(win_b[C:P, u, h], src[:, bass.ds(r + 1, 1), 2:WP].rearrange("p r w b -> p (r w) b"),
                                         ACT.Copy).then_inc(win_b_ready, 1)

            def copy(r, u, first):
                act.wait_ge(w_used, NQ * r + NQ)
                if not first:
                    act.wait_ge(turned, r - 1)
                for n in range(2):
                    nc.scalar.activation(sums[:, u, :, n * C:(n + 1) * C], acc[u][:, n], ACT.Copy).then_inc(copied, 1)

            windows(0, 0, True)
            windows(1, 1, True)
            copy(0, 0, True)
            windows(2, 0, False)
            copy(1, 1, True)
            windows(3, 1, False)
            with act.Fori(1, RH // 2 - 1) as rr:
                copy(rr * 2, 0, False)
                windows(rr * 2 + 2, 0, False)
                copy(rr * 2 + 1, 1, False)
                windows(rr * 2 + 3, 1, False)
            copy(RH - 2, 0, False)
            copy(RH - 1, 1, False)
            join_groups_scalar(nc, act, 1, bn, bs)
            act.wait_ge(bn_ready, 1)
            for b in range(B):
                nc.scalar.activation(xt[:, b, :], xt[:, b, :], ACT.Relu, bias=fold[:, 1:2],
                                     scale=fold[:, 0:1]).then_inc(relu_done, 1)

        @block.vector
        def _(dve):
            link = Chain(dve, own_dve)
            for u in range(2):
                nc.vector.memset(acc[u][:], 0.0).then_inc(acc_clear, 1)
            dve.wait_ge(x_in, 16)
            group_norm_vector(nc, dve, link, xt, gn, gs)
            nc.vector.tensor_copy(gn["st"][:, 0, 0:1], gn["st"][:, 0, 0:1]).then_inc(norm_done, 1)
            dve.wait_ge(xh_ready, 1)
            nc.vector.tensor_copy(xh[0:C, RH + 1], xh[C:P, 1]).then_inc(xh_ready, 1)
            nc.vector.tensor_copy(xh[C:P, 0], xh[0:C, RH]).then_inc(xh_ready, 1)
            dve.wait_ge(xh_ready, 3)

            def windows(r, u, first):
                if not first:
                    dve.wait_ge(w_used, NQ * r - NQ)
                for h in range(2):
                    src = xh[h * C:(h + 1) * C]
                    nc.vector.tensor_copy(win_a[0:C, u, h], src[:, bass.ds(r, 3)]).then_inc(win_a_ready, 1)
                    nc.vector.tensor_copy(win_a[C:P, u, h, :, 0:WP - 1], src[:, bass.ds(r, 3), 1:WP]).then_inc(win_a_ready, 1)

            def store(r, u):
                dve.wait_ge(turned, r + 1)
                bcol = bias[:, bass.ds(r * W, W)].rearrange("p (o w) -> p o w", o=1).to_broadcast([P, B, W])
                nc.vector.tensor_tensor(xt[:, :, bass.ds(r * W, W)], turn[:, :, 0:B].rearrange("p w b -> p b w"),
                                        bcol, ALU.add).then_inc(row_stored, 1)

            dve.wait_ge(consts_in, 80)
            for u in range(2):
                windows(u, u, True)
            with dve.Fori(1, RH // 2) as rr:
                for u in range(2):
                    windows(rr * 2 + u, u, False)
                    store(rr * 2 + (u - 2), u)
            for u in range(2):
                store(RH - 2 + u, u)
            dve.wait_ge(row_stored, RH)
            for b in range(B):
                last = nc.vector.bn_stats(bn["st"][:, b, :], xt[:, b, :])
            link(last)
            nc.vector.bn_aggr(bn["mv"][:, 0, :], bn["st"][:].rearrange("p b s -> p (b s)")).then_inc(bs["row_stats"], 1)
            join_groups_vector(nc, dve, link, bn["mv"][:, 0, 0:1], bn["mv"][:, 0, 1:2], 1, bn, bs)
            link(nc.vector.tensor_tensor(fold[:, 0:1], bn["scale"][:, 0:1], affine[:, 0:1], ALU.mult))
            link(nc.vector.tensor_tensor(fold[:, 1:2], bn["mean"][:, 0:1], fold[:, 0:1], ALU.mult))
            nc.vector.tensor_tensor(fold[:, 1:2], affine[:, 1:2], fold[:, 1:2], ALU.subtract).then_inc(bn_ready, 1)
            dve.wait_ge(xr_in, 16)
            for b in range(B):
                dve.wait_ge(relu_done, b + 1)
                nc.vector.tensor_tensor(xt[:, b, :], xt[:, b, :], xr[:, b, :], ALU.add)

        @block.tensor
        def _(pe):
            pe.wait_ge(consts_in, 80)
            join_groups_tensor(nc, pe, gnmat[:], gn["mv"][:, :, 0], B, gn, gs)

            def turn_row(r, u, first):
                pe.wait_ge(copied, 2 * r + 2)
                if not first:
                    pe.wait_ge(row_stored, r)
                for n in range(W // G):
                    last = nc.tensor.transpose(turn[:, n * G:(n + 1) * G].rearrange("p g b -> p (g b)"), sums[:, u, n], ident[:])
                last.then_inc(turned, 1)

            def row(r, u, known):
                pe.wait_ge(win_b_ready, 4 * r + 4)
                if known is None or known >= 2:
                    pe.wait_ge(copied, 2 * r - 2)
                pe.wait_ge(win_a_ready, 4 * r + 4)
                for q in range(NQ):
                    pe.wait_ge(w_in[q], 16 * r + 16)
                    wt = ring[:, q]
                    for n in range(PX // G):
                        for m in range(4):
                            for h in range(2):
                                for g in range(G):
                                    j = q * PX + n * G + g
                                    mov = win_a[:, u, h, m, j] if m < 3 else win_b[:, u, h, j]
                                    nc.tensor.matmul(acc[u][g * QUAD:g * QUAD + B, h, j // G], mov, wt[:, n * G + g, 4 * h + m],
                                                     start=(j < G and m == 0), stop=False)
                    for n in range(PX // G):
                        for h in range(2):
                            for g in range(G):
                                j = q * PX + n * G + g
                                last = nc.tensor.matmul(acc[u][g * QUAD:g * QUAD + B, h, j // G],
                                                        win_a[h * C:(h + 1) * C, u, h, 2, j + 2 - h],
                                                        wt[h * C:(h + 1) * C, n * G + g, 8],
                                                        start=False, stop=(j >= W - G))
                    last.then_inc(w_used, 1)
                    if q == 0 and known != 0:
                        turn_row(r - 1, 1 - u, known == 1)

            pe.wait_ge(acc_clear, 2)
            row(0, 0, 0)
            row(1, 1, 1)
            with pe.Fori(1, RH // 2) as rr:
                for u in range(2):
                    row(rr * 2 + u, u, None)
            turn_row(RH - 1, 1, False)
            pe.wait_ge(w_used, RH * NQ)
            join_groups_tensor(nc, pe, bnmat[:], bn["mv"][:, 0, 0:1], 1, bn, bs)



ENTRY = 4 * C
NT = H * W // P


def layer1(nc, xt, d, row_stats):
    SLOTS = NT
    tables = [nc.dram_tensor(f"table{u}", (WP, WP, 4, C), F32, kind="Internal").ap() for u in range(2)]
    entries = [t.rearrange("y x n c -> (y x) (n c)") for t in tables]
    with ExitStack() as ctx:
        def sb(name, shape, dt=F32):
            return ctx.enter_context(nc.sbuf_tensor(name + "_1", shape, dt))

        def pb(name, shape):
            return ctx.enter_context(nc.psum_tensor(name + "_1", shape, F32))

        def sem(name):
            return ctx.enter_context(nc.semaphore(name + "_1"))

        gn, gs = stat_buffers(nc, ctx, "gn1")
        xn = sb("xn", [P, B, HALF])
        zero = sb("zero", [WP, ENTRY])
        pad01 = [sb(f"pad01_{u}", [P, WP, W]) for u in range(2)]
        pad22 = [sb(f"pad22_{u}", [P, WP, W]) for u in range(2)]
        pix = [sb(f"pix{u}", [P, NT, C]) for u in range(2)]
        gath = sb("gath", [P, SLOTS, TAPS, 4, C])
        cols = [sb(f"cols{u}", [P, TAPS, P]) for u in range(2)]
        wconv = sb("wconv", [P, 5, 27]); wreg = sb("wreg", [P, TAPS, C])
        ident = sb("ident", [P, P]); gnmat = sb("gnmat", [P, P])
        base = sb("base", [P, NT, 18]); obias = sb("obias", [P, 27])
        off = sb("off", [P, NT, 27]); pos = sb("pos", [P, NT, 18]); posi = sb("posi", [P, NT, 18], I32)
        low = sb("low", [P, NT, 18]); over = sb("over", [P, NT, 18])
        frac = sb("frac", [P, NT, 18]); rest = sb("rest", [P, NT, 18])
        gate = sb("gate", [P, NT, TAPS]); rowg = sb("rowg", [P, 2, NT, TAPS]); flat = sb("flat", [P, NT, TAPS])
        idx = [sb(f"idx{u}", [P, NT, TAPS], I32) for u in range(2)]
        wts = [sb(f"wts{u}", [P, NT, TAPS, 4]) for u in range(2)]
        p_off = pb("p_off", [P, 2, 256])
        p_pix = pb("p_pix", [P, NT, C])
        p_col = [pb(f"p_col{g}", [P, 3, P]) for g in range(3)]
        p_y = [pb(f"p_y{u}", [P, HALF]) for u in range(2)]

        consts_in = sem("consts_in"); own_dve = sem("own_dve"); norm_done = sem("norm_done"); xn_ready = sem("xn_ready")
        zero_ready = sem("zero_ready"); border_out = sem("border_out"); slot_free = sem("slot_free"); own_pool = sem("own_pool")
        pad_clear = sem("pad_clear"); pad_ready = sem("pad_ready"); conv_done = sem("conv_done")
        turned = sem("turned"); pix_ready = sem("pix_ready"); table_out = [sem(f"table_out{u}") for u in range(2)]
        off_ready = sem("off_ready"); gate_ready = sem("gate_ready"); coords_ready = sem("coords_ready")
        gath_in = [sem(f"gath_in{s}") for s in range(SLOTS)]
        weighted = sem("weighted"); turned_taps = sem("turned_taps"); cols_ready = sem("cols_ready")
        tile_done = sem("tile_done"); y_added = sem("y_added")
        block = ctx.enter_context(nc.Block())
        NCONST = 7

        def over_batches(eng, prep, main):
            prep(0, 0)
            prep(1, 1)
            main(0, 0)
            with eng.Fori(1, B // 2) as rr:
                prep(rr * 2, 0)
                main(rr * 2 - 1, 1)
                prep(rr * 2 + 1, 1)
                main(rr * 2, 0)
            main(B - 1, 1)

        def known(b):
            return isinstance(b, int)

        @block.sync
        def _(sp):
            for name, tile in (("wconv", wconv), ("wreg", wreg), ("ident", ident), ("gnmat", gnmat), ("base", base),
                               ("obias", obias)):
                sp.dma_start(tile[:], d[name][:]).then_inc(consts_in, 16)
            sp.wait_ge(zero_ready, 1)
            for table in tables:
                for e in (0, H, H + 1):
                    sp.dma_start(table[e].rearrange("x n c -> x (n c)"), zero[:]).then_inc(border_out, 16)
            sp.wait_ge(border_out, 96)
            for table in tables:
                for e in (0, H, H + 1):
                    sp.dma_start(table[:, e].rearrange("y n c -> y (n c)"), zero[:]).then_inc(border_out, 16)
            sp.wait_ge(border_out, 192)

            def prep(b, u):
                sp.wait_ge(pix_ready, b + 1)
                if not known(b):
                    sp.wait_ge(weighted, (b - 1) * NT * 2)
                for n in range(4):
                    y0, x0 = 1 - n // 2, 1 - n % 2
                    for r in range(4):
                        dst = tables[u][y0:y0 + H, x0:x0 + W, n, :].rearrange("(t r) x c -> r x t c", r=4)[r]
                        sp.dma_start(dst, pix[u][r * W:(r + 1) * W]).then_inc(table_out[u], 16)

            over_batches(sp, prep, lambda b, u: None)
            for u in range(2):
                sp.wait_ge(table_out[u], 256 * (B // 2))

        @block.gpsimd
        def _(pool):
            nc.gpsimd.memset(zero[:], 0.0).then_inc(zero_ready, 1)
            for tile in (*pad01, *pad22):
                nc.gpsimd.memset(tile[:], 0.0).then_inc(pad_clear, 1)

            pool.wait_ge(border_out, 192)

            def main(b, u):
                pool.wait_ge(coords_ready, b + 1)
                if known(b):
                    pool.wait_ge(table_out[u], 256 * (b // 2 + 1))
                elif u == 0:
                    pool.wait_ge(table_out[u], b * 128 + 256)
                else:
                    pool.wait_ge(table_out[u], (b + 1) * 128)
                for t in range(NT):
                    if not (known(b) and b == 0 and t < SLOTS):
                        pool.wait_ge(turned_taps, (b * NT + (t + 1 - SLOTS)) * 3)
                        pool.sem_inc(slot_free, 1)
                    for k in range(TAPS):
                        nc.gpsimd.indirect_dma_start(
                            out=gath[:, t % SLOTS, k].rearrange("p n c -> p (n c)"), out_offset=None, in_=entries[u],
                            in_offset=bass.IndirectOffsetOnAxis(ap=idx[u][:, t, k:k + 1], axis=0),
                        ).then_inc(gath_in[t % SLOTS], 16)

            over_batches(pool, lambda b, u: None, main)

        @block.scalar
        def _(act):
            join_groups_scalar(nc, act, B, gn, gs)
            act.wait_ge(norm_done, 1)

            def normalise(batches):
                for b in batches:
                    last = nc.scalar.activation(xn[:, b, :], xt[:, b, :], ACT.Identity,
                                                bias=gn["shift"][:, b:b + 1], scale=gn["scale"][:, b:b + 1])
                last.then_inc(xn_ready, 1)

            normalise(range(1))
            act.wait_ge(pad_clear, 4)

            def prep(b, u):
                if not known(b):
                    act.wait_ge(conv_done, b - 1)
                act.wait_ge(xn_ready, 1 if known(b) and b == 0 else 2)
                for h in range(2):
                    src = xn[h * C:(h + 1) * C, bass.ds(b, 1), :].rearrange("p o (r w) -> p (o r) w", w=W)
                    rows, rows_on = slice(1 + h * RH, 1 + (h + 1) * RH), slice(h * RH, (h + 1) * RH)
                    nc.scalar.activation(pad01[u][0:C, rows, 1:W], src[:, :, 0:W - 1], ACT.Copy).then_inc(pad_ready, 1)
                    nc.scalar.activation(pad01[u][C:P, rows], src, ACT.Copy).then_inc(pad_ready, 1)
                    nc.scalar.activation(pad22[u][0:C, rows, 0:W - 1], src[:, :, 1:W], ACT.Copy).then_inc(pad_ready, 1)
                    nc.scalar.activation(pad22[u][C:P, rows_on, 0:W - 1], src[:, :, 1:W], ACT.Copy).then_inc(pad_ready, 1)
                if known(b) and b == 0:
                    normalise(range(1, B))
                if known(b):
                    act.wait_ge(turned, b + 1)
                else:
                    act.wait_ge(turned, b + 1)
                    act.wait_ge(table_out[u], b * 128 if u == 0 else (b - 1) * 128)
                nc.scalar.activation(pix[u][:], p_pix[:], ACT.Copy).then_inc(pix_ready, 1)
                act.wait_ge(off_ready, b + 1)
                nc.scalar.activation(gate[:], off[:, :, 18:27], ACT.Sigmoid).then_inc(gate_ready, 1)

            def main(b, u):
                for t in range(NT):
                    if not (known(b) and b == 0 and t < 2):
                        act.wait_ge(tile_done, b * NT + (t - 1))
                    for g in range(3):
                        act.wait_ge(turned_taps, (b * NT + t) * 3 + (g + 1))
                        nc.scalar.activation(cols[t % 2][:, 3 * g:3 * g + 3], p_col[g][:], ACT.Copy).then_inc(cols_ready, 1)

            over_batches(act, prep, main)

        @block.vector
        def _(dve):
            link = Chain(dve, own_dve)
            group_norm_vector(nc, dve, link, xt, gn, gs)
            dve.nop().then_inc(norm_done, 1)
            dve.wait_ge(consts_in, 96)
            start = link.n
            STEPS = 13

            def prep(b, u):
                step = Chain(dve, own_dve, b * STEPS + start)
                tt, ts = nc.vector.tensor_tensor, nc.vector.tensor_scalar
                dve.wait_ge(conv_done, b + 1)
                if not (known(b) and b == 0):
                    dve.wait_ge(gate_ready, b)
                step(tt(off[:], p_off[:, u, 0:NT * 27].rearrange("p (t n) -> p t n", t=NT),
                        obias[:].rearrange("p (o n) -> p o n", o=1).to_broadcast([P, NT, 27]), ALU.add))
                tt(pos[:], off[:, :, 0:18], base[:], ALU.add).then_inc(off_ready, 1)
                dve.wait_ge(off_ready, b + 1)
                step(ts(pos[:], pos[:], -1.0, float(H), ALU.max, ALU.min))
                step(nc.vector.tensor_copy(posi[:], pos[:]))
                step(nc.vector.tensor_copy(low[:], posi[:]))
                step(tt(over[:], low[:], pos[:], ALU.is_gt))
                step(tt(low[:], low[:], over[:], ALU.subtract))
                step(tt(frac[:], pos[:], low[:], ALU.subtract))
                step(ts(rest[:], frac[:], -1.0, 1.0, ALU.mult, ALU.add))
                step(nc.vector.scalar_tensor_tensor(out=flat[:], in0=low[:, :, 0::2], scalar=float(WP), in1=low[:, :, 1::2],
                                                    op0=ALU.mult, op1=ALU.add))
                step(ts(idx[u][:], flat[:], float(WP + 1), None, ALU.add))
                dve.wait_ge(gate_ready, b + 1)
                step(ts(gate[:], gate[:], 2.0, None, ALU.mult))
                step(tt(rowg[:, 0], rest[:, :, 0::2], gate[:], ALU.mult))
                step(tt(rowg[:, 1], frac[:, :, 0::2], gate[:], ALU.mult))
                for n in range(4):
                    last = tt(wts[u][:, :, :, n], rowg[:, n // 2], (frac if n % 2 else rest)[:, :, 1::2], ALU.mult)
                last.then_inc(coords_ready, 1)
                dve.wait_ge(coords_ready, b + 1)

            def main(b, u):
                for t in range(NT):
                    uses = NT // SLOTS * b + t // SLOTS + 1
                    dve.wait_ge(gath_in[t % SLOTS], uses * (16 * TAPS))
                    e = gath[:, t % SLOTS]
                    g = e.rearrange("p k n c -> p (k n) c")
                    w = wts[u][:, t].rearrange("p k n -> p (k n)").rearrange("p (m o) -> p m o", o=1).to_broadcast([P, 4 * TAPS, C])
                    nc.vector.tensor_tensor(g, g, w, ALU.mult).then_inc(weighted, 1)
                    dve.wait_ge(weighted, (b * NT + t) * 2 + 1)
                    nc.vector.tensor_tensor(e[:, :, 0:2], e[:, :, 0:2], e[:, :, 2:4], ALU.add).then_inc(weighted, 1)
                dve.wait_ge(tile_done, b * NT + NT)
                nc.vector.tensor_tensor(xt[:, bass.ds(b, 1), :].rearrange("p o x -> p (o x)"),
                                        xt[:, bass.ds(b, 1), :].rearrange("p o x -> p (o x)"), p_y[u][:], ALU.add).then_inc(y_added, 1)
                dve.wait_ge(y_added, b + 1)
                nc.vector.bn_stats(row_stats[:, bass.ds(b, 1), :].rearrange("p o s -> p (o s)"),
                                   xt[:, bass.ds(b, 1), :].rearrange("p o x -> p (o x)"))

            over_batches(dve, prep, main)

        @block.tensor
        def _(pe):
            pe.wait_ge(consts_in, 96)
            join_groups_tensor(nc, pe, gnmat[:], gn["mv"][:, :, 0], B, gn, gs)
            pe.wait_ge(xn_ready, 1)

            def prep(b, u):
                if not (known(b) and b == 0):
                    pe.wait_ge(pix_ready, b)
                pe.wait_ge(pad_ready, b * 8 + 8)
                if not known(b):
                    pe.wait_ge(coords_ready, b - 1)
                for t in range(NT):
                    for m in range(5):
                        k = C if m == 4 else P
                        src, r0 = (pad01[u], m) if m < 3 else (pad22[u], 2 * (m - 3))
                        lhs = src[0:k, 4 * t + r0:4 * t + r0 + 4].rearrange("p r w -> p (r w)")
                        last = nc.tensor.matmul(p_off[:, u, t * 27:(t + 1) * 27], lhs, wconv[0:k, m],
                                                start=(m == 0), stop=(m == 4))
                last.then_inc(conv_done, 1)
                for t in range(NT):
                    last = nc.tensor.transpose(p_pix[:, t], pad01[u][C:P, 1 + 4 * t:5 + 4 * t].rearrange("p r w -> p (r w)"),
                                               ident[C:P, C:P])
                last.then_inc(turned, 1)

            def main(b, u):
                if not known(b):
                    pe.wait_ge(y_added, b - 1)
                elif b >= 2:
                    pe.wait_ge(y_added, b - 1)

                def finish(t):
                    pe.wait_ge(cols_ready, (b * NT + (t + 1)) * 3)
                    h, q = t // 4, t % 4
                    for k in range(TAPS):
                        last = nc.tensor.matmul(p_y[u][h * C:(h + 1) * C, q * P:(q + 1) * P], wreg[:, k], cols[t % 2][:, k],
                                                start=(k == 0), stop=(k == TAPS - 1))
                    last.then_inc(tile_done, 1)

                for t in range(NT):
                    pe.wait_ge(weighted, (b * NT + (t + 1)) * 2)
                    for g in range(3):
                        if not (known(b) and b == 0 and t < 1):
                            pe.wait_ge(cols_ready, (b * NT + (t - 1)) * 3 + (g + 1))
                        for k in range(3):
                            last = nc.tensor.transpose(p_col[g][:, k],
                                                       gath[:, t % SLOTS, 3 * g + k, 0:2].rearrange("p n c -> p (n c)"), ident[:])
                        last.then_inc(turned_taps, 1)
                    if t:
                        finish(t - 1)
                finish(NT - 1)

            over_batches(pe, prep, main)



MAP_K, REACH = 7, 3
THRESHOLD = 0.8


def layer2(nc, xt, d, early, row_stats):
    N = B * H * W
    with ExitStack() as ctx:
        def sb(name, shape, dt=F32):
            return ctx.enter_context(nc.sbuf_tensor(name + "_2", shape, dt))

        def pb(name, shape):
            return ctx.enter_context(nc.psum_tensor(name + "_2", shape, F32))

        def sem(name):
            return ctx.enter_context(nc.semaphore(name + "_2"))

        gn, gs = stat_buffers(nc, ctx, "gn2")
        xn = sb("xn", [P, B, HALF]); maskc = sb("maskc", [P, B, HALF])
        scratch = [sb(f"scratch{u}", [P, HALF]) for u in range(2)]
        spare = sb("spare", [P, 2, HALF])
        upper = [sb(f"upper{u}", [P, HALF]) for u in range(2)]
        lower = [sb(f"lower{u}", [P, HALF]) for u in range(2)]
        band = sb("band", [P, 12, P]); ident = sb("ident", [P, P]); gnmat = sb("gnmat", [P, P]); bnmat = sb("bnmat", [P, P])
        ones = sb("ones", [P, P]); mbias = sb("mbias", [P, 2])
        pooled = sb("pooled", [P, 2, NT + 2, B])
        attn = sb("attn", [P, NT + 2, B])
        mask = sb("mask", [P, NT, B]); mod = sb("mod", [P, 2, NT, B])
        sums = sb("sums", [P, 4, B])
        tot = sb("tot", [P, 4]); pair = sb("pair", [P, 4]); size = sb("size", [P, 2]); sizew = sb("sizew", [P, 2])
        rs = sb("rs", [P, 2]); rq = sb("rq", [P, 2]); mu = sb("mu", [P, 2]); amp2 = sb("amp2", [P, 2]); amp = sb("amp", [P, 2])
        tmp = sb("tmp", [P, 2]); cst = sb("cst", [P, 2]); damp = sb("damp", [P, 1]); dcst = sb("dcst", [P, 1]); ncst = sb("ncst", [P, 1])
        p_t = [pb(f"p_t{u}", [P, 4, 2, C]) for u in range(2)]
        p_m = pb("p_m", [P, 4, P])
        p_g = [pb(f"p_g{u}", [P, HALF]) for u in range(2)]
        p_b = [pb(f"p_b{u}", [P, HALF]) for u in range(2)]

        consts_in = sem("consts_in"); own_dve = sem("own_dve"); norm_done = sem("norm_done"); xn_ready = sem("xn_ready")
        turned = sem("turned"); reduced = sem("reduced"); pooled_ready = sem("pooled_ready"); map_conv = sem("map_conv")
        attn_ready = sem("attn_ready"); mods_conv = sem("mods_conv"); mask_ready = sem("mask_ready"); counted = sem("counted")
        mask_spread = sem("mask_spread"); maskc_ready = sem("maskc_ready"); masked_sums = sem("masked_sums")
        plain_sums = sem("plain_sums"); totals = sem("totals"); paired = sem("paired"); amp2_ready = sem("amp2_ready")
        amp_ready = sem("amp_ready"); coef_ready = sem("coef_ready"); affine_ready = sem("affine_ready")
        mod_ready = sem("mod_ready"); mod_spread = sem("mod_spread"); joined = sem("joined"); batch_done = sem("batch_done")
        zeroed = sem("zeroed"); own_pool = sem("own_pool")
        block = ctx.enter_context(nc.Block())

        @block.sync
        def _(sp):
            for name, tile in (("gnmat", gnmat), ("bnmat", bnmat), ("ident", ident), ("band", band), ("mbias", mbias)):
                sp.dma_start(tile[:], d[name][:]).then_inc(consts_in, 16)
            tiles, early_in = early
            for name, tile in tiles.items():
                sp.dma_start(tile[:], d[name][:]).then_inc(early_in, 16)

        @block.gpsimd
        def _(pool):
            nc.gpsimd.memset(pooled[:], 0.0).then_inc(zeroed, 1)
            nc.gpsimd.memset(attn[:], 0.0).then_inc(zeroed, 1)
            nc.gpsimd.memset(ones[:], 1.0).then_inc(zeroed, 1)
            for b in range(B):
                u = b % 2
                pool.wait_ge(affine_ready, b + 1)
                nc.gpsimd.tensor_tensor(upper[u][:], upper[u][:], maskc[:, b], ALU.mult).then_inc(own_pool, 1)
                pool.wait_ge(own_pool, b + 1)
                nc.gpsimd.tensor_tensor(upper[u][:], upper[u][:], lower[u][:], ALU.add).then_inc(joined, 1)

        @block.scalar
        def _(act):
            join_groups_scalar(nc, act, B, gn, gs)
            act.wait_ge(norm_done, 1)
            for b in range(B):
                nc.scalar.activation(xn[:, b, :], xt[:, b, :], ACT.Identity, bias=gn["shift"][:, b:b + 1],
                                     scale=gn["scale"][:, b:b + 1]).then_inc(xn_ready, 1)
            act.wait_ge(map_conv, 1)
            nc.scalar.activation(attn[:, 1:NT + 1].rearrange("p t b -> p (t b)"), p_m[:, 0], ACT.Sigmoid).then_inc(attn_ready, 1)
            act.wait_ge(xn_ready, B)
            for b in range(B):
                if b:
                    act.wait_ge(plain_sums, 2 * b)
                nc.scalar.activation(spare[:, 0], xn[:, b], ACT.Copy, accum_out=sums[:, 2, b:b + 1]).then_inc(plain_sums, 1)
                nc.scalar.activation(spare[:, 1], xn[:, b], ACT.Square, accum_out=sums[:, 3, b:b + 1]).then_inc(plain_sums, 1)
                act.wait_ge(mask_spread, b + 1)
                nc.scalar.activation(maskc[:, b], p_g[b % 2][:], ACT.Copy).then_inc(maskc_ready, 1)
            act.wait_ge(amp2_ready, 1)
            nc.scalar.activation(amp[:], amp2[:], ACT.Sqrt).then_inc(amp_ready, 1)
            act.wait_ge(coef_ready, 1)
            for b in range(B):
                u = b % 2
                if b >= 2:
                    act.wait_ge(batch_done, b - 1)
                nc.scalar.activation(upper[u][:], xn[:, b], ACT.Identity, bias=dcst[:], scale=damp[:])
                nc.scalar.activation(lower[u][:], xn[:, b], ACT.Identity, bias=ncst[:], scale=amp[:, 1:2]).then_inc(affine_ready, 1)

        @block.vector
        def _(dve):
            tt, ts, stt = nc.vector.tensor_tensor, nc.vector.tensor_scalar, nc.vector.scalar_tensor_tensor
            link = Chain(dve, own_dve)
            group_norm_vector(nc, dve, link, xt, gn, gs, row_stats)
            dve.nop().then_inc(norm_done, 1)
            dve.wait_ge(zeroed, 2)
            for b in range(B):
                dve.wait_ge(turned, b + 1)
                for n, op in ((0, ALU.add), (1, ALU.max)):
                    last = nc.vector.tensor_reduce(pooled[:, n, 1:NT + 1, b].rearrange("p (h q) -> p q h", h=2),
                                                   p_t[b % 2][:], AX.X, op)
                last.then_inc(reduced, 1)
            dve.wait_ge(reduced, B)
            ts(pooled[:, 0], pooled[:, 0], 1.0 / C, None, ALU.mult).then_inc(pooled_ready, 1)
            dve.wait_ge(attn_ready, 1)
            ts(mask[:], attn[:, 1:NT + 1], THRESHOLD, None, ALU.is_ge).then_inc(mask_ready, 1)
            dve.wait_ge(mods_conv, 1)
            dve.wait_ge(counted, 1)
            link(ts(mod[:, 0].rearrange("p t b -> p (t b)"), p_m[:, 1], mbias[:, 0:1], 1.0, ALU.add, ALU.add))
            ts(mod[:, 1].rearrange("p t b -> p (t b)"), p_m[:, 2], mbias[:, 1:2], None, ALU.add).then_inc(mod_ready, 1)
            link(nc.vector.tensor_reduce(size[:, 0:1], p_m[:, 3], AX.X, ALU.add))
            link(ts(size[:, 1:2], size[:, 0:1], -1.0, float(N), ALU.mult, ALU.add))
            link(ts(sizew[:], size[:], 1.0, None, ALU.max))
            for b in range(B):
                dve.wait_ge(maskc_ready, b + 1)
                s = scratch[b % 2]
                link(stt(out=s[:], in0=xn[:, b], scalar=1.0, in1=maskc[:, b], op0=ALU.mult, op1=ALU.mult,
                         accum_out=sums[:, 0, b:b + 1]))
                stt(out=s[:], in0=s[:], scalar=1.0, in1=xn[:, b], op0=ALU.mult, op1=ALU.mult,
                    accum_out=sums[:, 1, b:b + 1]).then_inc(masked_sums, 1)
            dve.wait_ge(masked_sums, B)
            dve.wait_ge(plain_sums, 2 * B)
            nc.vector.tensor_reduce(tot[:], sums[:], AX.X, ALU.add).then_inc(totals, 1)
            dve.wait_ge(paired, 1)
            link(ts(pair[:], gn["ps"][:, 0:4], 2.0, None, ALU.mult))
            link(nc.vector.tensor_copy(rs[:, 0:1], pair[:, 0:1]))
            link(tt(rs[:, 1:2], pair[:, 2:3], pair[:, 0:1], ALU.subtract))
            link(nc.vector.tensor_copy(rq[:, 0:1], pair[:, 1:2]))
            link(tt(rq[:, 1:2], pair[:, 3:4], pair[:, 1:2], ALU.subtract))
            link(nc.vector.reciprocal(tmp[:], sizew[:]))
            link(tt(mu[:], rs[:], tmp[:], ALU.mult))
            link(tt(tmp[:], mu[:], rs[:], ALU.mult))
            link(tt(rq[:], rq[:], tmp[:], ALU.subtract))
            link(ts(rq[:], rq[:], 0.0, 1.0 / N, ALU.max, ALU.mult))
            link(ts(rq[:], rq[:], GN_EPS, None, ALU.add))
            link(nc.vector.reciprocal(tmp[:], rq[:]))
            link(ts(amp2[:], sizew[:], 1.0 / N, None, ALU.mult))
            tt(amp2[:], amp2[:], tmp[:], ALU.mult).then_inc(amp2_ready, 1)
            dve.wait_ge(amp_ready, 1)
            link(tt(cst[:], amp[:], mu[:], ALU.mult))
            link(tt(damp[:], amp[:, 0:1], amp[:, 1:2], ALU.subtract))
            link(tt(dcst[:], cst[:, 1:2], cst[:, 0:1], ALU.subtract))
            ts(ncst[:], cst[:, 1:2], -1.0, None, ALU.mult).then_inc(coef_ready, 1)
            for b in range(B):
                u = b % 2
                dve.wait_ge(joined, b + 1)
                dve.wait_ge(mod_spread, b + 1)
                link(tt(upper[u][:], upper[u][:], p_g[u][:], ALU.mult))
                link(tt(upper[u][:], upper[u][:], p_b[u][:], ALU.add))
                tt(xt[:, b], xt[:, b], upper[u][:], ALU.add).then_inc(batch_done, 1)
                dve.wait_ge(batch_done, b + 1)
                nc.vector.bn_stats(row_stats[:, b], xt[:, b])

        @block.tensor
        def _(pe):
            pe.wait_ge(consts_in, 80)
            join_groups_tensor(nc, pe, gnmat[:], gn["mv"][:, :, 0], B, gn, gs)
            for b in range(B):
                pe.wait_ge(xn_ready, b + 1)
                if b >= 2:
                    pe.wait_ge(reduced, b - 1)
                for q in range(4):
                    last = nc.tensor.transpose(p_t[b % 2][:, q].rearrange("p h c -> p (h c)"), xn[:, b, q * P:(q + 1) * P], ident[:])
                last.then_inc(turned, 1)

            def conv(out, src, m0, first, stop):
                for dt in range(3):
                    last = nc.tensor.matmul(out, band[:, m0 + dt], src[:, dt:dt + NT].rearrange("p t b -> p (t b)"),
                                            start=(first and dt == 0), stop=(stop and dt == 2))
                return last

            pe.wait_ge(zeroed, 3)
            pe.wait_ge(pooled_ready, 1)
            conv(p_m[:, 0], pooled[:, 0], 0, True, False)
            conv(p_m[:, 0], pooled[:, 1], 3, False, True).then_inc(map_conv, 1)
            pe.wait_ge(attn_ready, 1)
            conv(p_m[:, 1], attn, 6, True, True)
            conv(p_m[:, 2], attn, 9, True, True).then_inc(mods_conv, 1)
            pe.wait_ge(mask_ready, 1)
            nc.tensor.matmul(p_m[:, 3], ones[:], mask[:].rearrange("p t b -> p (t b)"), start=True, stop=True).then_inc(counted, 1)

            def spread(out, src, b):
                for q in range(4):
                    for h in range(2):
                        last = nc.tensor.matmul(out[h * C:(h + 1) * C, q * P:(q + 1) * P],
                                                src[:, h * 4 + q, b:b + 1].to_broadcast([P, C]), ident[:], start=True, stop=True)
                return last

            for b in range(B):
                if b >= 2:
                    pe.wait_ge(maskc_ready, b - 1)
                spread(p_g[b % 2], mask, b).then_inc(mask_spread, 1)
            pe.wait_ge(totals, 1)
            nc.tensor.matmul(gn["ps"][:, 0:4], bnmat[:], tot[:], start=True, stop=True).then_inc(paired, 1)
            pe.wait_ge(mod_ready, 1)
            pe.wait_ge(maskc_ready, B)
            for b in range(B):
                if b >= 2:
                    pe.wait_ge(batch_done, b - 1)
                spread(p_g[b % 2], mod[:, 0], b)
                spread(p_b[b % 2], mod[:, 1], b).then_inc(mod_spread, 1)



ATT = 4
EARLY = {"inw": [P, 3 * ATT, HALF], "inb": [P, 3 * ATT, HALF], "hidw": [P, ATT, ATT, HALF]}


def early_tiles(nc, ctx):
    tiles = {name: ctx.enter_context(nc.sbuf_tensor(name + "_early", shape, F32)) for name, shape in EARLY.items()}
    return tiles, ctx.enter_context(nc.semaphore("early_in"))


def layer3(nc, xt, d, out, early, row_stats):
    A = ATT
    tiles, early_in = early
    inw, inb, hidw = (tiles[name] for name in EARLY)
    PAIRED = (1, 2)
    with ExitStack() as ctx:
        def sb(name, shape, dt=F32):
            return ctx.enter_context(nc.sbuf_tensor(name + "_3", shape, dt))

        def sem(name):
            return ctx.enter_context(nc.semaphore(name + "_3"))

        hidb = sb("hidb", [P, A, HALF])
        outw = sb("outw", [P, A, HALF]); outb = sb("outb", [P, HALF])
        ident = sb("ident", [P, P]); before = sb("before", [P, P]); follow = sb("follow", [P, P])
        first = sb("first", [P, 1])
        xh = [sb(f"xh{u}", [P, HALF]) for u in range(2)]
        xres = sb("xres", [P, HALF])
        recip = sb("recip", [P, HALF])
        expo, lost = xt[:, 0:A], xt[:, A:2 * A]
        z = [xt[:, 2 * A:4 * A], sb("z1", [P, 2 * A, HALF])]
        value_y = sb("value_y", [P, A * (HALF + 1)])
        value = value_y[:, 0:A * HALF].rearrange("p (i x) -> p i x", i=A)
        y = value_y[:].rearrange("p (i x) -> p i x", i=A)
        work = sb("work", [P, A * (A + 1), HALF])
        kv = work[:].rearrange("p (i j) x -> p i j x", j=A + 1)
        hid = work[:, 0:A * A].rearrange("p (a j) x -> p a j x", j=A)
        gated = work[:, A * A:]
        scale = sb("scale", [P, B]); shift = sb("shift", [P, B])
        gnmat = work[:, 0, 0:P]
        gn = {"mv": work[:, 2, 0:2 * B].rearrange("p (b s) -> p b s", b=B),
              "mean": work[:, 3, 0:B], "dev": work[:, 4, 0:B], "var": work[:, 5, 0:B], "sd": work[:, 6, 0:B], "scale": scale, "shift": shift}
        gs = {name: ctx.enter_context(nc.semaphore(f"gn3_{name}")) for name in STAT_SEMS}
        p_num = ctx.enter_context(nc.psum_tensor("p_num_3", [P, A + 1, HALF], F32))
        p_out = ctx.enter_context(nc.psum_tensor("p_out_3", [P, HALF], F32))
        p_carry = [ctx.enter_context(nc.psum_tensor(f"p_carry{n}_3", [P, HALF], F32)) for n in range(2)]
        p_first = p_carry[0][:, 32:32 + A]
        gn["ps"] = p_carry[0]
        resid = nc.dram_tensor("resid", (B, P, HALF), F32, kind="Internal").ap()

        consts_in = sem("consts_in"); gnmat_in = sem("gnmat_in"); own_dve = sem("own_dve"); norm_done = sem("norm_done")
        v_scaled = sem("v_scaled"); v_biased = sem("v_biased"); xh_ready = sem("xh_ready"); scaled = sem("scaled"); biased = sem("biased"); soft = sem("soft")
        multiplied = sem("multiplied"); last_row = sem("last_row"); scanned = sem("scanned"); carried = sem("carried"); queried = sem("queried"); summed = sem("summed"); denominator = sem("denominator")
        y_ready = sem("y_ready"); shifted = sem("shifted"); y_first = sem("y_first")
        hid_scaled = sem("hid_scaled"); hid_paired = sem("hid_paired"); hid_summed = sem("hid_summed"); tanh_ready = sem("tanh_ready")
        saved = sem("saved"); x_in = [sem(f"x_in{u}") for u in range(2)]; res_in = sem("res_in"); out_done = sem("out_done")
        own_act = sem("own_act"); expd = sem("expd"); lost_ready = sem("lost_ready"); logd = sem("logd"); relud = sem("relud")
        key_copied = sem("key_copied"); gated_ready = sem("gated_ready"); out_summed = sem("out_summed"); added = sem("added")
        block = ctx.enter_context(nc.Block())

        def known(b):
            return isinstance(b, int)

        def over_batches(eng, main):
            main(0, 0, 2)
            with eng.Fori(0, B // 2 - 2) as rr:
                main(rr * 2 + 1, 1, 2)
                main(rr * 2 + 2, 0, 2)
            main(B - 3, 1, 2)
            main(B - 2, 0, 1)
            main(B - 1, 1, 0)

        @block.sync
        def _(sp):
            sp.dma_start(gnmat, d["gnmat"][:]).then_inc(gnmat_in, 16)
            for b in range(B):
                sp.dma_start(resid[b], xt[:, b]).then_inc(saved, 16)
            for name, tile in (("ident", ident), ("before", before), ("follow", follow), ("first", first),
                               ("hidb", hidb), ("outw", outw), ("outb", outb)):
                sp.dma_start(tile[:], d[name][:]).then_inc(consts_in, 16)
            sp.wait_ge(saved, 16 * B)

            def load(b, u):
                sp.dma_start(xh[u][:], resid[bass.ds(b, 1)].rearrange("o p x -> (o p) x")).then_inc(x_in[u], 16)

            def main(b, u, following):
                if not (known(b) and b == 0):
                    sp.wait_ge(out_done, b * 16)
                sp.dma_start(xres[:], resid[bass.ds(b, 1)].rearrange("o p x -> (o p) x")).then_inc(res_in, 16)
                if following == 2:
                    sp.wait_ge(v_scaled, b + 1)
                    sp.wait_ge(scaled, b * 2 + 2)
                    load(b + 2, u)
                sp.wait_ge(added, b + 1)
                sp.dma_start(out[:, bass.ds(b, 1)].rearrange("p o x -> p (o x)"), xres[:]).then_inc(out_done, 16)

            over_batches(sp, main)
            sp.wait_ge(out_done, 16 * B)

        @block.gpsimd
        def _(pool):
            tt = nc.gpsimd.tensor_tensor

            def project(b, u, g):
                pool.wait_ge(xh_ready, b + 1)
                if g and not (known(b) and b < 2):
                    pool.wait_ge(queried, b * A - A)
                part = z[u][:, g * A:(g + 1) * A]
                tt(part, inw[:, (1 - g) * A:(2 - g) * A],
                   xh[u][:].rearrange("p (o x) -> p o x", o=1).to_broadcast([P, A, HALF]), ALU.mult).then_inc(scaled, 1)

            def add_bias(b, u, g):
                part = z[u][:, g * A:(g + 1) * A]
                pool.wait_ge(scaled, b * 2 + (g + 1))
                tt(part, part, inb[:, (1 - g) * A:(2 - g) * A], ALU.add).then_inc(biased, 1)

            def lost_part(b, g):
                pool.wait_ge(expd, b * 2 + (g + 1))
                tt(lost, expo, lost, ALU.subtract).then_inc(lost_ready, 1)

            def softplus_end(b, u, g):
                pool.wait_ge(relud, b * 2 + (g + 1))
                part = z[u][:, g * A:(g + 1) * A]
                tt(part, part, lost, ALU.add).then_inc(soft, 1)

            def main(b, u, following):
                softplus_end(b, u, 1)
                if not (known(b) and b == 0):
                    pool.wait_ge(out_summed, b)
                tt(kv[:, A - 1, 0:A], z[u][:, A - 1:A].to_broadcast([P, A, HALF]), value, ALU.mult).then_inc(last_row, 1)
                if following:
                    lost_part(b + 1, 0)
                    project(b + 1, 1 - u, 1)
                    add_bias(b + 1, 1 - u, 1)
                    softplus_end(b + 1, 1 - u, 0)
                if following == 2:
                    pool.wait_ge(key_copied, b * 2 + 2)
                    pool.wait_ge(multiplied, b * 2 + 2)
                    pool.wait_ge(last_row, b + 1)
                    project(b + 2, u, 0)
                for a in PAIRED:
                    pool.wait_ge(hid_scaled, b * A + (a + 1))
                    tt(hid[:, a, 0:2], hid[:, a, 0:2], hid[:, a, 2:4], ALU.add).then_inc(hid_paired, 1)
                if following:
                    lost_part(b + 1, 1)
                for a in range(A):
                    pool.wait_ge(tanh_ready, b * A + (a + 1))
                    tt(gated[:, a], gated[:, a], outw[:, a], ALU.mult).then_inc(gated_ready, 1)
                if following == 2:
                    add_bias(b + 2, u, 0)

            lost_part(0, 0)
            softplus_end(0, 0, 0)
            lost_part(0, 1)
            project(1, 1, 0)
            add_bias(1, 1, 0)
            over_batches(pool, main)

        @block.scalar
        def _(act):
            join_groups_scalar(nc, act, B, gn, gs)
            act.wait_ge(norm_done, 1)

            def normalise(b, u):
                if known(b) and b < 2:
                    source = xt[:, b]
                else:
                    act.wait_ge(x_in[u], b // 2 * 16 if known(b) else (b * 8 if u == 0 else b * 8 - 8))
                    source = xh[u][:]
                nc.scalar.activation(xh[u][:], source, ACT.Identity,
                                     bias=shift[:, bass.ds(b, 1)], scale=scale[:, bass.ds(b, 1)]).then_inc(xh_ready, 1)

            def exponential(b, u, g):
                step = Chain(act, own_act, (b * 2 + g) * 3)
                if not (known(b) and b == 0 and g == 0):
                    act.wait_ge(relud, b * 2 + g)
                    act.wait_ge(soft, b * 2 + g)
                act.wait_ge(biased, b * 2 + (g + 1))
                step(nc.scalar.activation(expo, z[u][:, g * A:(g + 1) * A], ACT.Abs))
                step(nc.scalar.activation(expo, expo, ACT.Exp, scale=-1.0))
                step(nc.scalar.activation(lost, expo, ACT.Copy, bias=1.0))
                nc.scalar.activation(lost, lost, ACT.Copy, bias=-1.0).then_inc(expd, 1)

            def logarithm(b, g):
                act.wait_ge(lost_ready, b * 2 + (g + 1))
                nc.scalar.activation(expo, expo, ACT.Ln, bias=1.0).then_inc(logd, 1)

            def copy_keys(b, u, rows):
                act.wait_ge(soft, b * 2 + 1)
                nc.scalar.activation(kv[:, rows, A], z[u][:, rows], ACT.Copy).then_inc(key_copied, 1)

            def main(b, u, following):
                if following:
                    exponential(b + 1, 1 - u, 0)
                if following == 2:
                    normalise(b + 2, u)
                if following:
                    logarithm(b + 1, 0)
                act.wait_ge(shifted, b + 1)
                nc.scalar.activation(y[:, :, 0], p_first, ACT.Identity, bias=first[:]).then_inc(y_first, 1)
                if following:
                    exponential(b + 1, 1 - u, 1)
                for a in range(A):
                    act.wait_ge(hid_summed, b * A + (a + 1))
                    nc.scalar.activation(gated[:, a], p_num[:, a], ACT.Tanh).then_inc(tanh_ready, 1)
                if following:
                    logarithm(b + 1, 1)
                    copy_keys(b + 1, 1 - u, slice(0, A - 1))
                    act.wait_ge(out_summed, b + 1)
                    copy_keys(b + 1, 1 - u, slice(A - 1, A))

            normalise(0, 0)
            normalise(1, 1)
            act.wait_ge(consts_in, 112)
            act.wait_ge(xh_ready, 2)
            act.wait_ge(saved, 16 * B)
            exponential(0, 0, 0)
            logarithm(0, 0)
            exponential(0, 0, 1)
            logarithm(0, 1)
            copy_keys(0, 0, slice(0, A - 1))
            copy_keys(0, 0, slice(A - 1, A))
            over_batches(act, main)

        @block.vector
        def _(dve):
            tt, ts, stt = nc.vector.tensor_tensor, nc.vector.tensor_scalar, nc.vector.scalar_tensor_tensor
            link = Chain(dve, own_dve)
            group_norm_vector(nc, dve, link, xt, gn, gs, row_stats)
            dve.nop().then_inc(norm_done, 1)
            dve.wait_ge(consts_in, 112)
            dve.wait_ge(early_in, 16 * len(EARLY))
            dve.wait_ge(saved, 16 * B)
            start = link.n

            def values(b, u):
                dve.wait_ge(xh_ready, b + 1)
                if not (known(b) and b == 0):
                    dve.wait_ge(hid_scaled, b * A)
                tt(value, inw[:, 2 * A:], xh[u][:].rearrange("p (o x) -> p o x", o=1).to_broadcast([P, A, HALF]),
                   ALU.mult).then_inc(v_scaled, 1)

            def value_bias(b):
                dve.wait_ge(v_scaled, b + 1)
                tt(value, value, inb[:, 2 * A:], ALU.add).then_inc(v_biased, 1)
                dve.wait_ge(v_biased, b + 1)

            def relu_log(b, u, g):
                dve.wait_ge(logd, b * 2 + (g + 1))
                part = z[u][:, g * A:(g + 1) * A]
                stt(out=part, in0=part, scalar=0.0, in1=expo, op0=ALU.max, op1=ALU.add).then_inc(relud, 1)

            def keys_x_values(u, rows):
                shape = [P, rows.stop - rows.start, A, HALF]
                tt(kv[:, rows, 0:A], z[u][:, rows].rearrange("p i (o x) -> p i o x", o=1).to_broadcast(shape),
                   value.rearrange("p (o j) x -> p o j x", o=1).to_broadcast(shape), ALU.mult).then_inc(multiplied, 1)

            def first_rows(b, u):
                dve.wait_ge(soft, b * 2 + 1)
                if not (known(b) and b == 0):
                    dve.wait_ge(hid_summed, b * A - 1)
                keys_x_values(u, slice(0, A - 2))
                if not (known(b) and b == 0):
                    dve.wait_ge(hid_summed, b * A)
                keys_x_values(u, slice(A - 2, A - 1))

            def scan(i):
                for n in range(i * (A + 1), (i + 1) * (A + 1)):
                    last = nc.vector.tensor_tensor_scan(out=work[:, n], data0=work[:, n], data1=work[:, n], initial=0.0,
                                                        op0=ALU.add, op1=ALU.bypass)
                last.then_inc(scanned, 1)

            def times_query(b, u, i):
                dve.wait_ge(scanned, b * A + (i + 1))
                dve.wait_ge(carried, b * A + (i + 1))
                for j in range(A + 1):
                    last = stt(out=kv[:, i, j], in0=kv[:, i, j], scalar=p_carry[i % 2][:, j:j + 1], in1=z[u][:, A + i],
                               op0=ALU.add, op1=ALU.mult)
                last.then_inc(queried, 1)

            def output(b):
                dve.wait_ge(out_summed, b + 1)
                dve.wait_ge(res_in, b * 16 + 16)
                tt(xres[:], xres[:], p_out[:], ALU.add).then_inc(added, 1)

            def main(b, u, following):
                relu_log(b, u, 1)
                dve.wait_ge(multiplied, b * 2 + 2)
                dve.wait_ge(key_copied, b * 2 + 1)
                scan(0)
                scan(1)
                if not (known(b) and b == 0):
                    output(b - 1)
                dve.wait_ge(soft, b * 2 + 2)
                times_query(b, u, 0)
                scan(2)
                times_query(b, u, 1)
                dve.wait_ge(last_row, b + 1)
                dve.wait_ge(key_copied, b * 2 + 2)
                scan(3)
                times_query(b, u, 2)
                times_query(b, u, 3)
                if following:
                    relu_log(b + 1, 1 - u, 0)
                dve.wait_ge(denominator, b + 1)
                nc.vector.reciprocal(recip[:], p_num[:, A]).then_inc(own_dve, 1)
                dve.wait_ge(own_dve, b + (start + 1))
                dve.wait_ge(summed, b + 1)
                tt(y[:, :, 1:], p_num[:, 0:A], recip[:].rearrange("p (o x) -> p o x", o=1).to_broadcast([P, A, HALF]),
                   ALU.mult).then_inc(y_ready, 1)
                dve.wait_ge(y_ready, b + 1)
                dve.wait_ge(y_first, b + 1)
                for a in range(A):
                    tt(hid[:, a], hidw[:, a], y[:, :, 0:HALF], ALU.mult).then_inc(hid_scaled, 1)
                if following:
                    values(b + 1, 1 - u)
                    value_bias(b + 1)
                    first_rows(b + 1, 1 - u)

            for g in range(2):
                dve.wait_ge(xh_ready, 1)
                part = z[0][:, g * A:(g + 1) * A]
                tt(part, inw[:, (1 - g) * A:(2 - g) * A],
                   xh[0][:].rearrange("p (o x) -> p o x", o=1).to_broadcast([P, A, HALF]), ALU.mult).then_inc(scaled, 1)
                dve.wait_ge(scaled, g + 1)
                tt(part, part, inb[:, (1 - g) * A:(2 - g) * A], ALU.add).then_inc(biased, 1)
            values(0, 0)
            value_bias(0)
            relu_log(0, 0, 0)
            first_rows(0, 0)
            over_batches(dve, main)
            output(B - 1)

        @block.tensor
        def _(pe):
            pe.wait_ge(gnmat_in, 16)
            join_groups_tensor(nc, pe, gnmat[:], gn["mv"][:, :, 0], B, gn, gs)
            pe.wait_ge(consts_in, 112)

            def carry(b, i):
                pe.wait_ge(scanned, b * A + (i + 1))
                nc.tensor.matmul(p_carry[i % 2][:, 0:A + 1], before[:], kv[:, i, :, HALF - 1], start=True, stop=True).then_inc(carried, 1)

            def sum_row(b, i):
                pe.wait_ge(queried, b * A + (i + 1))
                for j in range(A + 1):
                    j = (j + A) % (A + 1)
                    last = nc.tensor.matmul(p_num[:, j], ident[:], kv[:, i, j], start=(i == 0), stop=(i == A - 1))
                    if i == A - 1 and j == A:
                        last.then_inc(denominator, 1)
                return last

            def main(b, u, following):
                carry(b, 0)
                carry(b, 1)
                for i in range(A - 2):
                    sum_row(b, i)
                    carry(b, i + 2)
                sum_row(b, A - 2)
                sum_row(b, A - 1).then_inc(summed, 1)
                pe.wait_ge(y_ready, b + 1)
                nc.tensor.matmul(p_first, follow[:], y[:, :, HALF], start=True, stop=True).then_inc(shifted, 1)
                for a in range(A):
                    nc.tensor.matmul(p_num[:, a], ident[:], hidb[:, a], start=True, stop=False)
                    if a in PAIRED:
                        pe.wait_ge(hid_paired, b * len(PAIRED) + (PAIRED.index(a) + 1))
                    else:
                        pe.wait_ge(hid_scaled, b * A + (a + 1))
                    terms = 2 if a in PAIRED else A
                    for j in range(terms):
                        last = nc.tensor.matmul(p_num[:, a], ident[:], hid[:, a, j], start=False, stop=(j == terms - 1))
                    last.then_inc(hid_summed, 1)
                if not (known(b) and b == 0):
                    pe.wait_ge(added, b)
                nc.tensor.matmul(p_out[:], ident[:], outb[:], start=True, stop=False)
                for a in range(A):
                    pe.wait_ge(gated_ready, b * A + (a + 1))
                    last = nc.tensor.matmul(p_out[:], ident[:], gated[:, a], start=False, stop=(a == A - 1))
                last.then_inc(out_summed, 1)

            over_batches(pe, main)


def build_program(nc, d, out):
    with nc.sbuf_tensor("xt", [P, B, HALF], F32) as xt, nc.sbuf_tensor("row_stats", [P, B, 6], F32) as row_stats:
        layer0(nc, xt, d)
        layer1(nc, xt, d, row_stats)
        with ExitStack() as ctx:
            early = early_tiles(nc, ctx)
            layer2(nc, xt, d, early, row_stats)
            layer3(nc, xt, d, out, early, row_stats)


def layouts(inp):
    import numpy as np
    f = lambda n: np.asarray(inp[n])
    a = {}
    x = f("x").reshape(B, C, 2, HALF)
    a["x"] = x.transpose(2, 1, 0, 3).reshape(P, B, HALF)
    w = f("L0_conv_weight").reshape(C, 2, RH, 4, 8, C, 3, 3)
    w0 = np.zeros((RH, 4, 2, C, 8, 9, C), np.float32)
    t = w.transpose(1, 2, 3, 5, 4, 6, 7, 0)
    for h in range(2):
        for m in range(3):
            w0[:, :, 0, :, :, 4 * h + m] = t[h, :, :, :, :, m, 0]
            w0[:, :, 1, :, :, 4 * h + m] = t[h, :, :, :, :, m, 1]
        w0[:, :, 0, :, :, 4 * h + 3] = t[h, :, :, :, :, 0, 2]
        w0[:, :, 1, :, :, 4 * h + 3] = t[h, :, :, :, :, 1, 2]
        w0[:, :, h, :, :, 8] = t[h, :, :, :, :, 2, 2]
    a["w0"] = w0.reshape(RH, 4, P, 8, 9, C)
    a["bias0"] = f("L0_conv_bias").reshape(C, 2, HALF).transpose(1, 0, 2).reshape(P, HALF)
    a["affine0"] = np.stack([np.tile(f("L0_conv_gamma"), 2), np.tile(f("L0_conv_beta"), 2)], axis=1)
    p = np.arange(P)
    a["gnmat"] = (((p[:, None] % C) // 2 == (p[None, :] % C) // 2) / 4.0).astype(np.float32)
    a["bnmat"] = ((p[:, None] % C == p[None, :] % C) / 2.0).astype(np.float32)
    w = np.concatenate([f("L1_conv_offset_w"), f("L1_conv_mod_w")], axis=0)
    w1 = np.zeros((2, C, 5, 27), np.float32)
    for m in range(3):
        w1[0, :, m] = w[:, :, m, 0].T
        w1[1, :, m] = w[:, :, m, 1].T
    w1[0, :, 3], w1[1, :, 3], w1[0, :, 4] = w[:, :, 0, 2].T, w[:, :, 1, 2].T, w[:, :, 2, 2].T
    a["wconv"] = w1.reshape(P, 5, 27)
    r = f("L1_conv_reg_w").reshape(C, C, TAPS)
    a["wreg"] = np.tile(r.transpose(1, 2, 0), (2, 1, 1))
    a["ident"] = np.eye(P, dtype=np.float32)
    a["obias"] = np.tile(np.concatenate([f("L1_conv_offset_b"), f("L1_conv_mod_b")]), (P, 1))
    t, k = np.arange(NT), np.arange(TAPS)
    base = np.zeros((P, NT, TAPS, 2), np.float32)
    base[..., 0] = (4 * t[None, :] + p[:, None] // W)[:, :, None] + k // 3 - 1
    base[..., 1] = (p % W)[:, None, None] + k % 3 - 1
    a["base"] = base.reshape(P, NT, 18)
    band = np.zeros((P, 4, 3, P), np.float32)
    kern = [f("L2_conv_w1")[0, 0], f("L2_conv_w1")[0, 1], f("L2_conv_wg")[0, 0], f("L2_conv_wb")[0, 0]]
    for n, w in enumerate(kern):
        for dt in range(3):
            for r in range(4):
                for q in range(4):
                    dy = 4 * (dt - 1) + r - q + REACH
                    if 0 <= dy < MAP_K:
                        for x in range(W):
                            for o in range(max(0, x - REACH), min(W, x + REACH + 1)):
                                band[r * W + x, n, dt, q * W + o] = w[dy, x - o + REACH]
    a["band"] = band.reshape(P, 12, P)
    a["mbias"] = np.tile(np.concatenate([f("L2_conv_bg"), f("L2_conv_bb")]), (P, 1))
    def by_position(v, lead):
        v = v.reshape(lead + (C, 2, HALF, -1))
        n = len(lead)
        v = v.transpose((n + 1, n) + tuple(range(n)) + (n + 3, n + 2))
        return v.reshape((P,) + lead + (-1, HALF))
    a["inw"] = by_position(f("L3_conv_in_proj_weight"), (3,)).reshape(P, 12, HALF)
    a["inb"] = by_position(f("L3_conv_in_proj_bias"), (3,)).reshape(P, 12, HALF)
    a["hidw"] = by_position(f("L3_conv_hid_proj_weight"), (4,))
    a["hidb"] = by_position(f("L3_conv_hid_proj_bias"), (4,)).reshape(P, 4, HALF)
    a["outw"] = by_position(f("L3_conv_out_proj_weight"), (4,)).reshape(P, 4, HALF)
    a["outb"] = by_position(f("L3_conv_out_proj_bias"), ()).reshape(P, HALF)
    segment = 2 * (p % C) + p // C
    a["before"] = (segment[:, None] < segment[None, :]).astype(np.float32)
    a["follow"] = (segment[:, None] + 1 == segment[None, :]).astype(np.float32)
    a["first"] = (segment == 0).astype(np.float32).reshape(P, 1)
    return a


def kernel(**inputs):
    import numpy as np
    import concourse.bacc as bacc
    from concourse.bass_utils import run_bass_kernel_spmd

    arrays = {"in_" + n: np.ascontiguousarray(v) for n, v in layouts(inputs).items()}
    nc = bacc.Bacc("TRN2", target_bir_lowering=False, num_devices=1)
    d = {n[3:]: nc.dram_tensor(n, a.shape, mybir.dt.from_np(a.dtype), kind="ExternalInput").ap() for n, a in arrays.items()}
    y = nc.dram_tensor("y", (P, B, HALF), F32, kind="ExternalOutput").ap()
    build_program(nc, d, y)
    got = run_bass_kernel_spmd(nc, [arrays], core_ids=[0]).results[0]["y"]
    return got.reshape(2, C, B, RH, W).transpose(2, 1, 0, 3, 4).reshape(B, C, H, W)
```
